# Optimizing a Trainium2 kernel written in Bass

```python
import numpy as np
import jax
import jax.numpy as jnp

def _softmax(x, axis=-1):
    return jax.nn.softmax(x, axis=axis)

def _gelu(x):
    return jax.nn.gelu(x, approximate=True)

def _silu(x):
    return jax.nn.silu(x)

def _sigmoid(x):
    return jax.nn.sigmoid(x)

def _layernorm(x, axis=-1, eps=1e-05):
    m = jnp.mean(x, axis=axis, keepdims=True)
    v = jnp.var(x, axis=axis, keepdims=True)
    return (x - m) / jnp.sqrt(v + eps)

def _scatter_add(tgt, idx, src, axis=0):
    return tgt.at[idx].add(src)

def _segment_sum(src, seg, n):
    return jax.ops.segment_sum(src, seg, n)
kernel_name = 'mk_gnn_resnorm_d4_gnn_r32_54dcc8'

def setup_inputs(seed: int=0):
    np.random.seed(seed)
    _w = jnp.asarray

    def _rec_inputs():
        import jax
        import jax.numpy as jnp
        _gk = jax.random.key(seed)
        x = -0.0003713 + 1 * jax.random.normal(jax.random.fold_in(_gk, 1), (3125, 128), jnp.float32)
        src = jax.random.randint(jax.random.fold_in(_gk, 2), (100000,), 0, 3125, jnp.int32)
        dst = jnp.minimum((3125 * jax.random.uniform(jax.random.fold_in(_gk, 3), (100000,)) ** 2.0).astype(jnp.int32), 99999)
        _o = jnp.argsort(dst, stable=True)
        src = src[_o]
        dst = dst[_o]
        edge_type_8 = jax.random.randint(jax.random.fold_in(_gk, 13), (100000,), 0, 8, jnp.int32)
        return (x, src, dst, edge_type_8)
    x, src, dst, edge_type_8 = _rec_inputs()

    def _L0_gnn_setup():
        import jax, jax.numpy as jnp
        import numpy as np
        N_NODES = 3125
        N_EDGES = 50000
        IN_DIM = 128
        HID_DIM = 128

        def _gcn_conv(x, row, col, norm, W, b, n_nodes):
            h = x @ W
            msg = h[row] * norm[:, None]
            out = jax.ops.segment_sum(msg, col, num_segments=n_nodes)
            return out + b
        key = jax.random.key(seed)
        k_x, k_e, k_w1, k_w2, k_b1, k_b2 = jax.random.split(key, 6)
        x = jax.random.normal(k_x, (N_NODES, IN_DIM), dtype=jnp.float32)
        edge_index = jax.random.randint(k_e, (2, N_EDGES), 0, N_NODES, dtype=jnp.int64)
        s1 = 1.0 / np.sqrt(IN_DIM)
        s2 = 1.0 / np.sqrt(HID_DIM)
        W1 = jax.random.uniform(k_w1, (IN_DIM, HID_DIM), jnp.float32, -s1, s1)
        b1 = jnp.zeros((HID_DIM,), jnp.float32)
        W2 = jax.random.uniform(k_w2, (HID_DIM, HID_DIM), jnp.float32, -s2, s2)
        b2 = jnp.zeros((HID_DIM,), jnp.float32)
        return {'x': x, 'edge_index': edge_index, 'W1': W1, 'b1': b1, 'W2': W2, 'b2': b2}
    _L0_gnn_all = _L0_gnn_setup()
    _L0_gnn_in = {k: v for k, v in _L0_gnn_all.items() if k in ('W1', 'b1', 'W2', 'b2')}
    del _L0_gnn_all

    def _L1_gnn_setup():
        import jax, jax.numpy as jnp
        import numpy as np
        N_NODES = 50000
        N_EDGES = 18750
        D_IN = 128
        D_OUT = 128
        N_REL = 8

        def _rgcn(x, edge_index, edge_type, weight, self_weight, bias):
            num_nodes = x.shape[0]
            src, dst = (edge_index[0], edge_index[1])
            seg_rd = edge_type * num_nodes + dst
            deg = jax.ops.segment_sum(jnp.ones_like(dst, dtype=x.dtype), seg_rd, num_segments=N_REL * num_nodes)
            deg = jnp.maximum(deg, 1.0)
            norm = 1.0 / deg[seg_rd]
            hw = jnp.einsum('nd,rdo->rno', x, weight)
            msg = hw.reshape(N_REL * num_nodes, -1)[edge_type * num_nodes + src]
            msg = msg * norm[:, None]
            out = jax.ops.segment_sum(msg, dst, num_segments=num_nodes)
            out = out + x @ self_weight + bias
            return out
        key = jax.random.key(seed)
        k1, k2, k3, k4, k5, k6 = jax.random.split(key, 6)
        x = jax.random.normal(k1, (N_NODES, D_IN), dtype=jnp.float32)
        edge_index = jax.random.randint(k2, (2, N_EDGES), 0, N_NODES, dtype=jnp.int64)
        edge_type = jax.random.randint(k3, (N_EDGES,), 0, N_REL, dtype=jnp.int64)
        lim = float(np.sqrt(6.0 / (D_IN + D_OUT)))
        weight = jax.random.uniform(k4, (N_REL, D_IN, D_OUT), minval=-lim, maxval=lim, dtype=jnp.float32)
        self_weight = jax.random.uniform(k5, (D_IN, D_OUT), minval=-lim, maxval=lim, dtype=jnp.float32)
        bias = jnp.zeros((D_OUT,), dtype=jnp.float32)
        return {'x': x, 'edge_index': edge_index, 'edge_type': edge_type, 'weight': weight, 'self_weight': self_weight, 'bias': bias}
    _L1_gnn_all = _L1_gnn_setup()
    _L1_gnn_in = {k: v for k, v in _L1_gnn_all.items() if k in ('weight', 'self_weight', 'bias')}
    del _L1_gnn_all

    def _L2_gnn_setup():
        import jax, jax.numpy as jnp
        import numpy as np
        N_NODES = 3125
        N_EDGES = 18750
        DIM = 128
        LN_EPS = 1e-05
        key = jax.random.key(seed)
        ks = jax.random.split(key, 12)
        s = 1.0 / np.sqrt(DIM)
        return {'h': jax.random.normal(ks[0], (N_NODES, DIM), dtype=jnp.float32), 'edge_src': jax.random.randint(ks[1], (N_EDGES,), 0, N_NODES, dtype=jnp.int32), 'edge_dst': jax.random.randint(ks[2], (N_EDGES,), 0, N_NODES, dtype=jnp.int32), 'W_self': jax.random.uniform(ks[3], (DIM, DIM), jnp.float32, -s, s), 'b_self': jax.random.uniform(ks[4], (DIM,), jnp.float32, -s, s), 'W_neigh': jax.random.uniform(ks[5], (DIM, DIM), jnp.float32, -s, s), 'b_neigh': jax.random.uniform(ks[6], (DIM,), jnp.float32, -s, s), 'W_gate': jax.random.uniform(ks[7], (DIM, 2 * DIM), jnp.float32, -s, s), 'b_gate': jax.random.uniform(ks[8], (DIM,), jnp.float32, -s, s), 'ln_gamma': jnp.ones((DIM,), jnp.float32), 'ln_beta': jnp.zeros((DIM,), jnp.float32)}
    _L2_gnn_all = _L2_gnn_setup()
    _L2_gnn_in = {k: v for k, v in _L2_gnn_all.items() if k in ('W_self', 'b_self', 'W_neigh', 'b_neigh', 'W_gate', 'b_gate', 'ln_gamma', 'ln_beta')}
    del _L2_gnn_all

    def _L3_gnn_setup():
        import jax, jax.numpy as jnp
        import numpy as np
        N = 625
        E = 10000
        IN_DIM = 128
        HID = 64
        HEADS = 8
        OUT_DIM = 128
        NEG_SLOPE = 0.2

        def _glorot(key, shape):
            fan_in = shape[0] if len(shape) > 1 else shape[-1]
            return jax.random.normal(key, shape, dtype=jnp.float32) / jnp.sqrt(jnp.float32(fan_in))

        def _gat_layer(x, src, dst, W, a_src, a_dst, b, heads, concat):
            n = x.shape[0]
            h = (x @ W).reshape(n, heads, -1)
            al_src = jnp.sum(h * a_src[None], axis=-1)
            al_dst = jnp.sum(h * a_dst[None], axis=-1)
            e = jax.nn.leaky_relu(al_src[src] + al_dst[dst], NEG_SLOPE)
            emax = jax.ops.segment_max(e, dst, num_segments=n)
            ex = jnp.exp(e - emax[dst])
            den = jax.ops.segment_sum(ex, dst, num_segments=n)
            alpha = ex / (den[dst] + 1e-16)
            out = jax.ops.segment_sum(h[src] * alpha[:, :, None], dst, num_segments=n)
            out = out.reshape(n, -1) if concat else out.mean(axis=1)
            return out + b
        key = jax.random.key(seed)
        ks = jax.random.split(key, 16)
        x = jax.random.normal(ks[0], (N, IN_DIM), dtype=jnp.float32)
        edge_index = jax.random.randint(ks[1], (2, E), 0, N, dtype=jnp.int32)
        HC = HEADS * HID
        return {'x': x, 'edge_index': edge_index, 'W1': _glorot(ks[2], (IN_DIM, HC)), 'a_src1': _glorot(ks[3], (HEADS, HID)), 'a_dst1': _glorot(ks[4], (HEADS, HID)), 'b1': jnp.zeros((HC,), jnp.float32), 'W2': _glorot(ks[5], (HC, HC)), 'a_src2': _glorot(ks[6], (HEADS, HID)), 'a_dst2': _glorot(ks[7], (HEADS, HID)), 'b2': jnp.zeros((HC,), jnp.float32), 'W3': _glorot(ks[8], (HC, OUT_DIM)), 'a_src3': _glorot(ks[9], (1, OUT_DIM)), 'a_dst3': _glorot(ks[10], (1, OUT_DIM)), 'b3': jnp.zeros((OUT_DIM,), jnp.float32)}
    _L3_gnn_all = _L3_gnn_setup()
    _L3_gnn_in = {k: v for k, v in _L3_gnn_all.items() if k in ('W1', 'a_src1', 'a_dst1', 'b1', 'W2', 'a_src2', 'a_dst2', 'b2', 'W3', 'a_src3', 'a_dst3', 'b3')}
    del _L3_gnn_all
    return {'x': x, 'src': src, 'dst': dst, 'edge_type_8': edge_type_8, 'L0_gnn_W1': _L0_gnn_in['W1'], 'L0_gnn_b1': _L0_gnn_in['b1'], 'L0_gnn_W2': _L0_gnn_in['W2'], 'L0_gnn_b2': _L0_gnn_in['b2'], 'L1_gnn_weight': _L1_gnn_in['weight'], 'L1_gnn_self_weight': _L1_gnn_in['self_weight'], 'L1_gnn_bias': _L1_gnn_in['bias'], 'L2_gnn_W_self': _L2_gnn_in['W_self'], 'L2_gnn_b_self': _L2_gnn_in['b_self'], 'L2_gnn_W_neigh': _L2_gnn_in['W_neigh'], 'L2_gnn_b_neigh': _L2_gnn_in['b_neigh'], 'L2_gnn_W_gate': _L2_gnn_in['W_gate'], 'L2_gnn_b_gate': _L2_gnn_in['b_gate'], 'L2_gnn_ln_gamma': _L2_gnn_in['ln_gamma'], 'L2_gnn_ln_beta': _L2_gnn_in['ln_beta'], 'L3_gnn_W1': _L3_gnn_in['W1'], 'L3_gnn_a_src1': _L3_gnn_in['a_src1'], 'L3_gnn_a_dst1': _L3_gnn_in['a_dst1'], 'L3_gnn_b1': _L3_gnn_in['b1'], 'L3_gnn_W2': _L3_gnn_in['W2'], 'L3_gnn_a_src2': _L3_gnn_in['a_src2'], 'L3_gnn_a_dst2': _L3_gnn_in['a_dst2'], 'L3_gnn_b2': _L3_gnn_in['b2'], 'L3_gnn_W3': _L3_gnn_in['W3'], 'L3_gnn_a_src3': _L3_gnn_in['a_src3'], 'L3_gnn_a_dst3': _L3_gnn_in['a_dst3'], 'L3_gnn_b3': _L3_gnn_in['b3']}

def reference(x, src, dst, edge_type_8, L0_gnn_W1, L0_gnn_b1, L0_gnn_W2, L0_gnn_b2, L1_gnn_weight, L1_gnn_self_weight, L1_gnn_bias, L2_gnn_W_self, L2_gnn_b_self, L2_gnn_W_neigh, L2_gnn_b_neigh, L2_gnn_W_gate, L2_gnn_b_gate, L2_gnn_ln_gamma, L2_gnn_ln_beta, L3_gnn_W1, L3_gnn_a_src1, L3_gnn_a_dst1, L3_gnn_b1, L3_gnn_W2, L3_gnn_a_src2, L3_gnn_a_dst2, L3_gnn_b2, L3_gnn_W3, L3_gnn_a_src3, L3_gnn_a_dst3, L3_gnn_b3):
    import jax
    import jax.numpy as jnp

    def _L0_gnn_ref(x, edge_index, W1, b1, W2, b2):
        import jax, jax.numpy as jnp
        import numpy as np
        N_NODES = 3125
        N_EDGES = 50000
        IN_DIM = 128
        HID_DIM = 128

        def _gcn_conv(x, row, col, norm, W, b, n_nodes):
            h = x @ W
            msg = h[row] * norm[:, None]
            out = jax.ops.segment_sum(msg, col, num_segments=n_nodes)
            return out + b
        n = x.shape[0]
        loop = jnp.arange(n, dtype=edge_index.dtype)
        row = jnp.concatenate([edge_index[0], loop])
        col = jnp.concatenate([edge_index[1], loop])
        deg = jax.ops.segment_sum(jnp.ones(row.shape[0], x.dtype), col, num_segments=n)
        dis = jnp.where(deg > 0, jax.lax.rsqrt(jnp.maximum(deg, 1e-30)), 0.0)
        norm = dis[row] * dis[col]
        h = _gcn_conv(x, row, col, norm, W1, b1, n)
        h = jax.nn.relu(h)
        out = _gcn_conv(h, row, col, norm, W2, b2, n)
        return out

    def _L1_gnn_ref(x, edge_index, edge_type, weight, self_weight, bias):
        import jax, jax.numpy as jnp
        import numpy as np
        N_NODES = 50000
        N_EDGES = 18750
        D_IN = 128
        D_OUT = 128
        N_REL = 8

        def _rgcn(x, edge_index, edge_type, weight, self_weight, bias):
            num_nodes = x.shape[0]
            src, dst = (edge_index[0], edge_index[1])
            seg_rd = edge_type * num_nodes + dst
            deg = jax.ops.segment_sum(jnp.ones_like(dst, dtype=x.dtype), seg_rd, num_segments=N_REL * num_nodes)
            deg = jnp.maximum(deg, 1.0)
            norm = 1.0 / deg[seg_rd]
            hw = jnp.einsum('nd,rdo->rno', x, weight)
            msg = hw.reshape(N_REL * num_nodes, -1)[edge_type * num_nodes + src]
            msg = msg * norm[:, None]
            out = jax.ops.segment_sum(msg, dst, num_segments=num_nodes)
            out = out + x @ self_weight + bias
            return out
        return _rgcn(x, edge_index, edge_type, weight, self_weight, bias)

    def _L2_gnn_ref(h, edge_src, edge_dst, W_self, b_self, W_neigh, b_neigh, W_gate, b_gate, ln_gamma, ln_beta):
        import jax, jax.numpy as jnp
        import numpy as np
        N_NODES = 3125
        N_EDGES = 18750
        DIM = 128
        LN_EPS = 1e-05
        n = h.shape[0]
        hs = h @ W_self.T + b_self
        neigh_sum = jax.ops.segment_sum(h[edge_src], edge_dst, num_segments=n)
        counts = jax.ops.segment_sum(jnp.ones((edge_src.shape[0],), h.dtype), edge_dst, num_segments=n)
        has_pred = (counts > 0).astype(h.dtype)[:, None]
        neigh_mean = neigh_sum / jnp.maximum(counts, 1.0)[:, None]
        hn = neigh_mean @ W_neigh.T + b_neigh
        m = hs + has_pred * hn
        gate = jax.nn.sigmoid(jnp.concatenate([h, m], axis=-1) @ W_gate.T + b_gate)
        v = gate * m + (1.0 - gate) * h
        mu = jnp.mean(v, axis=-1, keepdims=True)
        var = jnp.mean(jnp.square(v - mu), axis=-1, keepdims=True)
        out = (v - mu) * jax.lax.rsqrt(var + LN_EPS) * ln_gamma + ln_beta
        return jax.nn.relu(out)

    def _L3_gnn_ref(x, edge_index, W1, a_src1, a_dst1, b1, W2, a_src2, a_dst2, b2, W3, a_src3, a_dst3, b3):
        import jax, jax.numpy as jnp
        import numpy as np
        N = 625
        E = 10000
        IN_DIM = 128
        HID = 64
        HEADS = 8
        OUT_DIM = 128
        NEG_SLOPE = 0.2

        def _glorot(key, shape):
            fan_in = shape[0] if len(shape) > 1 else shape[-1]
            return jax.random.normal(key, shape, dtype=jnp.float32) / jnp.sqrt(jnp.float32(fan_in))

        def _gat_layer(x, src, dst, W, a_src, a_dst, b, heads, concat):
            n = x.shape[0]
            h = (x @ W).reshape(n, heads, -1)
            al_src = jnp.sum(h * a_src[None], axis=-1)
            al_dst = jnp.sum(h * a_dst[None], axis=-1)
            e = jax.nn.leaky_relu(al_src[src] + al_dst[dst], NEG_SLOPE)
            emax = jax.ops.segment_max(e, dst, num_segments=n)
            ex = jnp.exp(e - emax[dst])
            den = jax.ops.segment_sum(ex, dst, num_segments=n)
            alpha = ex / (den[dst] + 1e-16)
            out = jax.ops.segment_sum(h[src] * alpha[:, :, None], dst, num_segments=n)
            out = out.reshape(n, -1) if concat else out.mean(axis=1)
            return out + b
        loops = jnp.arange(N, dtype=edge_index.dtype)
        src = jnp.concatenate([edge_index[0], loops])
        dst = jnp.concatenate([edge_index[1], loops])
        h = _gat_layer(x, src, dst, W1, a_src1, a_dst1, b1, HEADS, True)
        h = jax.nn.elu(h)
        h = _gat_layer(h, src, dst, W2, a_src2, a_dst2, b2, HEADS, True)
        h = jax.nn.elu(h)
        out = _gat_layer(h, src, dst, W3, a_src3, a_dst3, b3, 1, False)
        return out
    edge_index = jnp.stack([src, dst])
    x = _layernorm(x + _L0_gnn_ref(x, edge_index, L0_gnn_W1, L0_gnn_b1, L0_gnn_W2, L0_gnn_b2), axis=-1)
    x = _layernorm(x + _L1_gnn_ref(x, edge_index, edge_type_8, L1_gnn_weight, L1_gnn_self_weight, L1_gnn_bias), axis=-1)
    x = _layernorm(x + _L2_gnn_ref(x, src, dst, L2_gnn_W_self, L2_gnn_b_self, L2_gnn_W_neigh, L2_gnn_b_neigh, L2_gnn_W_gate, L2_gnn_b_gate, L2_gnn_ln_gamma, L2_gnn_ln_beta), axis=-1)
    x = _layernorm(x + _L3_gnn_ref(x, edge_index, L3_gnn_W1, L3_gnn_a_src1, L3_gnn_a_dst1, L3_gnn_b1, L3_gnn_W2, L3_gnn_a_src2, L3_gnn_a_dst2, L3_gnn_b2, L3_gnn_W3, L3_gnn_a_src3, L3_gnn_a_dst3, L3_gnn_b3), axis=-1)
    return x

_drawn_inputs = setup_inputs


def setup_inputs(seed=0):
    import zlib

    import numpy as np

    out = dict(_drawn_inputs(seed))
    spreads = {'L0_gnn_b1': (0.0, 0.1),
     'L0_gnn_b2': (0.0, 0.1),
     'L1_gnn_bias': (0.0, 0.1),
     'L2_gnn_ln_gamma': (1.0, 0.2),
     'L2_gnn_ln_beta': (0.0, 0.1),
     'L3_gnn_b1': (0.0, 0.1),
     'L3_gnn_b2': (0.0, 0.1),
     'L3_gnn_b3': (0.0, 0.1)}
    factors = {'L0_gnn_W1': 4.593,
     'L2_gnn_b_gate': 4.829,
     'L3_gnn_a_dst1': 2.831,
     'L3_gnn_a_dst2': 2.946,
     'L3_gnn_a_src3': 3.116,
     'L3_gnn_a_dst3': 4.038}
    for name, (base, spread) in spreads.items():
        noise = np.random.default_rng([zlib.crc32(name.encode()), seed]).standard_normal(out[name].shape)
        drawn = base * np.exp(spread * noise) if base else spread * noise
        out[name] = jnp.asarray(drawn.astype(out[name].dtype))
    for name, factor in factors.items():
        out[name] = (out[name] * factor).astype(out[name].dtype)
    return out
```

```python
from contextlib import ExitStack

import concourse.bass as bass
from concourse import mybir

F32 = mybir.dt.float32
I32 = mybir.dt.int32
ALU = mybir.AluOpType
ACT = mybir.ActivationFunctionType
AX = mybir.AxisListType.X

P = 128
N = 3125
E = 100000
D = 128
R = 8
HEADS, HID = 8, 64
HC = HEADS * HID
N_LOOP = 625
WINDOWS = -(-N // P)
W = WINDOWS + WINDOWS % 2
NP = W * P
B = 4
GROUP = B * P
GROUPS = -(-E // GROUP)
V = GROUPS + WINDOWS - 1
UNROLL = 4
CH = -(-GROUPS // P)
G_LAST = GROUPS - (CH - 1) * P
E_LAST = E - (GROUPS - 1) * GROUP
LOOP_W = -(-N_LOOP // P)
ROW = HC + 2 * HEADS
LN_EPS = 1e-5
SLOPE = 0.2
TINY = 1e-37

assert V % UNROLL == 0 and W % 2 == 0

LOOKUP = ("norm", "att1", "att8")
PHASES = [("pass", "count"), ("pass", "plain"), ("dense", "gcn1"), ("pass", "plain"), ("dense", "gcn2"),
          ("dense", "rel"), ("dense", "self"), ("pass", "norm"), ("pass", "plain"), ("dense", "mix"), ("dense", "gate"),
          ("dense", "h1"), ("pass", "att8"), ("dense", "h2"), ("pass", "att8"), ("dense", "h3"), ("pass", "att1")]
N_WEIGHTS = 9 + 2 + 2 + 3 + 6 + 2 + 3
DENSE = {"gcn1": (1, D, 0), "gcn2": (1, D, 0), "rel": (1, R * D, R * D), "self": (1, D, 0), "mix": (2, D, 0),
         "gate": (2, D, 0), "h1": (1, ROW, HC), "h2": (HC // P, ROW, HC), "h3": (HC // P, D + 2, D)}


def gained(kind, what):
    if kind == "pass":
        out = {"onehot_ready": V + 1, "sum_ready": V, "sum_added": V}
        if what in LOOKUP:
            out.update({"transposed": V + 1, "transposed_copied": V + 1, "looked_up": V + 1})
        if what != "plain":
            out["weighted"] = V
        if what in LOOKUP:
            out.update({"factor_made": V, "coef_made": 2 * V if what == "norm" else V})
        if what != "count":
            out.update({"index_staged": V, "gathered": V // 2 * 16})
        return out
    out = {"tile_staged": W, "tile_transposed": W, "tile_copied": W, "product_ready": W, "product_copied": W}
    if DENSE[what][2]:
        out["row_stored"] = W // 2 * 16
    return out


def before(phase, name):
    return sum(gained(*PHASES[k]).get(name, 0) for k in range(phase))


def gnn_kernel(nc, a, out):
    ctx = ExitStack()
    with ctx:
        def sb(name, shape, dt=F32):
            return ctx.enter_context(nc.sbuf_tensor(name, shape, dt))

        def ps(name, shape):
            return ctx.enter_context(nc.psum_tensor(name, shape, F32))

        sems = {}

        def sem(name):
            if name not in sems:
                sems[name] = ctx.enter_context(nc.semaphore(name))
            return sems[name]

        node_table = [nc.dram_tensor(f"node_table{k}", [NP, D], F32).ap() for k in range(3)]
        rel_table = nc.dram_tensor("rel_table", [NP, R * D], F32).ap()
        att_table = [nc.dram_tensor(f"att_table{k}", [NP, ROW], F32).ap() for k in range(2)]
        out_table = nc.dram_tensor("att_table2", [NP, D + 3], F32).ap()

        ident = sb("ident", [P, P])
        ones = sb("ones", [P, P])
        iota_col = sb("iota_col", [P, P])
        iota_part = sb("iota_part", [P, 1])
        iota_rel = sb("iota_rel", [P, B, R])
        iota_visit = sb("iota_visit", [P, V])
        thresholds = sb("thresholds", [P, WINDOWS - 1])
        above = sb("above", [P, WINDOWS - 1])
        step_visit = sb("step_visit", [P, WINDOWS - 1])
        step_int = sb("step_int", [P, WINDOWS - 1], I32)
        window_f = sb("window_f", [P, V])
        group_f = sb("group_f", [P, V])
        window_of = sb("window_of", [P, V + UNROLL], I32)
        edge_row = sb("edge_row", [P, V, B], I32)
        edge_rel_row = sb("edge_rel_row", [P, V, B], I32)
        edge_dst = sb("edge_dst", [P, V + 1, B])
        edge_type = sb("edge_type", [P, V, B])

        wide = sb("wide", [P, W, HC + HEADS])
        x_cur = sb("x_cur", [P, W, D])
        rel_norm = sb("rel_norm", [P, W, R])
        count = sb("count", [P, W])
        dis = sb("dis", [P, W])
        stat = sb("stat", [P, W])
        ab = sb("ab", [P, W, 2 * HEADS])
        uf = sb("uf", [P, W, 2 * HEADS])
        tv = sb("tv", [P, W, 2 * HEADS])
        peak = sb("peak", [P, HEADS])
        peak_all = sb("peak_all", [P, HEADS])
        loop_mask = sb("loop_mask", [P, LOOP_W])
        has = sb("has", [P, W])

        w_gcn = sb("w_gcn", [P, 2, D])
        w_rel = sb("w_rel", [P, R, D])
        w_self = sb("w_self", [P, D])
        w_mix = sb("w_mix", [P, 2, D])
        w_gate = sb("w_gate", [P, 2, D])
        w_h1 = sb("w_h1", [P, 1, ROW])
        w_h2 = sb("w_h2", [P, HC // P, ROW])
        w_h3 = sb("w_h3", [P, HC // P, D + 2])
        rows = sb("rows", [P, 9 * D])
        bias_wide = sb("bias_wide", [P, 2, HC])

        rows_g = sb("rows_g", [P, 2, B, ROW])
        rows_w = sb("rows_w", [P, 2, B, HC + HEADS])
        onehot = sb("onehot", [P, UNROLL, B, P])
        onehot_t = sb("onehot_t", [P, 2, B, P])
        index_now = sb("index_now", [P, 2, B], I32)
        factor = sb("factor", [P, B, 2 * HEADS])
        coef = sb("coef", [P, B])
        rel_hot = sb("rel_hot", [P, 2, B, R])
        tile_in = sb("tile_in", [P, 2, HC])
        tile_t = sb("tile_t", [P, 2, HC])
        tile_out = rows_w[:, :, :, :].rearrange("p s b c -> p s (b c)")
        loop_rows = rows_g[:, :, :, :].rearrange("p s b c -> p (s b c)")[:, 0:LOOP_W * HC].rearrange("p (w c) -> p w c", c=HC)
        flat = wide[:, :, :].rearrange("p w c -> p (w c)")
        raw = flat[:, 0:CH * 3 * GROUP].bitcast(I32).rearrange("p (c k e) -> p c k e", c=CH, k=3)
        lists = flat[:, CH * 3 * GROUP:2 * CH * 3 * GROUP].rearrange("p (c k e) -> p c k e", c=CH, k=3)
        select = flat[:, 2 * CH * 3 * GROUP:2 * CH * 3 * GROUP + CH * V].rearrange("p (c v) -> p c v", c=CH)
        compare = flat[:, 2 * CH * 3 * GROUP + CH * V:2 * CH * 3 * GROUP + CH * V + CH * GROUP]
        cat = flat[:, 0:W * 2 * D].rearrange("p (w c) -> p w c", w=W)
        z = flat[:, W * 2 * D:W * 3 * D].rearrange("p (w c) -> p w c", w=W)
        acc = flat[:, W * 3 * D:W * (4 * D + 1)].rearrange("p (w c) -> p w c", w=W)
        spare = rows_w[:, :, :, :].rearrange("p s b c -> p (s b c)")[:, 0:W * D].rearrange("p (w c) -> p w c", w=W)
        setup_rows = rows_g[:, :, :, :].rearrange("p s b c -> p (s b c)")
        att_rows = {"h1": setup_rows[:, 0:2 * HC].rearrange("p (k c) -> p k c", k=2),
                    "h2": setup_rows[:, 2 * HC:4 * HC].rearrange("p (k c) -> p k c", k=2),
                    "h3": setup_rows[:, 4 * HC:4 * HC + 2 * D].rearrange("p (k c) -> p k c", k=2)}
        setup_product = setup_rows[:, 5 * HC:6 * HC]

        ps_sum = ps("ps_sum", [P, 2, 512])
        ps_tail = ps("ps_tail", [P, 2, 512])
        ps_t = ps("ps_t", [P, 2, 512])
        ps_v = ps("ps_v", [P, 2, 512])

        BIAS = {}
        for k, name in enumerate(["L0_gnn_b1", "L0_gnn_b2", "L1_gnn_bias", "L2_gnn_b_self", "L2_gnn_b_neigh",
                                  "L2_gnn_b_gate", "L2_gnn_ln_gamma", "L2_gnn_ln_beta", "L3_gnn_b3"]):
            BIAS[name] = rows[:, k * D:(k + 1) * D]

        def over_windows(row):
            return row.unsqueeze(1).to_broadcast([P, W, row.shape[-1]])

        def over_features(column, n=D):
            return column.unsqueeze(2).to_broadcast([P, column.shape[1], n])

        def gather_table(phase):
            n_before = sum(1 for k in range(phase) if PHASES[k] == ("pass", "plain"))
            att_before = sum(1 for k in range(phase) if PHASES[k] == ("pass", "att8"))
            kind = PHASES[phase][1]
            if kind == "plain":
                return node_table[n_before], edge_row, D
            if kind == "norm":
                return rel_table.rearrange("n (r c) -> (n r) c", c=D), edge_rel_row, D
            if kind == "att8":
                return att_table[att_before], edge_row, ROW
            return out_table, edge_row, D + 3

        def lookup_values(kind):
            return (rel_norm, R) if kind == "norm" else (tv, 2 if kind == "att1" else 2 * HEADS)

        def loop_tiles(eng, head, body):
            head()
            body(0, 0, 0, False)
            body(1, 1, 0, False)
            with eng.Fori(1, W // 2 - 1) as i:
                body(i * 2, 0, i, False)
                body(i * 2 + 1, 1, i, False)
            body(W - 2, 0, W // 2 - 1, False)
            body(W - 1, 1, W // 2 - 1, True)

        def later(n, at):
            return not isinstance(n, int) or n >= at

        def loop_visits(eng, head, body, tail):
            head()
            for n in range(UNROLL):
                body(n, n)
            with eng.Fori(1, V // UNROLL) as i:
                for k in range(UNROLL):
                    body(i * UNROLL + k, k)
            tail()

        block = ctx.enter_context(nc.Block())

        @block.sync
        def _(sp):
            sp.wait_ge(sem("lists_cleared"), 1)
            for k, name in enumerate(["src", "dst", "edge_type_8"]):
                e = a[name]
                full = P * GROUP
                for c in range(CH - 1):
                    sp.dma_start(raw[:, c, k, :], e[c * full:(c + 1) * full].rearrange("(g e) -> g e", e=GROUP)).then_inc(sem("edges_loaded"), 16)
                start = (CH - 1) * full
                sp.dma_start(raw[0:G_LAST - 1, CH - 1, k, :],
                             e[start:start + (G_LAST - 1) * GROUP].rearrange("(g e) -> g e", e=GROUP)).then_inc(sem("edges_loaded"), 16)
                sp.dma_start(raw[G_LAST - 1:G_LAST, CH - 1, k, 0:E_LAST],
                             e[E - E_LAST:E].rearrange("(g e) -> g e", g=1)).then_inc(sem("edges_loaded"), 16)
            full = (N // P) * P
            sp.wait_ge(sem("x_cleared"), 1)
            sp.dma_start(x_cur[:, 0:N // P, :], a["x"][0:full, :].rearrange("(w p) c -> p w c", p=P)).then_inc(sem("x_loaded"), 16)
            sp.dma_start(x_cur[0:N - full, N // P, :], a["x"][full:N, :]).then_inc(sem("x_loaded"), 16)
            for name, row in BIAS.items():
                sp.dma_start(row, a[name].partition_broadcast(P)).then_inc(sem("weights_loaded"), 16)
            sp.dma_start(w_gcn[:, 0, :], a["L0_gnn_W1"]).then_inc(sem("weights_loaded"), 16)
            sp.dma_start(w_gcn[:, 1, :], a["L0_gnn_W2"]).then_inc(sem("weights_loaded"), 16)
            sp.dma_start(w_rel[:, :, :], a["L1_gnn_weight"].rearrange("r d o -> d r o")).then_inc(sem("weights_loaded"), 16)
            sp.dma_start(w_self[:, :], a["L1_gnn_self_weight"]).then_inc(sem("weights_loaded"), 16)
            sp.dma_start(tile_in[:, 0, 0:D], a["L2_gnn_W_self"]).then_inc(sem("weights_loaded"), 16)
            sp.dma_start(tile_in[:, 0, D:2 * D], a["L2_gnn_W_neigh"]).then_inc(sem("weights_loaded"), 16)
            sp.dma_start(tile_in[:, 0, 2 * D:4 * D], a["L2_gnn_W_gate"]).then_inc(sem("weights_loaded"), 16)
            sp.dma_start(w_h1[:, 0, 0:HC], a["L3_gnn_W1"]).then_inc(sem("weights_loaded"), 16)
            sp.dma_start(w_h2[:, :, 0:HC], a["L3_gnn_W2"].rearrange("(k p) c -> p k c", p=P)).then_inc(sem("weights_loaded"), 16)
            for k, side in enumerate(("src", "dst")):
                for layer, name in enumerate(("h1", "h2", "h3"), 1):
                    sp.dma_start(att_rows[name][:, k, :], a[f"L3_gnn_a_{side}{layer}"].rearrange("h c -> (h c)").partition_broadcast(P)).then_inc(sem("weights_loaded"), 16)
            for k in range(2):
                sp.dma_start(bias_wide[:, k, :], a[f"L3_gnn_b{k + 1}"].partition_broadcast(P)).then_inc(sem("weights_loaded"), 16)
            sp.dma_start(w_h3[:, :, 0:D], a["L3_gnn_W3"].rearrange("(k p) c -> p k c", p=P)).then_inc(sem("weights_loaded"), 16)

            node = 0
            att = 0
            for phase, (kind, what) in enumerate(PHASES):
                if kind == "pass" and what == "plain":
                    src = {0: z, 1: z, 2: x_cur}[node]
                    sp.wait_ge(sem("table_made"), node + 1)
                    sp.dma_start(node_table[node].rearrange("(w p) c -> p w c", p=P), src[:, :, :]).then_inc(sem("node_table_stored"), 16)
                    node += 1
                if kind == "dense" and DENSE[what][2]:
                    cols = DENSE[what][2]
                    table = {"rel": rel_table, "h1": att_table[0], "h2": att_table[1], "h3": out_table}[what]
                    copied, stored = before(phase, "product_copied"), before(phase, "row_stored")

                    with sp.Fori(0, W // 2) as i:
                        for s in range(2):
                            sp.wait_ge(sem("product_copied"), copied + i * 2 + s + 1)
                            sp.dma_start(table[bass.ds((i * 2 + s) * P, P), 0:cols], tile_out[:, s, 0:cols]).then_inc(sem(f"row_stored{s}"), 16)
                    for s in range(2):
                        sp.wait_ge(sem(f"row_stored{s}"), stored + W // 2 * 16)
                    sp.sem_inc(sem("rows_stored"), 1)
                if kind == "pass" and what in ("att8", "att1"):
                    att += 1
                    if what == "att8":
                        table, cols, tail = att_table[att - 1], HC, 2 * HEADS
                    else:
                        table, cols, tail = out_table, D, 3
                    sp.dma_start(loop_rows[:, :, 0:cols], table[0:LOOP_W * P, 0:cols].rearrange("(w p) c -> p w c", p=P)).then_inc(sem("loop_rows_loaded"), 16)
                    sp.wait_ge(sem("factors_made"), att)
                    sp.dma_start(table[:, cols:cols + tail].rearrange("(w p) c -> p w c", p=P), uf[:, :, 0:tail]).then_inc(sem("factors_stored"), 16)
            sp.wait_ge(sem("result_made"), 1)
            sp.dma_start(out[0:full, :].rearrange("(w p) c -> p w c", p=P), x_cur[:, 0:N // P, :]).then_inc(sem("result_stored"), 16)
            sp.dma_start(out[full:N, :], x_cur[0:N - full, N // P, :]).then_inc(sem("result_stored"), 16)
            sp.wait_ge(sem("result_stored"), 32)

        @block.gpsimd
        def _(pool):
            pool.memset(raw[:, CH - 1, :, :], 0).then_inc(sem("lists_cleared"), 1)
            pool.memset(x_cur[:, N // P:W, :], 0.0).then_inc(sem("x_cleared"), 1)
            pool.memset(ident[:, :], 0.0).then_inc(sem("ident_zero"), 1)
            pool.wait_ge(sem("ident_zero"), 1)
            pool.affine_select(out=ident[:, :], in_=ident[:, :], compare_op=ALU.not_equal, fill=1.0, base=0,
                               pattern=[[-1, P]], channel_multiplier=1).then_inc(sem("constants"), 1)
            pool.iota(iota_col[:, :], pattern=[[1, P]], base=0, channel_multiplier=0,
                      allow_small_or_imprecise_dtypes=True).then_inc(sem("constants"), 1)
            pool.iota(iota_part[:, :], pattern=[[0, 1]], base=0, channel_multiplier=1,
                      allow_small_or_imprecise_dtypes=True).then_inc(sem("constants"), 1)
            pool.iota(iota_rel[:, :, :], pattern=[[0, B], [1, R]], base=0, channel_multiplier=0,
                      allow_small_or_imprecise_dtypes=True).then_inc(sem("constants"), 1)
            pool.iota(iota_visit[:, :], pattern=[[1, V]], base=0, channel_multiplier=0,
                      allow_small_or_imprecise_dtypes=True).then_inc(sem("constants"), 1)
            pool.iota(thresholds[:, :], pattern=[[P, WINDOWS - 1]], base=P + 1, channel_multiplier=0,
                      allow_small_or_imprecise_dtypes=True).then_inc(sem("constants"), 1)
            for c in range(CH):
                pool.iota(compare[:, c * GROUP:(c + 1) * GROUP], pattern=[[1, GROUP]], base=c * P * GROUP, channel_multiplier=GROUP,
                          allow_small_or_imprecise_dtypes=True).then_inc(sem("constants"), 1)
            pool.iota(loop_mask[:, :], pattern=[[P, LOOP_W]], base=0, channel_multiplier=1,
                      allow_small_or_imprecise_dtypes=True).then_inc(sem("constants"), 1)
            pool.memset(ones[:, :], 1.0).then_inc(sem("constants"), 1)

            passes = 0
            att = 0
            node = 0
            for phase, (kind, what) in enumerate(PHASES):
                if kind != "pass":
                    continue
                passes += 1
                if what in ("att8", "att1"):
                    att += 1
                    pool.wait_ge(sem("peak_ready"), att)
                    nh = HEADS if what == "att8" else 1
                    pool.partition_all_reduce(peak_all[:, 0:nh], peak[:, 0:nh], P, bass.bass_isa.ReduceOp.max).then_inc(sem("peak_reduced"), 1)
                if what == "count":
                    continue
                table, index, cols = gather_table(phase)
                if what == "plain":
                    node += 1
                    pool.wait_ge(sem("node_table_stored"), 16 * node)
                elif what == "norm":
                    pool.wait_ge(sem("rows_stored"), 1)
                else:
                    pool.wait_ge(sem("factors_stored"), 16 * att)
                pool.wait_ge(sem("pass_begun"), passes)
                staged = before(phase, "index_staged")
                summed, weighted = before(phase, "sum_ready"), before(phase, "weighted")

                def gather(n, k):
                    s = k % 2
                    if later(n, 2):
                        if what == "att8":
                            pool.wait_ge(sem("weighted"), weighted + n - 1)
                        else:
                            pool.wait_ge(sem("sum_ready"), summed + n - 1)
                        pool.sem_inc(sem("gather_turn"), 1)
                    pool.tensor_copy(index_now[:, s:s + 1, :], index[:, bass.ds(n, 1), :]).then_inc(sem("index_staged"), 1)
                    pool.wait_ge(sem("index_staged"), staged + n + 1)
                    pool.sem_inc(sem("gather_turn"), 1)
                    for b in range(B):
                        pool.indirect_dma_start(rows_g[:, s, b, 0:cols], None, table,
                                                bass.IndirectOffsetOnAxis(ap=index_now[:, s, b:b + 1], axis=0)
                                                ).then_inc(sem(f"gathered{s * B + b}"), 16)

                loop_visits(pool, lambda: None, gather, lambda: None)

        def functions_before(what):
            if what not in ("att8", "att1"):
                return []
            nh, at = (HEADS, 0) if what == "att8" else (1, 1)
            return [(uf[:, :, at:at + nh], ACT.Exp, 1.0), (uf[:, :, at + nh:at + 2 * nh], ACT.Exp, SLOPE),
                    (tv[:, :, 0:nh], ACT.Exp, 1 - SLOPE), (tv[:, :, nh:2 * nh], ACT.Exp, SLOPE - 1)]

        def functions_after(what):
            norm = [(stat[:, :], ACT.Sqrt, 1.0)]
            if what == "count":
                return [(dis[:, :], ACT.Sqrt, 1.0)]
            if what in ("gcn2", "norm", "att1"):
                return norm
            if what == "gate":
                return [(z, ACT.Sigmoid, 1.0)] + norm + norm
            if what == "att8":
                return [(setup_rows[:, 0:n * HC], ACT.Exp, 1.0) for n in elu_parts()]
            return []

        def elu_parts():
            most = 2 * B * ROW // HC
            return [min(most, W - w) for w in range(0, W, most)]

        @block.scalar
        def _(act):
            act.wait_ge(sem("weights_turned"), 1)
            act.activation(w_mix[:, :, :].rearrange("p k c -> p (k c)"), ps_t[:, 0, 0:2 * D], ACT.Copy).then_inc(sem("weights_ready"), 1)
            act.activation(w_gate[:, :, :].rearrange("p k c -> p (k c)"), ps_t[:, 0, 2 * D:4 * D], ACT.Copy).then_inc(sem("weights_ready"), 1)
            asked = 0

            for phase, (kind, what) in enumerate(PHASES):
                for buffer, f, scale in functions_before(what):
                    asked += 1
                    act.wait_ge(sem("function_asked"), asked)
                    act.activation(buffer, buffer, f, scale=scale).then_inc(sem("function_done"), 1)
                if kind == "pass" and what in LOOKUP:
                    turned, looked = before(phase, "transposed"), before(phase, "looked_up")

                    def copy_onehot(m, k):
                        s = k % 2
                        act.wait_ge(sem("transposed"), turned + m + 1)
                        if later(m, 2):
                            act.wait_ge(sem("looked_up"), looked + m - 1)
                        act.activation(onehot_t[:, s, :, :].rearrange("p b c -> p (b c)"), ps_t[:, s, :],
                                       ACT.Copy).then_inc(sem("transposed_copied"), 1)

                    loop_visits(act, lambda: copy_onehot(0, 0), lambda n, k: copy_onehot(n + 1, k + 1), lambda: None)
                elif kind == "dense":
                    chunks, cols, to_table = DENSE[what]
                    turned, product, stored = (before(phase, x) for x in ("tile_transposed", "product_ready", "row_stored"))

                    def copy_tile(w, s):
                        act.wait_ge(sem("tile_transposed"), turned + w + 1)
                        if later(w, 2):
                            act.wait_ge(sem("product_ready"), product + w - 1)
                        act.activation(tile_t[:, s, 0:chunks * P], ps_t[:, s, 0:chunks * P], ACT.Copy).then_inc(sem("tile_copied"), 1)

                    def copy_product(w, s, turn):
                        act.wait_ge(sem("product_ready"), product + w + 1)
                        if not to_table:
                            act.activation(z[:, bass.ds(w, 1), :], ps_sum[:, s:s + 1, 0:D], ACT.Copy).then_inc(sem("product_copied"), 1)
                            return
                        if later(w, 2):
                            act.wait_ge(sem(f"row_stored{s}"), stored + turn * 16)
                        act.activation(tile_out[:, s, 0:min(to_table, 512)], ps_sum[:, s, 0:min(to_table, 512)], ACT.Copy)
                        if what == "rel":
                            last = act.activation(tile_out[:, s, 512:1024], ps_tail[:, s, :], ACT.Copy)
                        elif what == "h3":
                            last = act.activation(ab[:, bass.ds(w, 1), 0:2], ps_sum[:, s:s + 1, D:D + 2], ACT.Copy)
                        else:
                            last = act.activation(ab[:, bass.ds(w, 1), :], ps_tail[:, s:s + 1, 0:2 * HEADS], ACT.Copy)
                        last.then_inc(sem("product_copied"), 1)

                    def tile(w, s, turn, last):
                        if not last:
                            copy_tile(w + 1, 1 - s)
                        copy_product(w, s, turn)

                    loop_tiles(act, lambda: copy_tile(0, 0), tile)
                for buffer, f, scale in functions_after(what):
                    asked += 1
                    act.wait_ge(sem("function_asked"), asked)
                    act.activation(buffer, buffer, f, scale=scale).then_inc(sem("function_done"), 1)

        @block.tensor
        def _(pe):
            pe.wait_ge(sem("above_ready"), 1)
            pe.matmul(ps_v[:, 0, 0:WINDOWS - 1], ones[:, :], above[:, :], start=True, stop=True).then_inc(sem("above_summed"), 1)
            pe.wait_ge(sem("select_ready"), 1)
            for k, bank in ((0, ps_tail), (1, ps_sum), (2, ps_t)):
                for b in range(B):
                    for c in range(CH):
                        last = pe.matmul(bank[:, b // 2, b % 2 * 256:b % 2 * 256 + V], lists[:, c, k, b * P:(b + 1) * P],
                                         select[:, c, :], start=(c == 0), stop=(c == CH - 1))
            last.then_inc(sem("lists_ordered"), 1)
            pe.wait_ge(sem("weights_loaded"), 16 * N_WEIGHTS)
            pe.wait_ge(sem("lists_taken"), 1)
            for k in range(4):
                last = pe.transpose(ps_t[:, 0, k * P:(k + 1) * P], tile_in[:, 0, k * P:(k + 1) * P], ident[:, :])
            last.then_inc(sem("weights_turned"), 1)
            pe.wait_ge(sem("weights_ready"), 2 + 1)

            for phase, (kind, what) in enumerate(PHASES):
                at = {x: before(phase, x) for x in ("onehot_ready", "transposed_copied", "weighted", "gathered", "sum_added",
                                                    "tile_staged", "tile_copied", "product_copied")}
                if kind == "pass":
                    if what in LOOKUP:
                        values, n_values = lookup_values(what)

                    def look_up(m, k):
                        s, o = k % 2, k % UNROLL
                        window = pe.value_load(window_of[0:1, bass.ds(m, 1)], min_val=0, max_val=WINDOWS - 1)
                        pe.wait_ge(sem("onehot_ready"), at["onehot_ready"] + m + 1)
                        for b in range(B):
                            last = pe.transpose(ps_t[:, s, b * P:(b + 1) * P], onehot[:, o, b, :], ident[:, :])
                        last.then_inc(sem("transposed"), 1)
                        if later(m, 2):
                            pe.wait_ge(sem("weighted"), at["weighted"] + m - 1)
                        pe.wait_ge(sem("transposed_copied"), at["transposed_copied"] + m + 1)
                        for b in range(B):
                            last = pe.matmul(ps_v[:, s, b * n_values:(b + 1) * n_values], onehot_t[:, s, b, :],
                                             values[:, bass.ds(window, 1), 0:n_values], start=True, stop=True)
                        last.then_inc(sem("looked_up"), 1)

                    def sum_rows(n, k):
                        s = k % 2
                        if what == "plain":
                            pe.wait_ge(sem("onehot_ready"), at["onehot_ready"] + n + 1)
                        else:
                            pe.wait_ge(sem("weighted"), at["weighted"] + n + 1)
                        if later(n, 2):
                            pe.wait_ge(sem("sum_added"), at["sum_added"] + n - 1)
                        for b in range(B):
                            if what in ("plain", "norm"):
                                pe.wait_ge(sem(f"gathered{s * B + b}"), at["gathered"] + (n - s) * 8 + 16)
                            flags = {"start": b == 0, "stop": b == B - 1}
                            hot = onehot[:, k, b, :]
                            if what == "count":
                                last = pe.matmul(ps_sum[:, s, 0:R], hot, rel_hot[:, s, b, :], **flags)
                            elif what == "att8":
                                pe.matmul(ps_sum[:, s, :], hot, rows_w[:, s, b, 0:HC], **flags)
                                last = pe.matmul(ps_tail[:, s, 0:HEADS], hot, rows_w[:, s, b, HC:HC + HEADS], **flags)
                            else:
                                cols = D + 1 if what == "att1" else D
                                last = pe.matmul(ps_sum[:, s, 0:cols], hot, rows_g[:, s, b, 0:cols], **flags)
                        last.then_inc(sem("sum_ready"), 1)

                    def visit(n, k):
                        if what in LOOKUP:
                            look_up(n + 1, k + 1)
                        sum_rows(n, k)

                    loop_visits(pe, (lambda: look_up(0, 0)) if what in LOOKUP else (lambda: None), visit, lambda: None)
                else:
                    chunks, cols, to_table = DENSE[what]
                    weights = {"gcn1": w_gcn[:, 0:1, :], "gcn2": w_gcn[:, 1:2, :], "rel": w_rel[:, :, :].rearrange("p r c -> p (r c)").unsqueeze(1),
                               "self": w_self[:, :].unsqueeze(1), "mix": w_mix, "gate": w_gate, "h1": w_h1, "h2": w_h2, "h3": w_h3}[what]

                    def turn_tile(w, s):
                        pe.wait_ge(sem("tile_staged"), at["tile_staged"] + w + 1)
                        if later(w, 2):
                            pe.wait_ge(sem("tile_copied"), at["tile_copied"] + w - 1)
                        for c in range(chunks):
                            last = pe.transpose(ps_t[:, s, c * P:(c + 1) * P], tile_in[:, s, c * P:(c + 1) * P], ident[:, :])
                        last.then_inc(sem("tile_transposed"), 1)

                    def product(w, s):
                        pe.wait_ge(sem("tile_copied"), at["tile_copied"] + w + 1)
                        if later(w, 2):
                            pe.wait_ge(sem("product_copied"), at["product_copied"] + w - 1)
                        for c in range(chunks):
                            for lo, bank in ((0, ps_sum), (512, ps_tail)):
                                n = min(512, cols - lo)
                                if n > 0:
                                    last = pe.matmul(bank[:, s, 0:n], tile_t[:, s, c * P:(c + 1) * P], weights[:, c, lo:lo + n],
                                                     start=(c == 0), stop=(c == chunks - 1))
                        last.then_inc(sem("product_ready"), 1)

                    def tile(w, s, turn, last):
                        if not last:
                            turn_tile(w + 1, 1 - s)
                        product(w, s)

                    loop_tiles(pe, lambda: turn_tile(0, 0), tile)

        @block.vector
        def _(dve):
            steps = 0

            def step(ins):
                nonlocal steps
                steps += 1
                ins.then_inc(sem("dve_step"), 1)
                dve.wait_ge(sem("dve_step"), steps)

            asked = 0

            def ask():
                nonlocal asked
                asked += 1
                dve.sem_inc(sem("function_asked"), 1)
                dve.wait_ge(sem("function_done"), asked)

            def tt(out_, x, y, op):
                step(dve.tensor_tensor(out_, x, y, op))

            def layer_norm(x, scratch):
                step(dve.tensor_reduce(stat[:, :], x, AX, ALU.add))
                step(dve.tensor_scalar(stat[:, :], stat[:, :], 1.0 / D, None, ALU.mult))
                tt(x, x, over_features(stat[:, :]), ALU.subtract)
                tt(scratch, x, x, ALU.mult)
                step(dve.tensor_reduce(stat[:, :], scratch, AX, ALU.add))
                step(dve.tensor_scalar(stat[:, :], stat[:, :], 1.0 / D, LN_EPS, ALU.mult, ALU.add))
                ask()
                step(dve.reciprocal(stat[:, :], stat[:, :]))
                tt(x, x, over_features(stat[:, :]), ALU.mult)

            dve.wait_ge(sem("constants"), 8 + CH)
            dve.wait_ge(sem("edges_loaded"), 16 * 3 * (CH + 1))
            dve.tensor_copy(lists[:, :, 0, :], raw[:, :, 0, :])
            dve.tensor_copy(lists[:, :, 2, :], raw[:, :, 2, :])
            edge_ok = compare.rearrange("p (c e) -> p c e", c=CH)
            step(dve.tensor_scalar(edge_ok, edge_ok, float(E), None, ALU.is_lt))
            step(dve.tensor_scalar(lists[:, :, 1, :], raw[:, :, 1, :], 1.0, None, ALU.add))
            tt(lists[:, :, 1, :], lists[:, :, 1, :], edge_ok, ALU.mult)
            with dve.Fori(0, WINDOWS - 1) as k:
                dve.tensor_scalar(edge_ok, lists[:, :, 1, :], thresholds[:, bass.ds(k, 1)], None, ALU.is_ge).then_inc(sem("compared"), 1)
                dve.wait_ge(sem("compared"), k + 1)
                dve.tensor_reduce(above[:, bass.ds(k, 1)], edge_ok, mybir.AxisListType.XY, ALU.add).then_inc(sem("counted"), 1)
                dve.wait_ge(sem("counted"), k + 1)
            dve.sem_inc(sem("above_ready"), 1)
            step(dve.memset(window_f[:, :], 0.0))
            step(dve.memset(window_of[:, :], 0))
            dve.wait_ge(sem("above_summed"), 1)
            step(dve.tensor_scalar(step_int[:, :], ps_v[:, 0, 0:WINDOWS - 1], -1.0, float(E), ALU.mult, ALU.add))
            step(dve.tensor_scalar(step_int[:, :], step_int[:, :], GROUP.bit_length() - 1, None, ALU.arith_shift_right))
            step(dve.tensor_copy(above[:, :], step_int[:, :]))
            step(dve.tensor_scalar(step_visit[:, :], thresholds[:, :], -1.0, 1.0 / P, ALU.add, ALU.mult))
            tt(step_visit[:, :], step_visit[:, :], above[:, :], ALU.add)
            with dve.Fori(0, WINDOWS - 1) as k:
                dve.scalar_tensor_tensor(out=window_f[:, :], in0=iota_visit[:, :], scalar=step_visit[:, bass.ds(k, 1)],
                                         in1=window_f[:, :], op0=ALU.is_ge, op1=ALU.add).then_inc(sem("window_counted"), 1)
                dve.wait_ge(sem("window_counted"), k + 1)
            tt(group_f[:, :], iota_visit[:, :], window_f[:, :], ALU.subtract)
            for c in range(CH):
                step(dve.tensor_scalar(select[:, c, :], group_f[:, :], float(-c * P), iota_part[:, 0:1], ALU.add, ALU.is_equal))
            step(dve.tensor_copy(window_of[:, 0:V], window_f[:, :]))
            dve.sem_inc(sem("select_ready"), 1)
            step(dve.tensor_scalar(window_f[:, :], window_f[:, :], float(-P), -1.0, ALU.mult, ALU.add))
            step(dve.memset(edge_dst[:, V:V + 1, :], -1.0))
            dve.wait_ge(sem("lists_ordered"), 1)
            for b in range(B):
                bank = (slice(None), b // 2, slice(b % 2 * 256, b % 2 * 256 + V))
                step(dve.tensor_tensor(edge_dst[:, 0:V, b], ps_sum[bank], window_f[:, :], ALU.add))
                step(dve.tensor_copy(edge_row[:, :, b], ps_tail[bank]))
                step(dve.tensor_copy(edge_type[:, :, b], ps_t[bank]))
                step(dve.scalar_tensor_tensor(out=edge_rel_row[:, :, b], in0=ps_tail[bank], scalar=float(R),
                                              in1=edge_type[:, :, b], op0=ALU.mult, op1=ALU.add))
            dve.sem_inc(sem("lists_taken"), 1)
            step(dve.tensor_scalar(loop_mask[:, :], loop_mask[:, :], float(N_LOOP), None, ALU.is_lt))

            dve.wait_ge(sem("weights_loaded"), 16 * N_WEIGHTS)
            for name, weight, heads, c_head in (("h1", w_h1, HEADS, HID), ("h2", w_h2, HEADS, HID), ("h3", w_h3, 1, D)):
                cols = heads * c_head
                for c in range(DENSE[name][0]):
                    for side in range(2):
                        tt(setup_product[:, 0:cols], weight[:, c, 0:cols], att_rows[name][:, side, :], ALU.mult)
                        step(dve.tensor_reduce(weight[:, c, cols + side * heads:cols + (side + 1) * heads],
                                               setup_product[:, 0:cols].rearrange("p (h c) -> p h c", h=heads), AX, ALU.add))
            dve.sem_inc(sem("weights_ready"), 1)
            dve.wait_ge(sem("x_loaded"), 32)

            att = 0
            for phase, (kind, what) in enumerate(PHASES):
                at = {x: before(phase, x) for x in ("sum_ready", "sum_added", "looked_up", "gathered", "factor_made", "coef_made",
                                                    "tile_transposed", "tile_staged", "product_copied", "onehot_ready")}
                if kind == "pass":
                    nh = HEADS if what == "att8" else 1
                    if what == "count":
                        step(dve.memset(rel_norm[:, :, :], 0.0))
                    elif what in ("plain", "norm"):
                        step(dve.memset(acc, 0.0))
                    else:
                        att += 1
                        step(dve.tensor_reduce(peak[:, 0:nh], ab[:, :, 0:nh].rearrange("p w h -> p h w"), AX, ALU.max))
                        dve.sem_inc(sem("peak_ready"), 1)
                        dve.wait_ge(sem("peak_reduced"), att)
                        top = peak_all[:, 0:nh].unsqueeze(1).to_broadcast([P, W, nh])
                        first = 0 if what == "att8" else 1
                        if first:
                            step(dve.memset(uf[:, :, 0:1], 1.0))
                        tt(uf[:, :, first:first + nh], ab[:, :, 0:nh], top, ALU.subtract)
                        tt(uf[:, :, first + nh:first + 2 * nh], ab[:, :, 0:nh], top, ALU.subtract)
                        tt(ab[:, :, nh:2 * nh], ab[:, :, nh:2 * nh], top, ALU.add)
                        step(dve.tensor_scalar(tv[:, :, 0:nh], ab[:, :, nh:2 * nh], 0.0, None, ALU.min))
                        step(dve.tensor_scalar(tv[:, :, nh:2 * nh], ab[:, :, nh:2 * nh], 0.0, None, ALU.max))
                        for _ in functions_before(what):
                            ask()
                        dve.sem_inc(sem("factors_made"), 1)
                        tt(ab[:, 0:LOOP_W, 0:2 * nh], uf[:, 0:LOOP_W, first:first + 2 * nh], tv[:, 0:LOOP_W, 0:2 * nh], ALU.mult)
                        tt(ab[:, 0:LOOP_W, 0:nh], ab[:, 0:LOOP_W, 0:nh], ab[:, 0:LOOP_W, nh:2 * nh], ALU.max)
                        tt(ab[:, 0:LOOP_W, 0:nh], ab[:, 0:LOOP_W, 0:nh], loop_mask[:, :].unsqueeze(2).to_broadcast([P, LOOP_W, nh]), ALU.mult)
                        target, cols = (wide, HC) if what == "att8" else (acc, D)
                        if what == "att8":
                            step(dve.memset(wide[:, :, :], 0.0))
                        else:
                            step(dve.memset(acc, 0.0))
                        dve.wait_ge(sem("loop_rows_loaded"), 16 * att)
                        for w in range(LOOP_W):
                            dve.tensor_tensor(target[:, w, 0:cols].rearrange("p (h c) -> p h c", h=nh),
                                              loop_rows[:, w, 0:cols].rearrange("p (h c) -> p h c", h=nh),
                                              over_features(ab[:, w, 0:nh], cols // nh), ALU.mult)
                        step(dve.tensor_copy(target[:, 0:LOOP_W, cols:cols + nh], ab[:, 0:LOOP_W, 0:nh]))
                    dve.sem_inc(sem("pass_begun"), 1)

                    def make_onehot(m, k):
                        if later(m, UNROLL):
                            dve.wait_ge(sem("sum_ready"), at["sum_ready"] + m - UNROLL + 1)
                        for b in range(B):
                            last = dve.tensor_scalar(onehot[:, k % UNROLL, b, :], iota_col[:, :],
                                                     edge_dst[:, bass.ds(m, 1), b:b + 1].rearrange("p v b -> p (v b)"), None, ALU.is_equal)
                        last.then_inc(sem("onehot_ready"), 1)

                    def relations(n, s):
                        return dve.tensor_tensor(rel_hot[:, s, :, :], iota_rel[:, :, :],
                                                 edge_type[:, bass.ds(n, 1), :].rearrange("p v b -> p (v b)").unsqueeze(2).to_broadcast([P, B, R]),
                                                 ALU.is_equal)

                    def weigh(n, k):
                        s = k % 2
                        if what == "plain":
                            return
                        if what == "count":
                            if later(n, 2):
                                dve.wait_ge(sem("sum_ready"), at["sum_ready"] + n - 1)
                            relations(n, s).then_inc(sem("weighted"), 1)
                            return
                        looked = ps_v[:, s, :]
                        if what == "norm":
                            relations(n, s).then_inc(sem("factor_made"), 1)
                            dve.wait_ge(sem("factor_made"), at["factor_made"] + n + 1)
                            dve.wait_ge(sem("looked_up"), at["looked_up"] + n + 1)
                            dve.tensor_tensor(factor[:, :, 0:R], rel_hot[:, s, :, :], looked[:, 0:B * R].rearrange("p (b r) -> p b r", b=B),
                                              ALU.mult).then_inc(sem("coef_made"), 1)
                            dve.wait_ge(sem("coef_made"), at["coef_made"] + 2 * n + 1)
                            dve.tensor_reduce(coef[:, :], factor[:, :, 0:R], AX, ALU.add).then_inc(sem("coef_made"), 1)
                            dve.wait_ge(sem("coef_made"), at["coef_made"] + 2 * n + 2)
                        else:
                            for b in range(B):
                                dve.wait_ge(sem(f"gathered{s * B + b}"), at["gathered"] + (n - s) * 8 + 16)
                            dve.wait_ge(sem("looked_up"), at["looked_up"] + n + 1)
                            first = HC if what == "att8" else D + 1
                            dve.tensor_tensor(factor[:, :, 0:2 * nh], rows_g[:, s, :, first:first + 2 * nh],
                                              looked[:, 0:B * 2 * nh].rearrange("p (b r) -> p b r", b=B), ALU.mult).then_inc(sem("factor_made"), 1)
                            dve.wait_ge(sem("factor_made"), at["factor_made"] + n + 1)
                            if what == "att8" and later(n, 2):
                                dve.wait_ge(sem("sum_ready"), at["sum_ready"] + n - 1)
                            into = rows_w[:, s, :, HC:HC + nh] if what == "att8" else coef[:, :].unsqueeze(2)
                            dve.tensor_tensor(into, factor[:, :, 0:nh], factor[:, :, nh:2 * nh], ALU.max).then_inc(sem("coef_made"), 1)
                            dve.wait_ge(sem("coef_made"), at["coef_made"] + n + 1)
                        if what == "att8":
                            for b in range(B):
                                last = dve.tensor_tensor(rows_w[:, s, b, 0:HC].rearrange("p (h c) -> p h c", h=HEADS),
                                                         rows_g[:, s, b, 0:HC].rearrange("p (h c) -> p h c", h=HEADS),
                                                         over_features(rows_w[:, s, b, HC:HC + HEADS], HID), ALU.mult)
                        else:
                            for b in range(B):
                                last = dve.tensor_scalar(onehot[:, k, b, :], onehot[:, k, b, :], coef[:, b:b + 1], None, ALU.mult)
                        last.then_inc(sem("weighted"), 1)

                    def add_sum(n, k):
                        s = k % 2
                        window = dve.value_load(window_of[0:1, bass.ds(n, 1)], min_val=0, max_val=WINDOWS - 1)
                        dve.wait_ge(sem("sum_ready"), at["sum_ready"] + n + 1)
                        if later(n, 1):
                            dve.wait_ge(sem("sum_added"), at["sum_added"] + n)
                        if what == "att8":
                            dve.tensor_tensor(wide[:, bass.ds(window, 1), 0:HC], wide[:, bass.ds(window, 1), 0:HC], ps_sum[:, s:s + 1, :], ALU.add)
                            last = dve.tensor_tensor(wide[:, bass.ds(window, 1), HC:HC + HEADS], wide[:, bass.ds(window, 1), HC:HC + HEADS],
                                                     ps_tail[:, s:s + 1, 0:HEADS], ALU.add)
                        elif what == "count":
                            last = dve.tensor_tensor(rel_norm[:, bass.ds(window, 1), :], rel_norm[:, bass.ds(window, 1), :], ps_sum[:, s:s + 1, 0:R], ALU.add)
                        else:
                            cols = D + 1 if what == "att1" else D
                            last = dve.tensor_tensor(acc[:, bass.ds(window, 1), 0:cols], acc[:, bass.ds(window, 1), 0:cols],
                                                     ps_sum[:, s:s + 1, 0:cols], ALU.add)
                        last.then_inc(sem("sum_added"), 1)

                    def visit(n, k):
                        make_onehot(n + 1, k + 1)
                        weigh(n, k)
                        if later(n, 1):
                            add_sum(n - 1, k + 1)

                    loop_visits(dve, lambda: make_onehot(0, 0), visit, lambda: add_sum(V - 1, 1))
                    dve.wait_ge(sem("sum_added"), at["sum_added"] + V)
                    if what in LOOKUP:
                        dve.wait_ge(sem("looked_up"), at["looked_up"] + V + 1)
                else:
                    chunks, cols, to_table = DENSE[what]
                    source = {"rel": x_cur, "self": x_cur, "h1": x_cur, "gcn1": acc, "gcn2": acc, "mix": cat, "gate": cat,
                              "h2": wide, "h3": wide}[what]

                    def stage(w, s, turn, last):
                        if later(w, 2):
                            dve.wait_ge(sem("tile_transposed"), at["tile_transposed"] + w - 1)
                        dve.tensor_copy(tile_in[:, s:s + 1, 0:chunks * P], source[:, bass.ds(w, 1), 0:chunks * P]).then_inc(sem("tile_staged"), 1)

                    loop_tiles(dve, lambda: None, stage)
                    dve.wait_ge(sem("product_copied"), at["product_copied"] + W)

                if what == "count":
                    step(dve.tensor_reduce(count[:, :], rel_norm[:, :, :], AX, ALU.add))
                    step(dve.tensor_scalar(dis[:, :], count[:, :], 1.0, None, ALU.add))
                    ask()
                    step(dve.reciprocal(dis[:, :], dis[:, :]))
                    step(dve.tensor_scalar(rel_norm[:, :, :], rel_norm[:, :, :], 1.0, None, ALU.max))
                    step(dve.reciprocal(rel_norm[:, :, :], rel_norm[:, :, :]))
                    tt(z, x_cur[:, :, :], over_features(dis[:, :]), ALU.mult)
                    dve.sem_inc(sem("table_made"), 1)
                elif phase in (1, 3):
                    tt(acc[:, :, 0:D], acc[:, :, 0:D], z, ALU.add)
                    tt(acc[:, :, 0:D], acc[:, :, 0:D], over_features(dis[:, :]), ALU.mult)
                    dve.wait_ge(sem("node_table_stored"), 16 if phase == 1 else 32)
                elif what == "gcn1":
                    tt(z, z, over_windows(BIAS["L0_gnn_b1"]), ALU.add)
                    step(dve.tensor_scalar(z, z, 0.0, None, ALU.max))
                    tt(z, z, over_features(dis[:, :]), ALU.mult)
                    dve.sem_inc(sem("table_made"), 1)
                elif what == "gcn2":
                    tt(x_cur[:, :, :], x_cur[:, :, :], z, ALU.add)
                    tt(x_cur[:, :, :], x_cur[:, :, :], over_windows(BIAS["L0_gnn_b2"]), ALU.add)
                    layer_norm(x_cur[:, :, :], spare)
                elif what == "norm":
                    tt(x_cur[:, :, :], x_cur[:, :, :], z, ALU.add)
                    tt(x_cur[:, :, :], x_cur[:, :, :], acc[:, :, 0:D], ALU.add)
                    tt(x_cur[:, :, :], x_cur[:, :, :], over_windows(BIAS["L1_gnn_bias"]), ALU.add)
                    layer_norm(x_cur[:, :, :], spare)
                    dve.sem_inc(sem("table_made"), 1)
                elif phase == 8:
                    step(dve.tensor_scalar(has[:, :], count[:, :], 0.0, None, ALU.is_gt))
                    step(dve.tensor_scalar(count[:, :], count[:, :], 1.0, None, ALU.max))
                    step(dve.reciprocal(count[:, :], count[:, :]))
                    step(dve.tensor_copy(cat[:, :, 0:D], x_cur[:, :, :]))
                    tt(cat[:, :, D:2 * D], acc[:, :, 0:D], over_features(count[:, :]), ALU.mult)
                    dve.wait_ge(sem("node_table_stored"), 48)
                elif what == "mix":
                    tt(cat[:, :, D:2 * D], over_windows(BIAS["L2_gnn_b_neigh"]), over_features(has[:, :]), ALU.mult)
                    tt(cat[:, :, D:2 * D], cat[:, :, D:2 * D], z, ALU.add)
                    tt(cat[:, :, D:2 * D], cat[:, :, D:2 * D], over_windows(BIAS["L2_gnn_b_self"]), ALU.add)
                elif what == "gate":
                    tt(z, z, over_windows(BIAS["L2_gnn_b_gate"]), ALU.add)
                    ask()
                    tt(spare, cat[:, :, D:2 * D], x_cur[:, :, :], ALU.subtract)
                    tt(z, z, spare, ALU.mult)
                    tt(z, z, x_cur[:, :, :], ALU.add)
                    layer_norm(z, spare)
                    tt(z, z, over_windows(BIAS["L2_gnn_ln_gamma"]), ALU.mult)
                    tt(z, z, over_windows(BIAS["L2_gnn_ln_beta"]), ALU.add)
                    step(dve.tensor_scalar(z, z, 0.0, None, ALU.max))
                    tt(x_cur[:, :, :], x_cur[:, :, :], z, ALU.add)
                    layer_norm(x_cur[:, :, :], spare)
                elif what == "att8":
                    den = wide[:, :, HC:HC + HEADS]
                    step(dve.tensor_scalar(den, den, TINY, None, ALU.max))
                    step(dve.reciprocal(den, den))
                    heads = wide[:, :, 0:HC].rearrange("p w (h c) -> p w h c", h=HEADS)
                    tt(heads, heads, den.unsqueeze(3).to_broadcast([P, W, HEADS, HID]), ALU.mult)
                    tt(wide[:, :, 0:HC], wide[:, :, 0:HC], over_windows(bias_wide[:, att - 1, :]), ALU.add)
                    w = 0
                    for n in elu_parts():
                        part = wide[:, w:w + n, 0:HC]
                        low = setup_rows[:, 0:n * HC].rearrange("p (w c) -> p w c", w=n)
                        step(dve.tensor_scalar(low, part, 0.0, None, ALU.min))
                        ask()
                        step(dve.scalar_tensor_tensor(out=part, in0=low, scalar=-1.0, in1=part, op0=ALU.add, op1=ALU.max))
                        w += n
                elif what == "att1":
                    step(dve.tensor_scalar(stat[:, :], acc[:, :, D], TINY, None, ALU.max))
                    step(dve.reciprocal(stat[:, :], stat[:, :]))
                    tt(acc[:, :, 0:D], acc[:, :, 0:D], over_features(stat[:, :]), ALU.mult)
                    tt(x_cur[:, :, :], x_cur[:, :, :], acc[:, :, 0:D], ALU.add)
                    tt(x_cur[:, :, :], x_cur[:, :, :], over_windows(BIAS["L3_gnn_b3"]), ALU.add)
                    layer_norm(x_cur[:, :, :], spare)
                    dve.sem_inc(sem("result_made"), 1)


def kernel(**inputs):
    import numpy as np
    import concourse.bacc as bacc
    from concourse.bass_utils import run_bass_kernel_spmd

    nc = bacc.Bacc("TRN2", target_bir_lowering=False, num_devices=1)
    arrays, args = {}, {}
    for name, value in inputs.items():
        value = np.ascontiguousarray(value)
        arrays[f"in_{name}"] = value
        args[name] = nc.dram_tensor(f"in_{name}", value.shape, mybir.dt.from_np(value.dtype), kind="ExternalInput").ap()
    result = nc.dram_tensor("result", (N, D), F32, kind="ExternalOutput").ap()
    gnn_kernel(nc, args, result)
    return run_bass_kernel_spmd(nc, [arrays], core_ids=[0]).results[0]["result"]
```

```python
from contextlib import ExitStack

import concourse.bass as bass
from concourse import mybir

F32 = mybir.dt.float32
I32 = mybir.dt.int32
F16 = mybir.dt.float16
ALU = mybir.AluOpType
ACT = mybir.ActivationFunctionType
AX = mybir.AxisListType.X

P = 128
N = 3125
E = 100000
D = 128
R = 8
HEADS, HID = 8, 64
HC = HEADS * HID
HALF = (HC + HEADS) // 2
N_LOOP = 625
WINDOWS = -(-N // P)
W = WINDOWS + WINDOWS % 2
NP = W * P
B = 4
GROUP = B * P
GROUPS = -(-E // GROUP)
V = GROUPS + WINDOWS - 1
UNROLL = 4
AHEAD = 3
TILES = -(-E // P)
T_PAD = -(-TILES // (2 * UNROLL)) * 2 * UNROLL
DEG_LO = 25
DEG_HI = N // DEG_LO
CW = 16
CW_BLOCK = P // CW
C_WINDOWS = WINDOWS * CW_BLOCK
CB = 2
C_GROUPS = -(-E // (CB * P))
CV = -(-(C_GROUPS + C_WINDOWS - 1) // UNROLL) * UNROLL
C_COLS = WINDOWS * CW
RING = 8
STORE_LAG = 4
LOOP_W = -(-N_LOOP // P)
ROW = HC + 2 * HEADS
LN_EPS = 1e-5
SLOPE = 0.2
TINY = 1e-37

N_CONST = 13
assert V % UNROLL == 0 and W % 2 == 0 and DEG_HI * DEG_LO == N and CW_BLOCK == RING

PHASES = [("blocks", "plain"), ("dense", "gcn1"), ("blocks", "plain"), ("dense", "gcn2"),
          ("dense", "rel"), ("dense", "self"), ("pass", "norm"), ("blocks", "plain"), ("dense", "mix"), ("dense", "gate"),
          ("dense", "h1"), ("pass", "att8"), ("dense", "h2"), ("pass", "att8"), ("dense", "h3"), ("blocks", "att1")]
L0_SUM1, L0_SUM2, L2_SUM = (k for k, x in enumerate(PHASES) if x == ("blocks", "plain"))
N_WEIGHTS = 9 + 2 + 2 + 3 + 6 + 2 + 3
DENSE = {"gcn1": (1, D, 0), "gcn2": (1, D, 0), "rel": (1, R * D, R * D), "self": (1, D, 0), "mix": (2, D, 0),
         "gate": (2, D, 0), "h1": (1, ROW, HC), "h2": (HC // P, ROW, HC), "h3": (HC // P, D + 2, 0)}


def gained(kind, what):
    if kind == "pass":
        return {"onehot_ready": V + 2, "sum_ready": V, "sum_added": V, "transposed": V + 2, "transposed_copied": V + 2,
                "looked_up": V + 1, "weighted": V, "factor_made": V, "coef_made": 2 * V if what == "norm" else V,
                "index_staged": V + AHEAD, "gathered": V // 2 * 16}
    if kind == "blocks":
        out = {"block_summed": WINDOWS, "block_copied": WINDOWS, "block_loaded0": (WINDOWS + 1) // 2 * 16, "block_loaded1": WINDOWS // 2 * 16}
        if what == "att1":
            out.update({"slope1_made": WINDOWS, "slope2_made": WINDOWS, "slopes_joined": WINDOWS, "block_weighed": WINDOWS})
        return out
    out = {"tile_staged": W, "tile_transposed": W, "tile_copied": W, "product_ready": W, "product_copied": W}
    if DENSE[what][2]:
        out["row_stored"] = W // 2 * 16
    return out


def before(phase, name):
    return sum(gained(*PHASES[k]).get(name, 0) for k in range(phase))


def gnn_kernel(nc, a, out):
    ctx = ExitStack()
    with ctx:
        def sb(name, shape, dt=F32):
            return ctx.enter_context(nc.sbuf_tensor(name, shape, dt))

        def ps(name, shape):
            return ctx.enter_context(nc.psum_tensor(name, shape, F32))

        sems = {}

        def sem(name):
            if name not in sems:
                sems[name] = ctx.enter_context(nc.semaphore(name))
            return sems[name]

        c_matrix = nc.dram_tensor("c_matrix", [WINDOWS, P, CW_BLOCK, C_COLS], F32).ap()
        degree_rows = nc.dram_tensor("degree_rows", [NP * R], F32).ap()
        rel_table = nc.dram_tensor("rel_table", [NP, R * D], F32).ap()
        att_table = [nc.dram_tensor(f"att_table{k}", [NP, ROW], F32).ap() for k in range(2)]
        target_rows = nc.dram_tensor("target_rows", [2, NP], F32).ap()

        ident = sb("ident", [P, P])
        ones = sb("ones", [P, P])
        iota_col = sb("iota_col", [P, P])
        iota_part = sb("iota_part", [P, 1])
        iota_rel = sb("iota_rel", [P, B, R])
        iota_visit = sb("iota_visit", [P, CV])
        iota_row = sb("iota_row", [P, C_WINDOWS])
        iota_node = sb("iota_node", [P, DEG_LO])
        iota_deg = sb("iota_deg", [P, DEG_LO * R], F16)
        iota_16 = sb("iota_16", [P, P], F16)
        iota_c = sb("iota_c", [P, C_COLS], F16)
        window_of = sb("window_of", [P, V + UNROLL], I32)
        c_window = sb("c_window", [P, CV], I32)
        c_slot = sb("c_slot", [P, CV], I32)
        c_keep = sb("c_keep", [P, CV])
        c_end = sb("c_end", [P, C_WINDOWS], I32)
        edge_row = sb("edge_row", [P, V + AHEAD, B], I32)
        edge_rel_row = sb("edge_rel_row", [P, V + AHEAD, B], I32)
        edge_dst = sb("edge_dst", [P, V + 2, B])
        edge_type = sb("edge_type", [P, V, B])

        wide = sb("wide", [P, W, HC + HEADS])
        x_cur = sb("x_cur", [P, W, D])
        rel_norm = sb("rel_norm", [P, W, R])
        zero_row = sb("zero_row", [1, (NP - N) * R])
        count = sb("count", [P, W])
        dis = sb("dis", [P, W])
        stat = sb("stat", [P, W])
        ab = sb("ab", [P, W, 2 * HEADS])
        rel_degree = sb("rel_degree", [P, DEG_LO * R])
        node_degree = sb("node_degree", [P, DEG_LO])
        uf = sb("uf", [P, W, 2 * HEADS])
        tv = sb("tv", [P, W, 2 * HEADS])
        peak = sb("peak", [P, HEADS])
        peak_all = sb("peak_all", [P, HEADS])
        loop_mask = sb("loop_mask", [P, LOOP_W])
        has = sb("has", [P, W])

        w_gcn = sb("w_gcn", [P, 2, D])
        w_rel = sb("w_rel", [P, R, D])
        w_self = sb("w_self", [P, D])
        w_mix = sb("w_mix", [P, 2, D])
        w_gate = sb("w_gate", [P, 2, D])
        w_h1 = sb("w_h1", [P, 1, ROW])
        w_h2 = sb("w_h2", [P, HC // P, ROW])
        w_h3 = sb("w_h3", [P, HC // P, D + 2])
        rows = sb("rows", [P, 9 * D])
        bias_wide = sb("bias_wide", [P, 2, HC])

        rows_g = sb("rows_g", [P, 2, B, ROW])
        rows_w = sb("rows_w", [P, 2, B, HC + HEADS])
        onehot = sb("onehot", [P, UNROLL, B, P])
        onehot_t = sb("onehot_t", [P, 2, B, P])
        index_now = sb("index_now", [P, UNROLL, B], I32)
        factor = sb("factor", [P, B, 2 * HEADS])
        coef = sb("coef", [P, B])
        rel_hot = sb("rel_hot", [P, 2, B, R])
        tile_in = sb("tile_in", [P, 2, HC])
        tile_t = sb("tile_t", [P, 2, HC])
        tile_out = rows_w[:, :, :, :].rearrange("p s b c -> p s (b c)")
        loop_rows = rows_g[:, :, :, :].rearrange("p s b c -> p (s b c)")[:, 0:LOOP_W * HC].rearrange("p (w c) -> p w c", c=HC)

        flat = wide[:, :, :].rearrange("p w c -> p (w c)")
        CH, CCH = -(-GROUPS // P), -(-C_GROUPS // P)
        taken = [0]

        def scratch(cols, dt=F32):
            part = flat[:, taken[0]:taken[0] + cols]
            taken[0] += cols
            assert taken[0] <= W * (HC + HEADS)
            return part if dt is F32 else part.bitcast(dt)

        raw = scratch(CH * 3 * GROUP, I32).rearrange("p (c k e) -> p c k e", c=CH, k=3)
        c_raw = scratch(CCH * 2 * CB * P, I32).rearrange("p (c k e) -> p c k e", c=CCH, k=2)
        p_list, c_list = (flat[:, at:at + n].rearrange("p (c k e) -> p c k e", c=c, k=k)
                          for at, n, c, k in ((0, CH * 3 * GROUP, CH, 3), (CH * 3 * GROUP, CCH * 2 * CB * P, CCH, 2)))
        select = scratch(CH * V).rearrange("p (c v) -> p c v", c=CH)
        c_select = scratch(CCH * CV).rearrange("p (c v) -> p c v", c=CCH)
        free_order = scratch(2 * T_PAD, I32).rearrange("p (k t) -> p k t", k=2)
        deg_hi, deg_lo, deg_tmp = scratch(T_PAD), scratch(T_PAD), scratch(T_PAD)
        deg_int = scratch(T_PAD, I32)
        g_flat = rows_g[:, :, :, :].rearrange("p s b c -> p (s b c)")
        w_flat = rows_w[:, :, :, :].rearrange("p s b c -> p (s b c)")
        TH = 100
        below = w_flat[:, 0:TH * DEG_LO].rearrange("p (k d) -> p k d", k=TH)
        above = sb("above", [P, C_WINDOWS])
        step_row = sb("step_row", [P, C_WINDOWS])
        step_int = sb("step_int", [P, C_WINDOWS], I32)
        step_col = sb("step_col", [P, 4])
        window_f = sb("window_f", [P, CV])
        group_f = sb("group_f", [P, CV])
        reached = w_flat[:, 0:2 * CV].rearrange("p (c v) -> p c v", c=2)
        c_lo = sb("c_lo", [P, CV + 1, CB])
        c_key = sb("c_key", [P, CV + 1, CB])
        deg_hot = w_flat[:, 0:UNROLL * DEG_LO * R].bitcast(F16).rearrange("p (u c) -> p u c", u=2 * UNROLL)
        hi_hot = g_flat[:, RING * C_COLS:RING * C_COLS + UNROLL * P].bitcast(F16).rearrange("p (u c) -> p u c", u=2 * UNROLL)
        lo_hot = onehot[:, :, :, :].rearrange("p u b c -> p (u b c)")[:, 0:UNROLL * CB * P // 2].bitcast(F16) \
            .rearrange("p (u b c) -> p u b c", u=UNROLL, b=CB)
        key_hot = w_flat[:, 0:UNROLL * CB * C_COLS // 2].bitcast(F16).rearrange("p (u b c) -> p u b c", u=UNROLL, b=CB)
        c_int = tile_t[:, :, :].rearrange("p s c -> p (s c)")[:, 0:CV].bitcast(I32).rearrange("p (k v) -> p k v", k=2)
        ring = g_flat[:, 0:RING * C_COLS].rearrange("p (k c) -> p k c", k=RING)
        cat = flat[:, 0:W * 2 * D].rearrange("p (w c) -> p w c", w=W)
        z = flat[:, W * 2 * D:W * 3 * D].rearrange("p (w c) -> p w c", w=W)
        acc = flat[:, W * 3 * D:W * (4 * D + 1)].rearrange("p (w c) -> p w c", w=W)
        spare = rows_w[:, :, :, :].rearrange("p s b c -> p (s b c)")[:, 0:W * D].rearrange("p (w c) -> p w c", w=W)
        setup_rows = g_flat
        c_block = flat[:, 0:2 * CW_BLOCK * C_COLS].rearrange("p (s d h) -> p s d h", s=2, h=WINDOWS)
        slope1 = g_flat[:, 0:CW_BLOCK * C_COLS].rearrange("p (d h) -> p d h", h=WINDOWS)
        slope2 = flat[:, W * 2 * D:W * 2 * D + CW_BLOCK * C_COLS].rearrange("p (d h) -> p d h", h=WINDOWS)
        h_one = w_flat[:, 0:W * (D + 1)].rearrange("p (w c) -> p w c", w=W)
        target_now = tile_t[:, :, 0:2 * P].rearrange("p s (k d) -> p s k d", k=2)
        att_rows = {"h1": setup_rows[:, 0:2 * HC].rearrange("p (k c) -> p k c", k=2),
                    "h2": setup_rows[:, 2 * HC:4 * HC].rearrange("p (k c) -> p k c", k=2),
                    "h3": setup_rows[:, 4 * HC:4 * HC + 2 * D].rearrange("p (k c) -> p k c", k=2)}
        setup_product = setup_rows[:, 5 * HC:6 * HC]

        ps_sum = ps("ps_sum", [P, 2, 512])
        ps_tail = ps("ps_tail", [P, 2, 512])
        ps_t = ps("ps_t", [P, 2, 512])
        ps_v = ps("ps_v", [P, 2, 512])

        BIAS = {}
        for k, name in enumerate(["L0_gnn_b1", "L0_gnn_b2", "L1_gnn_bias", "L2_gnn_b_self", "L2_gnn_b_neigh",
                                  "L2_gnn_b_gate", "L2_gnn_ln_gamma", "L2_gnn_ln_beta", "L3_gnn_b3"]):
            BIAS[name] = rows[:, k * D:(k + 1) * D]

        def over_windows(row):
            return row.unsqueeze(1).to_broadcast([P, W, row.shape[-1]])

        def over_features(column, n=D):
            return column.unsqueeze(2).to_broadcast([P, column.shape[1], n])

        def gather_table(phase):
            att_before = sum(1 for k in range(phase) if PHASES[k] == ("pass", "att8"))
            kind = PHASES[phase][1]
            if kind == "norm":
                return rel_table.rearrange("n (r c) -> (n r) c", c=D), edge_rel_row, D
            return att_table[att_before], edge_row, ROW

        def lookup_values(kind):
            return (rel_norm, R) if kind == "norm" else (tv, 2 * HEADS)

        def loop_tiles(eng, head, body):
            head()
            body(0, 0, 0, False)
            body(1, 1, 0, False)
            with eng.Fori(1, W // 2 - 1) as i:
                body(i * 2, 0, i, False)
                body(i * 2 + 1, 1, i, False)
            body(W - 2, 0, W // 2 - 1, False)
            body(W - 1, 1, W // 2 - 1, True)

        def loop_blocks(eng, body):
            body(0, 0, 0)
            body(1, 1, 0)
            with eng.Fori(1, WINDOWS // 2) as i:
                body(i * 2, 0, i)
                body(i * 2 + 1, 1, i)
            body(WINDOWS - 1, 0, WINDOWS // 2)

        def later(n, at):
            return not isinstance(n, int) or n >= at

        def loop_visits(eng, head, body, tail, visits=V):
            head()
            for n in range(UNROLL):
                body(n, n)
            with eng.Fori(1, visits // UNROLL) as i:
                for k in range(UNROLL):
                    body(i * UNROLL + k, k)
            tail()

        def loop_batches(eng, body):
            body(0, 0)
            body(1, 1)
            with eng.Fori(1, T_PAD // UNROLL // 2) as i:
                body(i * 2, 0)
                body(i * 2 + 1, 1)

        N_TARGETS = (CW, P)
        N_EDGE_LOADS = 2 * (-(-(C_GROUPS - 1) // P) + 1) + 3 * (-(-(GROUPS - 1) // P) + 1)
        WALKS = [(C_WINDOWS, CV, C_GROUPS, CB, 2), (WINDOWS, V, GROUPS, B, 3)]

        def ordered(walk, k, b, half):
            if walk == 0:
                return (ps_sum, ps_tail, ps_t, ps_v)[2 * k + b][:, half, 0:CV // 2]
            return (ps_tail, ps_sum, ps_t)[k][:, b // 2, b % 2 * 256 + half * (V // 2):b % 2 * 256 + (half + 1) * (V // 2)]

        block = ctx.enter_context(nc.Block())

        @block.sync
        def _(sp):
            sp.wait_ge(sem("lists_cleared"), 3)
            for k, name in enumerate(["dst", "edge_type_8"]):
                whole = E // P
                sp.dma_start(free_order[:, k, 0:whole], a[name][0:whole * P].rearrange("(p t) -> p t", p=P)).then_inc(sem("free_loaded"), 16)
                sp.dma_start(free_order[0:E - whole * P, k, whole:whole + 1],
                             a[name][whole * P:E].rearrange("(p t) -> p t", t=1)).then_inc(sem("free_loaded"), 16)
            for lists, names, groups, size in ((c_raw, ("src", "dst"), C_GROUPS, CB * P), (raw, ("src", "dst", "edge_type_8"), GROUPS, GROUP)):
                for k, name in enumerate(names):
                    for g in range(0, groups - 1, P):
                        n = min(P, groups - 1 - g)
                        sp.dma_start(lists[0:n, g // P, k, :], a[name][g * size:(g + n) * size].rearrange("(g e) -> g e", e=size)
                                     ).then_inc(sem("edges_loaded"), 16)
                    g = (groups - 1) % P
                    sp.dma_start(lists[g:g + 1, (groups - 1) // P, k, 0:E - (groups - 1) * size],
                                 a[name][(groups - 1) * size:E].rearrange("(g e) -> g e", g=1)).then_inc(sem("edges_loaded"), 16)
            full = (N // P) * P
            sp.wait_ge(sem("x_cleared"), 1)
            sp.dma_start(x_cur[:, 0:N // P, :], a["x"][0:full, :].rearrange("(w p) c -> p w c", p=P)).then_inc(sem("x_loaded"), 16)
            sp.dma_start(x_cur[0:N - full, N // P, :], a["x"][full:N, :]).then_inc(sem("x_loaded"), 16)
            for name, row in BIAS.items():
                sp.dma_start(row, a[name].partition_broadcast(P)).then_inc(sem("weights_loaded"), 16)
            sp.dma_start(w_gcn[:, 0, :], a["L0_gnn_W1"]).then_inc(sem("weights_loaded"), 16)
            sp.dma_start(w_gcn[:, 1, :], a["L0_gnn_W2"]).then_inc(sem("weights_loaded"), 16)
            sp.dma_start(w_rel[:, :, :], a["L1_gnn_weight"].rearrange("r d o -> d r o")).then_inc(sem("weights_loaded"), 16)
            sp.dma_start(w_self[:, :], a["L1_gnn_self_weight"]).then_inc(sem("weights_loaded"), 16)
            sp.dma_start(tile_in[:, 0, 0:D], a["L2_gnn_W_self"]).then_inc(sem("weights_loaded"), 16)
            sp.dma_start(tile_in[:, 0, D:2 * D], a["L2_gnn_W_neigh"]).then_inc(sem("weights_loaded"), 16)
            sp.dma_start(tile_in[:, 0, 2 * D:4 * D], a["L2_gnn_W_gate"]).then_inc(sem("weights_loaded"), 16)
            sp.dma_start(w_h1[:, 0, 0:HC], a["L3_gnn_W1"]).then_inc(sem("weights_loaded"), 16)
            sp.dma_start(w_h2[:, :, 0:HC], a["L3_gnn_W2"].rearrange("(k p) c -> p k c", p=P)).then_inc(sem("weights_loaded"), 16)
            for k, side in enumerate(("src", "dst")):
                for layer, name in enumerate(("h1", "h2", "h3"), 1):
                    sp.dma_start(att_rows[name][:, k, :], a[f"L3_gnn_a_{side}{layer}"].rearrange("h c -> (h c)").partition_broadcast(P)).then_inc(sem("weights_loaded"), 16)
            for k in range(2):
                sp.dma_start(bias_wide[:, k, :], a[f"L3_gnn_b{k + 1}"].partition_broadcast(P)).then_inc(sem("weights_loaded"), 16)
            sp.dma_start(w_h3[:, :, 0:D], a["L3_gnn_W3"].rearrange("(k p) c -> p k c", p=P)).then_inc(sem("weights_loaded"), 16)

            sp.wait_ge(sem("degree_rows_made"), 1)
            sp.dma_start(degree_rows[0:N * R].rearrange("(p c) -> p c", p=DEG_HI), rel_degree[0:DEG_HI, :]).then_inc(sem("degree_rows_stored"), 16)
            sp.dma_start(degree_rows[N * R:NP * R].rearrange("(a c) -> a c", a=1), zero_row[0:1, 0:(NP - N) * R]).then_inc(sem("degree_rows_stored"), 16)
            sp.wait_ge(sem("degree_rows_stored"), 32)
            sp.dma_start(rel_norm[:, :, :], degree_rows.rearrange("(w p r) -> p w r", p=P, r=R)).then_inc(sem("degrees_loaded"), 16)

            sp.wait_ge(sem("c_walk_ready"), 1)
            for w in range(RING - STORE_LAG, RING):
                sp.sem_inc(sem(f"c_stored{w}"), 16)
            with sp.Fori(0, WINDOWS) as j:
                for w in range(CW_BLOCK):
                    end = sp.value_load(c_end[0:1, bass.ds(j * CW_BLOCK + w, 1)], min_val=1, max_val=CV)
                    sp.wait_ge(sem("c_added"), end)
                    sp.dma_start(c_matrix[bass.ds(j, 1), :, w, :].rearrange("j p c -> p (j c)"), ring[:, w, :]).then_inc(sem(f"c_stored{w}"), 16)
                    sp.wait_ge(sem(f"c_stored{(w - STORE_LAG) % RING}"), j * 16 + 16)
                    sp.sem_inc(sem("c_windows_free"), 1)
            for w in range(RING - STORE_LAG, RING):
                sp.wait_ge(sem(f"c_stored{w}"), WINDOWS * 16 + 16)
                sp.sem_inc(sem("c_windows_free"), 1)

            att = 0
            for phase, (kind, what) in enumerate(PHASES):
                if kind == "blocks":
                    if what == "att1":
                        sp.wait_ge(sem("factors_made"), 3)
                        sp.dma_start(target_rows.rearrange("k (w p) -> (k w) p", p=P), tile_in[0:2 * W, 1, 0:P]).then_inc(sem("target_rows_stored"), 16)
                        sp.wait_ge(sem("target_rows_stored"), 16)
                    sp.wait_ge(sem("blocks_begun"), 1 + sum(PHASES[k][0] == "blocks" for k in range(phase)))
                    summed = before(phase, "block_summed")

                    def load_block(j, s, turn):
                        if later(j, 2):
                            sp.wait_ge(sem("block_summed"), summed + j - 1)
                        sp.dma_start(flat[:, s * CW_BLOCK * C_COLS:(s + 1) * CW_BLOCK * C_COLS],
                                     c_matrix[bass.ds(j, 1), :, :, :].rearrange("j p w c -> p (j w c)")).then_inc(sem(f"block_loaded{s}"), 16)
                        if what == "att1":
                            for k in range(2):
                                sp.dma_start(tile_t[:, s, k * P:(k + 1) * P], target_rows[k, bass.ds(j * P, P)].partition_broadcast(P)
                                             ).then_inc(sem(f"target_loaded{s}"), 16)

                    loop_blocks(sp, load_block)
                if kind == "dense" and DENSE[what][2]:
                    cols = DENSE[what][2]
                    table = {"rel": rel_table, "h1": att_table[0], "h2": att_table[1]}[what]
                    copied, stored = before(phase, "product_copied"), before(phase, "row_stored")

                    with sp.Fori(0, W // 2) as i:
                        for s in range(2):
                            sp.wait_ge(sem("product_copied"), copied + i * 2 + s + 1)
                            sp.dma_start(table[bass.ds((i * 2 + s) * P, P), 0:cols], tile_out[:, s, 0:cols]).then_inc(sem(f"row_stored{s}"), 16)
                    for s in range(2):
                        sp.wait_ge(sem(f"row_stored{s}"), stored + W // 2 * 16)
                    sp.sem_inc(sem("rows_stored"), 1)
                if what == "att8":
                    att += 1
                    table = att_table[att - 1]
                    sp.dma_start(loop_rows[:, :, 0:HC], table[0:LOOP_W * P, 0:HC].rearrange("(w p) c -> p w c", p=P)).then_inc(sem("loop_rows_loaded"), 16)
                    sp.wait_ge(sem("factors_made"), att)
                    sp.dma_start(table[:, HC:ROW].rearrange("(w p) c -> p w c", p=P), uf[:, :, :]).then_inc(sem("factors_stored"), 16)
            sp.wait_ge(sem("result_made"), 1)
            sp.dma_start(out[0:full, :].rearrange("(w p) c -> p w c", p=P), x_cur[:, 0:N // P, :]).then_inc(sem("result_stored"), 16)
            sp.dma_start(out[full:N, :], x_cur[0:N - full, N // P, :]).then_inc(sem("result_stored"), 16)
            sp.wait_ge(sem("result_stored"), 32)

        @block.gpsimd
        def _(pool):
            pool.memset(free_order, -30000).then_inc(sem("lists_cleared"), 1)
            pool.memset(c_raw[:, CCH - 1, :, :], -1).then_inc(sem("lists_cleared"), 1)
            pool.memset(raw[:, CH - 1, :, :], -1).then_inc(sem("lists_cleared"), 1)
            pool.memset(x_cur[:, N // P:W, :], 0.0).then_inc(sem("x_cleared"), 1)
            pool.memset(ident[:, :], 0.0).then_inc(sem("ident_zero"), 1)
            pool.wait_ge(sem("ident_zero"), 1)
            pool.affine_select(out=ident[:, :], in_=ident[:, :], compare_op=ALU.not_equal, fill=1.0, base=0,
                               pattern=[[-1, P]], channel_multiplier=1).then_inc(sem("constants"), 1)
            pool.iota(iota_col[:, :], pattern=[[1, P]], base=0, channel_multiplier=0,
                      allow_small_or_imprecise_dtypes=True).then_inc(sem("constants"), 1)
            pool.iota(iota_part[:, :], pattern=[[0, 1]], base=0, channel_multiplier=1,
                      allow_small_or_imprecise_dtypes=True).then_inc(sem("constants"), 1)
            pool.iota(iota_rel[:, :, :], pattern=[[0, B], [1, R]], base=0, channel_multiplier=0,
                      allow_small_or_imprecise_dtypes=True).then_inc(sem("constants"), 1)
            for tile, pattern, base, across in (
                    (iota_visit[:, :], [[1, CV]], 0, 0), (iota_row[:, :], [[1, C_WINDOWS]], 0, 0), (iota_node[:, :], [[1, DEG_LO]], 0, DEG_LO),
                    (iota_deg[:, :], [[1, DEG_LO * R]], 0, 0), (iota_c[:, :], [[1, C_COLS]], 0, 0), (iota_16[:, :], [[1, P]], 0, 0)):
                pool.iota(tile, pattern=pattern, base=base, channel_multiplier=across,
                          allow_small_or_imprecise_dtypes=True).then_inc(sem("constants"), 1)
            pool.memset(zero_row[:, :], 0.0).then_inc(sem("constants"), 1)
            pool.iota(loop_mask[:, :], pattern=[[P, LOOP_W]], base=0, channel_multiplier=1,
                      allow_small_or_imprecise_dtypes=True).then_inc(sem("constants"), 1)
            pool.memset(ones[:, :], 1.0).then_inc(sem("constants"), 1)

            passes = 0
            att = 0
            for phase, (kind, what) in enumerate(PHASES):
                if what in ("att8", "att1"):
                    att += 1
                    pool.wait_ge(sem("peak_ready"), att)
                    nh = HEADS if what == "att8" else 1
                    pool.partition_all_reduce(peak_all[:, 0:nh], peak[:, 0:nh], P, bass.bass_isa.ReduceOp.max).then_inc(sem("peak_reduced"), 1)
                if what == "att1":
                    pool.wait_ge(sem("blocks_begun"), sum(k == "blocks" for k, _ in PHASES))

                    def slope_one(j, s, turn):
                        pool.wait_ge(sem(f"target_loaded{s}"), turn * 32 + 32)
                        if later(j, 1):
                            pool.wait_ge(sem("slopes_joined"), j)
                        pool.tensor_tensor(slope1, uf[:, 0:WINDOWS, 0].unsqueeze(1).to_broadcast([P, P, WINDOWS]),
                                           target_now[:, s, 0, :].unsqueeze(2).to_broadcast([P, P, WINDOWS]), ALU.mult
                                           ).then_inc(sem("slope1_made"), 1)

                    loop_blocks(pool, slope_one)
                if kind != "pass":
                    continue
                passes += 1
                table, index, cols = gather_table(phase)
                if what == "norm":
                    pool.wait_ge(sem("rows_stored"), 1)
                else:
                    pool.wait_ge(sem("factors_stored"), 16 * att)
                pool.wait_ge(sem("pass_begun"), passes)
                staged = before(phase, "index_staged")
                summed, weighted = before(phase, "sum_ready"), before(phase, "weighted")

                def gather(n, k):
                    s = k % 2
                    if later(n, 2):
                        if what == "att8":
                            pool.wait_ge(sem("weighted"), weighted + n - 1)
                        else:
                            pool.wait_ge(sem("sum_ready"), summed + n - 1)
                        pool.sem_inc(sem("gather_turn"), 1)
                    pool.wait_ge(sem("index_staged"), staged + n + 1)
                    pool.sem_inc(sem("gather_turn"), 1)
                    for b in range(B):
                        pool.indirect_dma_start(rows_g[:, s, b, 0:cols], None, table,
                                                bass.IndirectOffsetOnAxis(ap=index_now[:, k, b:b + 1], axis=0)
                                                ).then_inc(sem(f"gathered{s * B + b}"), 16)

                loop_visits(pool, lambda: None, gather, lambda: None)

        def functions_before(what):
            if what not in ("att8", "att1"):
                return []
            nh, at = (HEADS if what == "att8" else 1), 0
            return [(uf[:, :, at:at + nh], ACT.Exp, 1.0), (uf[:, :, at + nh:at + 2 * nh], ACT.Exp, SLOPE),
                    (tv[:, :, 0:nh], ACT.Exp, 1 - SLOPE), (tv[:, :, nh:2 * nh], ACT.Exp, SLOPE - 1)]

        def functions_after(what):
            norm = [(stat[:, :], ACT.Sqrt, 1.0)]
            if what in ("gcn2", "norm", "att1"):
                return norm
            if what == "gate":
                return [(z, ACT.Sigmoid, 1.0)] + norm + norm
            if what == "att8":
                return [(setup_rows[:, 0:n * HC], ACT.Exp, 1.0) for n in elu_parts()]
            return []

        def elu_parts():
            most = 2 * B * ROW // HC
            return [min(most, W - w) for w in range(0, W, most)]

        @block.scalar
        def _(act):
            act.wait_ge(sem("weights_turned"), 1)
            act.activation(w_mix[:, :, :].rearrange("p k c -> p (k c)"), ps_t[:, 0, 0:2 * D], ACT.Copy).then_inc(sem("weights_ready"), 1)
            act.activation(w_gate[:, :, :].rearrange("p k c -> p (k c)"), ps_t[:, 0, 2 * D:4 * D], ACT.Copy).then_inc(sem("weights_ready"), 1)
            asked = 1
            act.wait_ge(sem("function_asked"), asked)
            act.activation(dis[:, :], dis[:, :], ACT.Sqrt).then_inc(sem("function_done"), 1)

            for phase, (kind, what) in enumerate(PHASES):
                for buffer, f, scale in functions_before(what):
                    asked += 1
                    act.wait_ge(sem("function_asked"), asked)
                    act.activation(buffer, buffer, f, scale=scale).then_inc(sem("function_done"), 1)
                if kind == "blocks":
                    summed = before(phase, "block_summed")
                    cols = D + 1 if what == "att1" else D

                    def copy_block(j, s, turn):
                        act.wait_ge(sem("block_summed"), summed + j + 1)
                        act.activation(acc[:, bass.ds(j, 1), 0:cols], ps_sum[:, s:s + 1, 0:cols], ACT.Copy).then_inc(sem("block_copied"), 1)

                    loop_blocks(act, copy_block)
                if kind == "pass":
                    turned, looked = before(phase, "transposed"), before(phase, "looked_up")

                    index = gather_table(phase)[1]
                    summed = before(phase, "sum_ready")

                    def stage_index(n, k):
                        if later(n, UNROLL):
                            act.wait_ge(sem("sum_ready"), summed + n - UNROLL + 1)
                        act.activation(index_now[:, k % UNROLL:k % UNROLL + 1, :], index[:, bass.ds(n, 1), :], ACT.Copy).then_inc(sem("index_staged"), 1)

                    def copy_onehot(m, k):
                        s = k % 2
                        act.wait_ge(sem("transposed"), turned + m + 1)
                        if later(m, 2):
                            act.wait_ge(sem("looked_up"), looked + m - 1)
                        act.activation(onehot_t[:, s, :, :].rearrange("p b c -> p (b c)"), ps_t[:, s, :],
                                       ACT.Copy).then_inc(sem("transposed_copied"), 1)

                    def start():
                        for n in range(AHEAD):
                            stage_index(n, n)
                        copy_onehot(0, 0)
                        copy_onehot(1, 1)

                    def visit(n, k):
                        copy_onehot(n + 2, k + 2)
                        stage_index(n + AHEAD, k + AHEAD)

                    loop_visits(act, start, visit, lambda: None)
                elif kind == "dense":
                    chunks, cols, to_table = DENSE[what]
                    turned, product, stored = (before(phase, x) for x in ("tile_transposed", "product_ready", "row_stored"))

                    def copy_tile(w, s):
                        act.wait_ge(sem("tile_transposed"), turned + w + 1)
                        if later(w, 2):
                            act.wait_ge(sem("product_ready"), product + w - 1)
                        act.activation(tile_t[:, s, 0:chunks * P], ps_t[:, s, 0:chunks * P], ACT.Copy).then_inc(sem("tile_copied"), 1)

                    def copy_product(w, s, turn):
                        act.wait_ge(sem("product_ready"), product + w + 1)
                        if what == "h3":
                            act.activation(h_one[:, bass.ds(w, 1), 0:D], ps_sum[:, s:s + 1, 0:D], ACT.Copy)
                            act.activation(ab[:, bass.ds(w, 1), 0:2], ps_sum[:, s:s + 1, D:D + 2], ACT.Copy).then_inc(sem("product_copied"), 1)
                            return
                        if not to_table:
                            act.activation(z[:, bass.ds(w, 1), :], ps_sum[:, s:s + 1, 0:D], ACT.Copy).then_inc(sem("product_copied"), 1)
                            return
                        if later(w, 2):
                            act.wait_ge(sem(f"row_stored{s}"), stored + turn * 16)
                        act.activation(tile_out[:, s, 0:min(to_table, 512)], ps_sum[:, s, 0:min(to_table, 512)], ACT.Copy)
                        if what == "rel":
                            last = act.activation(tile_out[:, s, 512:1024], ps_tail[:, s, :], ACT.Copy)
                        else:
                            last = act.activation(ab[:, bass.ds(w, 1), :], ps_tail[:, s:s + 1, 0:2 * HEADS], ACT.Copy)
                        last.then_inc(sem("product_copied"), 1)

                    def tile(w, s, turn, last):
                        if not last:
                            copy_tile(w + 1, 1 - s)
                        copy_product(w, s, turn)

                    loop_tiles(act, lambda: copy_tile(0, 0), tile)
                for buffer, f, scale in functions_after(what):
                    asked += 1
                    act.wait_ge(sem("function_asked"), asked)
                    act.activation(buffer, buffer, f, scale=scale).then_inc(sem("function_done"), 1)

        @block.tensor
        def _(pe):
            def degree_batch(j, s):
                pe.wait_ge(sem("degree_batch_ready"), j + 1)
                for k in range(UNROLL):
                    last = pe.matmul(ps_v[:, 0, 0:DEG_LO * R], hi_hot[:, s * UNROLL + k, :], deg_hot[:, s * UNROLL + k, :],
                                     start=(isinstance(j, int) and j == 0 and k == 0), stop=True, skip_group_check=True)
                last.then_inc(sem("degree_batch_added"), 1)

            loop_batches(pe, degree_batch)

            for n, (windows, visits, groups, tiles, values) in enumerate(WALKS):
                pe.wait_ge(sem("above_ready"), n + 1)
                pe.matmul(ps_v[:, 0, 0:windows - 1], ones[:, :], above[:, 0:windows - 1], start=True, stop=True)
                for c in range(-(-(windows - 1) // P)):
                    k = min(P, windows - 1 - c * P)
                    last = pe.matmul(ps_v[0:k, 1, c:c + 1], above[:, c * P:c * P + k], ones[:, 0:1], start=True, stop=True)
                last.then_inc(sem("above_summed"), 1)
                pe.wait_ge(sem("reached_ready"), n + 1)
                parts = -(-(windows - 1) // P)
                for half in range(2):
                    for c in range(parts):
                        k = min(P, windows - 1 - c * P)
                        last = pe.matmul(ps_t[:, half, 0:visits // 2], ones[0:k, :], reached[0:k, c, half * (visits // 2):(half + 1) * (visits // 2)],
                                         start=(c == 0), stop=(c == parts - 1))
                last.then_inc(sem("windows_summed"), 1)
                pe.wait_ge(sem("select_ready"), n + 1)
                pick, source = (c_select, c_list) if n == 0 else (select, p_list)
                chunks = -(-groups // P)
                for k in range(values):
                    for b in range(tiles):
                        for half in range(2):
                            for c in range(chunks):
                                last = pe.matmul(ordered(n, k, b, half), source[:, c, k, b * P:(b + 1) * P],
                                                 pick[:, c, half * (visits // 2):(half + 1) * (visits // 2)], start=(c == 0), stop=(c == chunks - 1))
                last.then_inc(sem("lists_ordered"), 1)
            pe.wait_ge(sem("weights_loaded"), 16 * N_WEIGHTS)
            pe.wait_ge(sem("lists_taken"), 2)
            for k in range(4):
                last = pe.transpose(ps_t[:, 0, k * P:(k + 1) * P], tile_in[:, 0, k * P:(k + 1) * P], ident[:, :])
            last.then_inc(sem("weights_turned"), 1)
            pe.wait_ge(sem("weights_ready"), 2 + 1)

            def count_pairs(n, k):
                window = pe.value_load(c_window[0:1, bass.ds(n, 1)], min_val=0, max_val=C_WINDOWS - 1)
                pe.wait_ge(sem("c_windows_free"), window + 1)
                pe.wait_ge(sem("c_key_ready"), n + 1)
                if later(n, 2):
                    pe.wait_ge(sem("c_added"), n - 1)
                for b in range(CB):
                    last = pe.matmul(ps_sum[:, k % 2, 0:C_COLS], lo_hot[:, k, b, :], key_hot[:, k, b, :], start=(b == 0), stop=(b == CB - 1))
                last.then_inc(sem("c_summed"), 1)

            loop_visits(pe, lambda: None, count_pairs, lambda: None, CV)

            for phase, (kind, what) in enumerate(PHASES):
                at = {x: before(phase, x) for x in ("onehot_ready", "transposed_copied", "weighted", "gathered", "sum_added",
                                                    "tile_staged", "tile_copied", "product_copied", "block_copied", "block_weighed",
                                                    "block_loaded0", "block_loaded1")}
                if kind == "blocks":
                    rows_of = {L0_SUM1: z, L0_SUM2: z, L2_SUM: x_cur}.get(phase, h_one)
                    cols = D + 1 if what == "att1" else D
                    if what == "att1":
                        pe.wait_ge(sem("targets_ready"), 1)
                        pe.transpose(ps_v[0:2 * W, 0, 0:P], tile_in[:, 0, 0:2 * W], ident[:, :]).then_inc(sem("targets_transposed"), 1)
                    pe.wait_ge(sem("blocks_begun"), 1 + sum(PHASES[k][0] == "blocks" for k in range(phase)))

                    def sum_block(j, s, turn):
                        pe.wait_ge(sem(f"block_loaded{s}"), at[f"block_loaded{s}"] + turn * 16 + 16)
                        if what == "att1":
                            pe.wait_ge(sem("block_weighed"), at["block_weighed"] + j + 1)
                        if later(j, 2):
                            pe.wait_ge(sem("block_copied"), at["block_copied"] + j - 1)
                        for h in range(WINDOWS):
                            counts = slope2[:, :, h] if what == "att1" else c_block[:, s, :, h]
                            last = pe.matmul(ps_sum[:, s, 0:cols], counts, rows_of[:, h, 0:cols], start=(h == 0), stop=(h == WINDOWS - 1))
                        last.then_inc(sem("block_summed"), 1)

                    loop_blocks(pe, sum_block)
                elif kind == "pass":
                    values, n_values = lookup_values(what)

                    def turn_onehot(m, k):
                        s, o = k % 2, k % UNROLL
                        pe.wait_ge(sem("onehot_ready"), at["onehot_ready"] + m + 1)
                        for b in range(B):
                            last = pe.transpose(ps_t[:, s, b * P:(b + 1) * P], onehot[:, o, b, :], ident[:, :])
                        last.then_inc(sem("transposed"), 1)

                    def look_up(m, k):
                        s = k % 2
                        window = pe.value_load(window_of[0:1, bass.ds(m, 1)], min_val=0, max_val=WINDOWS - 1)
                        if later(m, 2):
                            pe.wait_ge(sem("weighted"), at["weighted"] + m - 1)
                        pe.wait_ge(sem("transposed_copied"), at["transposed_copied"] + m + 1)
                        for b in range(B):
                            last = pe.matmul(ps_v[:, s, b * n_values:(b + 1) * n_values], onehot_t[:, s, b, :],
                                             values[:, bass.ds(window, 1), 0:n_values], start=True, stop=True)
                        last.then_inc(sem("looked_up"), 1)

                    def sum_rows(n, k):
                        s = k % 2
                        pe.wait_ge(sem("weighted"), at["weighted"] + n + 1)
                        if later(n, 2):
                            pe.wait_ge(sem("sum_added"), at["sum_added"] + n - 1)
                        for b in range(B):
                            if what == "norm":
                                pe.wait_ge(sem(f"gathered{s * B + b}"), at["gathered"] + (n - s) * 8 + 16)
                            flags = {"start": b == 0, "stop": b == B - 1}
                            hot = onehot[:, k, b, :]
                            if what == "att8":
                                pe.matmul(ps_sum[:, s, 0:HALF], hot, rows_w[:, s, b, 0:HALF], **flags)
                                last = pe.matmul(ps_tail[:, s, 0:HALF], hot, rows_w[:, s, b, HALF:2 * HALF], **flags)
                            else:
                                last = pe.matmul(ps_sum[:, s, 0:D], hot, rows_g[:, s, b, 0:D], **flags)
                        last.then_inc(sem("sum_ready"), 1)

                    def visit(n, k):
                        look_up(n + 1, k + 1)
                        turn_onehot(n + 2, k + 2)
                        sum_rows(n, k)

                    def start():
                        turn_onehot(0, 0)
                        look_up(0, 0)
                        turn_onehot(1, 1)

                    loop_visits(pe, start, visit, lambda: None)
                else:
                    chunks, cols, to_table = DENSE[what]
                    weights = {"gcn1": w_gcn[:, 0:1, :], "gcn2": w_gcn[:, 1:2, :], "rel": w_rel[:, :, :].rearrange("p r c -> p (r c)").unsqueeze(1),
                               "self": w_self[:, :].unsqueeze(1), "mix": w_mix, "gate": w_gate, "h1": w_h1, "h2": w_h2, "h3": w_h3}[what]

                    def turn_tile(w, s):
                        pe.wait_ge(sem("tile_staged"), at["tile_staged"] + w + 1)
                        if later(w, 2):
                            pe.wait_ge(sem("tile_copied"), at["tile_copied"] + w - 1)
                        for c in range(chunks):
                            last = pe.transpose(ps_t[:, s, c * P:(c + 1) * P], tile_in[:, s, c * P:(c + 1) * P], ident[:, :])
                        last.then_inc(sem("tile_transposed"), 1)

                    def product(w, s):
                        pe.wait_ge(sem("tile_copied"), at["tile_copied"] + w + 1)
                        if later(w, 2):
                            pe.wait_ge(sem("product_copied"), at["product_copied"] + w - 1)
                        for c in range(chunks):
                            for lo, bank in ((0, ps_sum), (512, ps_tail)):
                                n = min(512, cols - lo)
                                if n > 0:
                                    last = pe.matmul(bank[:, s, 0:n], tile_t[:, s, c * P:(c + 1) * P], weights[:, c, lo:lo + n],
                                                     start=(c == 0), stop=(c == chunks - 1))
                        last.then_inc(sem("product_ready"), 1)

                    def tile(w, s, turn, last):
                        if not last:
                            turn_tile(w + 1, 1 - s)
                        product(w, s)

                    loop_tiles(pe, lambda: turn_tile(0, 0), tile)

        @block.vector
        def _(dve):
            steps = 0

            def step(ins):
                nonlocal steps
                steps += 1
                ins.then_inc(sem("dve_step"), 1)
                dve.wait_ge(sem("dve_step"), steps)

            asked = 0

            def ask():
                nonlocal asked
                asked += 1
                dve.sem_inc(sem("function_asked"), 1)
                dve.wait_ge(sem("function_done"), asked)

            def tt(out_, x, y, op):
                step(dve.tensor_tensor(out_, x, y, op))

            def layer_norm(x, scratch):
                step(dve.tensor_reduce(stat[:, :], x, AX, ALU.add))
                step(dve.tensor_scalar(stat[:, :], stat[:, :], 1.0 / D, None, ALU.mult))
                tt(x, x, over_features(stat[:, :]), ALU.subtract)
                tt(scratch, x, x, ALU.mult)
                step(dve.tensor_reduce(stat[:, :], scratch, AX, ALU.add))
                step(dve.tensor_scalar(stat[:, :], stat[:, :], 1.0 / D, LN_EPS, ALU.mult, ALU.add))
                ask()
                step(dve.reciprocal(stat[:, :], stat[:, :]))
                tt(x, x, over_features(stat[:, :]), ALU.mult)

            dve.wait_ge(sem("constants"), N_CONST)
            dve.wait_ge(sem("free_loaded"), 64)
            step(dve.tensor_copy(deg_hi, free_order[:, 0, :]))
            step(dve.tensor_scalar(deg_lo, deg_hi, 1.0 / DEG_LO, 0.5 / DEG_LO - 0.5, ALU.mult, ALU.add))
            step(dve.tensor_copy(deg_int, deg_lo))
            step(dve.tensor_copy(deg_lo, deg_int))
            step(dve.scalar_tensor_tensor(out=deg_hi, in0=deg_lo, scalar=-float(DEG_LO), in1=deg_hi, op0=ALU.mult, op1=ALU.add))
            step(dve.tensor_scalar(deg_hi, deg_hi, float(R), None, ALU.mult))
            step(dve.tensor_copy(deg_tmp, free_order[:, 1, :]))
            tt(deg_tmp, deg_tmp, deg_hi, ALU.add)
            step(dve.tensor_copy(deg_hi, deg_lo))
            step(dve.tensor_copy(deg_lo, deg_tmp))
            dve.sem_inc(sem("degree_keys_ready"), 1)

            def degree_onehots(j, s):
                if later(j, 2):
                    dve.wait_ge(sem("degree_batch_added"), j - 1)
                for k in range(UNROLL):
                    tile, slot = bass.ds(j * UNROLL + k, 1), s * UNROLL + k
                    dve.tensor_scalar(hi_hot[:, slot, :], iota_16[:, :], deg_hi[:, tile], None, ALU.is_equal)
                    last = dve.tensor_scalar(deg_hot[:, slot, :], iota_deg[:, :], deg_lo[:, tile], None, ALU.is_equal)
                last.then_inc(sem("degree_batch_ready"), 1)

            loop_batches(dve, degree_onehots)
            dve.wait_ge(sem("degree_batch_added"), T_PAD // UNROLL)
            step(dve.tensor_copy(rel_degree[:, :], ps_v[:, 0, 0:DEG_LO * R]))
            dve.sem_inc(sem("degree_rows_made"), 1)
            step(dve.tensor_reduce(node_degree[:, :], rel_degree[:, :].rearrange("p (d r) -> p d r", r=R), AX, ALU.add))

            dve.wait_ge(sem("edges_loaded"), 16 * N_EDGE_LOADS)
            for n, (windows, visits, groups, tiles, values) in enumerate(WALKS):
                size = N_TARGETS[n]
                for k in range(0, windows - 1, TH):
                    m = min(TH, windows - 1 - k)
                    step(dve.tensor_scalar(step_row[:, 0:m], iota_row[:, k:k + m], 1.0, float(size), ALU.add, ALU.mult))
                    tt(below[:, 0:m, :], iota_node[:, :].unsqueeze(1).to_broadcast([P, m, DEG_LO]),
                       step_row[:, 0:m].unsqueeze(2).to_broadcast([P, m, DEG_LO]), ALU.is_ge)
                    tt(below[:, 0:m, :], below[:, 0:m, :], node_degree[:, :].unsqueeze(1).to_broadcast([P, m, DEG_LO]), ALU.mult)
                    step(dve.tensor_reduce(above[:, k:k + m], below[:, 0:m, :], AX, ALU.add))
                dve.sem_inc(sem("above_ready"), 1)
                int_list, float_list = ((c_raw, c_list), (raw, p_list))[n]
                for k in range(values):
                    step(dve.tensor_scalar(float_list[:, :, k, :], int_list[:, :, k, :], 1.0 if k == 1 else 0.0, None, ALU.add if k == 1 else ALU.max))
                dve.wait_ge(sem("above_summed"), n + 1)
                shift = (tiles * P).bit_length() - 1
                parts = -(-(windows - 1) // P)
                step(dve.tensor_scalar(step_int[:, 0:windows - 1], ps_v[:, 0, 0:windows - 1], -1.0, float(E), ALU.mult, ALU.add))
                step(dve.tensor_scalar(step_int[:, 0:windows - 1], step_int[:, 0:windows - 1], shift, None, ALU.arith_shift_right))
                step(dve.tensor_copy(step_row[:, 0:windows - 1], step_int[:, 0:windows - 1]))
                step(dve.scalar_tensor_tensor(out=step_row[:, 0:windows - 1], in0=step_row[:, 0:windows - 1], scalar=1.0,
                                              in1=iota_row[:, 0:windows - 1], op0=ALU.add, op1=ALU.add))
                if n == 0:
                    step(dve.memset(c_end[:, :], CV))
                    step(dve.tensor_copy(c_end[:, 0:windows - 1], step_row[:, 0:windows - 1]))
                for c in range(parts):
                    k = min(P, windows - 1 - c * P)
                    step(dve.tensor_scalar(step_int[0:k, c:c + 1], ps_v[0:k, 1, c:c + 1], -1.0, float(E), ALU.mult, ALU.add))
                    step(dve.tensor_scalar(step_int[0:k, c:c + 1], step_int[0:k, c:c + 1], shift, None, ALU.arith_shift_right))
                    step(dve.tensor_copy(step_col[0:k, c:c + 1], step_int[0:k, c:c + 1]))
                    step(dve.scalar_tensor_tensor(out=step_col[0:k, c:c + 1], in0=step_col[0:k, c:c + 1], scalar=float(c * P + 1),
                                                  in1=iota_part[0:k, :], op0=ALU.add, op1=ALU.add))
                    step(dve.tensor_scalar(reached[0:k, c, 0:visits], iota_visit[0:k, 0:visits], step_col[0:k, c:c + 1], None, ALU.is_ge))
                dve.sem_inc(sem("reached_ready"), 1)
                dve.wait_ge(sem("windows_summed"), n + 1)
                half = visits // 2
                step(dve.tensor_copy(window_f[:, 0:half], ps_t[:, 0, 0:half]))
                step(dve.tensor_copy(window_f[:, half:visits], ps_t[:, 1, 0:half]))
                tt(group_f[:, 0:visits], iota_visit[:, 0:visits], window_f[:, 0:visits], ALU.subtract)
                pick = (c_select, select)[n]
                for c in range(-(-groups // P)):
                    step(dve.tensor_scalar(pick[:, c, :], group_f[:, 0:visits], float(-c * P), iota_part[:, 0:1], ALU.add, ALU.is_equal))
                dve.sem_inc(sem("select_ready"), 1)
                if n == 0:
                    step(dve.tensor_copy(c_window[:, :], window_f[:, :]))
                    step(dve.tensor_scalar(c_slot[:, :], c_window[:, :], RING - 1, None, ALU.bitwise_and))
                    step(dve.memset(c_keep[:, 0:1], 0.0))
                    tt(c_keep[:, 1:CV], window_f[:, 1:CV], window_f[:, 0:CV - 1], ALU.is_equal)
                else:
                    step(dve.memset(window_of[:, :], 0))
                    step(dve.tensor_copy(window_of[:, 0:V], window_f[:, 0:V]))
                step(dve.tensor_scalar(window_f[:, 0:visits], window_f[:, 0:visits], float(-size), -1.0, ALU.mult, ALU.add))
                dve.wait_ge(sem("lists_ordered"), n + 1)
                for b in range(tiles):
                    for half in range(2):
                        v = slice(half * (visits // 2), (half + 1) * (visits // 2))
                        if n == 0:
                            source, rest = c_int[:, 0, 0:visits // 2], c_int[:, 1, 0:visits // 2]
                            target, inside = group_f[:, 0:visits // 2], group_f[:, visits // 2:visits]
                            step(dve.tensor_copy(source, ordered(n, 0, b, half)))
                            step(dve.tensor_scalar(rest, source, P - 1, None, ALU.bitwise_and))
                            step(dve.tensor_copy(c_lo[:, v, b], rest))
                            step(dve.tensor_scalar(rest, source, P.bit_length() - 1, None, ALU.arith_shift_right))
                            tt(target, ordered(n, 1, b, half), window_f[:, v], ALU.add)
                            step(dve.scalar_tensor_tensor(out=c_key[:, v, b], in0=target, scalar=float(WINDOWS), in1=rest, op0=ALU.mult, op1=ALU.add))
                            step(dve.tensor_scalar(inside, target, 0.0, None, ALU.is_ge))
                            step(dve.scalar_tensor_tensor(out=inside, in0=target, scalar=float(CW), in1=inside, op0=ALU.is_lt, op1=ALU.mult))
                            step(dve.scalar_tensor_tensor(out=c_key[:, v, b], in0=c_key[:, v, b], scalar=1.0, in1=inside, op0=ALU.add, op1=ALU.mult))
                        else:
                            step(dve.tensor_tensor(edge_dst[:, v, b], ordered(n, 1, b, half), window_f[:, v], ALU.add))
                            step(dve.tensor_copy(edge_row[:, v, b], ordered(n, 0, b, half)))
                            step(dve.tensor_copy(edge_type[:, v, b], ordered(n, 2, b, half)))
                            step(dve.scalar_tensor_tensor(out=edge_rel_row[:, v, b], in0=ordered(n, 0, b, half), scalar=float(R),
                                                          in1=edge_type[:, v, b], op0=ALU.mult, op1=ALU.add))
                if n == 0:
                    step(dve.memset(c_key[:, CV:CV + 1, :], 0.0))
                    step(dve.memset(c_lo[:, CV:CV + 1, :], 0.0))
                    step(dve.tensor_scalar(c_key[:, :, :], c_key[:, :, :], -1.0, None, ALU.add))
                else:
                    step(dve.memset(edge_dst[:, V:V + 2, :], -1.0))
                    step(dve.memset(edge_row[:, V:V + AHEAD, :], 0))
                    step(dve.memset(edge_rel_row[:, V:V + AHEAD, :], 0))
                dve.sem_inc(sem("lists_taken"), 1)
            step(dve.tensor_scalar(loop_mask[:, :], loop_mask[:, :], float(N_LOOP), None, ALU.is_lt))

            dve.wait_ge(sem("weights_loaded"), 16 * N_WEIGHTS)
            for name, weight, heads, c_head in (("h1", w_h1, HEADS, HID), ("h2", w_h2, HEADS, HID), ("h3", w_h3, 1, D)):
                cols = heads * c_head
                for c in range(DENSE[name][0]):
                    for side in range(2):
                        tt(setup_product[:, 0:cols], weight[:, c, 0:cols], att_rows[name][:, side, :], ALU.mult)
                        step(dve.tensor_reduce(weight[:, c, cols + side * heads:cols + (side + 1) * heads],
                                               setup_product[:, 0:cols].rearrange("p (h c) -> p h c", h=heads), AX, ALU.add))
            dve.sem_inc(sem("weights_ready"), 1)

            step(dve.memset(ring, 0.0))
            dve.sem_inc(sem("c_windows_free"), RING - STORE_LAG)
            dve.sem_inc(sem("c_walk_ready"), 1)

            def source_column(n, k):
                for b in range(CB):
                    dve.tensor_scalar(lo_hot[:, k % UNROLL, b, :], iota_16[:, :],
                                      c_lo[:, bass.ds(n, 1), b:b + 1].rearrange("p v b -> p (v b)"), None, ALU.is_equal)
                    last = dve.tensor_scalar(key_hot[:, k % UNROLL, b, :], iota_c[:, :],
                                             c_key[:, bass.ds(n, 1), b:b + 1].rearrange("p v b -> p (v b)"), None, ALU.is_equal)
                last.then_inc(sem("c_key_ready"), 1)

            def add_window(n, k):
                slot = dve.value_load(c_slot[0:1, bass.ds(n, 1)], min_val=0, max_val=RING - 1)
                dve.wait_ge(sem("c_summed"), n + 1)
                if later(n, 1):
                    dve.wait_ge(sem("c_added"), n)
                dve.scalar_tensor_tensor(out=ring[:, bass.ds(slot, 1), :].rearrange("p k c -> p (k c)"),
                                         in0=ring[:, bass.ds(slot, 1), :].rearrange("p k c -> p (k c)"),
                                         scalar=c_keep[:, bass.ds(n, 1)], in1=ps_sum[:, k % 2, 0:C_COLS],
                                         op0=ALU.mult, op1=ALU.add).then_inc(sem("c_added"), 1)

            def count_visit(n, k):
                source_column(n + 1, k + 1)
                if later(n, 1):
                    add_window(n - 1, k + 1)

            loop_visits(dve, lambda: source_column(0, 0), count_visit, lambda: add_window(CV - 1, 1), CV)
            dve.wait_ge(sem("c_windows_free"), RING + C_WINDOWS)

            dve.wait_ge(sem("x_loaded"), 32)
            dve.wait_ge(sem("degrees_loaded"), 16)
            step(dve.tensor_reduce(count[:, :], rel_norm[:, :, :], AX, ALU.add))
            step(dve.tensor_scalar(dis[:, :], count[:, :], 1.0, None, ALU.add))
            ask()
            step(dve.reciprocal(dis[:, :], dis[:, :]))
            step(dve.tensor_scalar(rel_norm[:, :, :], rel_norm[:, :, :], 1.0, None, ALU.max))
            step(dve.reciprocal(rel_norm[:, :, :], rel_norm[:, :, :]))
            tt(z, x_cur[:, :, :], over_features(dis[:, :]), ALU.mult)

            att = 0
            for phase, (kind, what) in enumerate(PHASES):
                at = {x: before(phase, x) for x in ("sum_ready", "sum_added", "looked_up", "gathered", "factor_made", "coef_made",
                                                    "block_summed", "block_copied", "block_loaded0", "block_loaded1", "tile_transposed", "tile_staged", "product_copied", "onehot_ready", "transposed_copied")}
                nh = HEADS if what == "att8" else 1
                if what in ("plain", "norm", "att1"):
                    step(dve.memset(acc, 0.0))
                if what in ("att8", "att1"):
                    att += 1
                    step(dve.tensor_reduce(peak[:, 0:nh], ab[:, :, 0:nh].rearrange("p w h -> p h w"), AX, ALU.max))
                    dve.sem_inc(sem("peak_ready"), 1)
                    dve.wait_ge(sem("peak_reduced"), att)
                    top = peak_all[:, 0:nh].unsqueeze(1).to_broadcast([P, W, nh])
                    tt(uf[:, :, 0:nh], ab[:, :, 0:nh], top, ALU.subtract)
                    tt(uf[:, :, nh:2 * nh], ab[:, :, 0:nh], top, ALU.subtract)
                    tt(ab[:, :, nh:2 * nh], ab[:, :, nh:2 * nh], top, ALU.add)
                    step(dve.tensor_scalar(tv[:, :, 0:nh], ab[:, :, nh:2 * nh], 0.0, None, ALU.min))
                    step(dve.tensor_scalar(tv[:, :, nh:2 * nh], ab[:, :, nh:2 * nh], 0.0, None, ALU.max))
                    for _ in functions_before(what):
                        ask()
                    if what == "att1":
                        step(dve.tensor_copy(tile_in[:, 0, 0:2 * W].rearrange("p (k w) -> p w k", k=2), tv[:, :, 0:2]))
                        dve.sem_inc(sem("targets_ready"), 1)
                        dve.wait_ge(sem("targets_transposed"), 1)
                        step(dve.tensor_copy(tile_in[0:2 * W, 1, 0:P], ps_v[0:2 * W, 0, 0:P]))
                    dve.sem_inc(sem("factors_made"), 1)
                    tt(ab[:, 0:LOOP_W, 0:2 * nh], uf[:, 0:LOOP_W, 0:2 * nh], tv[:, 0:LOOP_W, 0:2 * nh], ALU.mult)
                    tt(ab[:, 0:LOOP_W, 0:nh], ab[:, 0:LOOP_W, 0:nh], ab[:, 0:LOOP_W, nh:2 * nh], ALU.max)
                    tt(ab[:, 0:LOOP_W, 0:nh], ab[:, 0:LOOP_W, 0:nh], loop_mask[:, :].unsqueeze(2).to_broadcast([P, LOOP_W, nh]), ALU.mult)
                if what == "att8":
                    step(dve.memset(wide[:, :, :], 0.0))
                    dve.wait_ge(sem("loop_rows_loaded"), 16 * att)
                    for w in range(LOOP_W):
                        dve.tensor_tensor(wide[:, w, 0:HC].rearrange("p (h c) -> p h c", h=nh),
                                          loop_rows[:, w, 0:HC].rearrange("p (h c) -> p h c", h=nh),
                                          over_features(ab[:, w, 0:nh], HID), ALU.mult)
                    step(dve.tensor_copy(wide[:, 0:LOOP_W, HC:HC + nh], ab[:, 0:LOOP_W, 0:nh]))
                if what == "att1":
                    step(dve.memset(h_one[:, :, D:D + 1], 1.0))

                if kind == "blocks":
                    dve.sem_inc(sem("blocks_begun"), 1)
                    if what == "att1":
                        def weigh_block(j, s, turn):
                            shape = [P, P, WINDOWS]
                            dve.wait_ge(sem(f"target_loaded{s}"), turn * 32 + 32)
                            if later(j, 1):
                                dve.wait_ge(sem("block_summed"), at["block_summed"] + j)
                            dve.tensor_tensor(slope2, uf[:, 0:WINDOWS, 1].unsqueeze(1).to_broadcast(shape),
                                              target_now[:, s, 1, :].unsqueeze(2).to_broadcast(shape), ALU.mult).then_inc(sem("slope2_made"), 1)
                            dve.wait_ge(sem("slope2_made"), j + 1)
                            dve.wait_ge(sem("slope1_made"), j + 1)
                            dve.tensor_tensor(slope2, slope2, slope1, ALU.max).then_inc(sem("slopes_joined"), 1)
                            dve.wait_ge(sem("slopes_joined"), j + 1)
                            dve.wait_ge(sem(f"block_loaded{s}"), at[f"block_loaded{s}"] + turn * 16 + 16)
                            dve.tensor_tensor(slope2, slope2, c_block[:, s, :, :], ALU.mult).then_inc(sem("block_weighed"), 1)

                        loop_blocks(dve, weigh_block)
                    dve.wait_ge(sem("block_copied"), at["block_copied"] + WINDOWS)
                elif kind == "pass":
                    dve.sem_inc(sem("pass_begun"), 1)

                    def make_onehot(m, k):
                        if later(m, UNROLL):
                            dve.wait_ge(sem("sum_ready"), at["sum_ready"] + m - UNROLL + 1)
                        for b in range(B):
                            last = dve.tensor_scalar(onehot[:, k % UNROLL, b, :], iota_col[:, :],
                                                     edge_dst[:, bass.ds(m, 1), b:b + 1].rearrange("p v b -> p (v b)"), None, ALU.is_equal)
                        last.then_inc(sem("onehot_ready"), 1)

                    def relations(n, s):
                        return dve.tensor_tensor(rel_hot[:, s, :, :], iota_rel[:, :, :],
                                                 edge_type[:, bass.ds(n, 1), :].rearrange("p v b -> p (v b)").unsqueeze(2).to_broadcast([P, B, R]),
                                                 ALU.is_equal)

                    def weigh(n, k):
                        s = k % 2
                        looked = ps_v[:, s, :]
                        if what == "norm":
                            relations(n, s).then_inc(sem("factor_made"), 1)
                            dve.wait_ge(sem("factor_made"), at["factor_made"] + n + 1)
                            dve.wait_ge(sem("looked_up"), at["looked_up"] + n + 1)
                            dve.tensor_tensor(factor[:, :, 0:R], rel_hot[:, s, :, :], looked[:, 0:B * R].rearrange("p (b r) -> p b r", b=B),
                                              ALU.mult).then_inc(sem("coef_made"), 1)
                            dve.wait_ge(sem("coef_made"), at["coef_made"] + 2 * n + 1)
                            dve.tensor_reduce(coef[:, :], factor[:, :, 0:R], AX, ALU.add).then_inc(sem("coef_made"), 1)
                            dve.wait_ge(sem("coef_made"), at["coef_made"] + 2 * n + 2)
                        else:
                            for b in range(B):
                                dve.wait_ge(sem(f"gathered{s * B + b}"), at["gathered"] + (n - s) * 8 + 16)
                            dve.wait_ge(sem("looked_up"), at["looked_up"] + n + 1)
                            first = HC
                            dve.tensor_tensor(factor[:, :, 0:2 * nh], rows_g[:, s, :, first:first + 2 * nh],
                                              looked[:, 0:B * 2 * nh].rearrange("p (b r) -> p b r", b=B), ALU.mult).then_inc(sem("factor_made"), 1)
                            dve.wait_ge(sem("factor_made"), at["factor_made"] + n + 1)
                            if what == "att8" and later(n, 2):
                                dve.wait_ge(sem("sum_ready"), at["sum_ready"] + n - 1)
                            into = rows_w[:, s, :, HC:HC + nh]
                            dve.tensor_tensor(into, factor[:, :, 0:nh], factor[:, :, nh:2 * nh], ALU.max).then_inc(sem("coef_made"), 1)
                            dve.wait_ge(sem("coef_made"), at["coef_made"] + n + 1)
                        if what == "att8":
                            for b in range(B):
                                last = dve.tensor_tensor(rows_w[:, s, b, 0:HC].rearrange("p (h c) -> p h c", h=HEADS),
                                                         rows_g[:, s, b, 0:HC].rearrange("p (h c) -> p h c", h=HEADS),
                                                         over_features(rows_w[:, s, b, HC:HC + HEADS], HID), ALU.mult)
                        else:
                            for b in range(B):
                                last = dve.tensor_scalar(onehot[:, k, b, :], onehot[:, k, b, :], coef[:, b:b + 1], None, ALU.mult)
                        last.then_inc(sem("weighted"), 1)

                    def add_sum(n, k):
                        s = k % 2
                        window = dve.value_load(window_of[0:1, bass.ds(n, 1)], min_val=0, max_val=WINDOWS - 1)
                        dve.wait_ge(sem("sum_ready"), at["sum_ready"] + n + 1)
                        if later(n, 1):
                            dve.wait_ge(sem("sum_added"), at["sum_added"] + n)
                        if what == "att8":
                            for half, bank in enumerate((ps_sum, ps_tail)):
                                into = wide[:, bass.ds(window, 1), half * HALF:(half + 1) * HALF]
                                last = dve.tensor_tensor(into, into, bank[:, s:s + 1, 0:HALF], ALU.add)
                        else:
                            cols = D
                            last = dve.tensor_tensor(acc[:, bass.ds(window, 1), 0:cols], acc[:, bass.ds(window, 1), 0:cols],
                                                     ps_sum[:, s:s + 1, 0:cols], ALU.add)
                        last.then_inc(sem("sum_added"), 1)

                    def visit(n, k):
                        make_onehot(n + 2, k + 2)
                        weigh(n, k)
                        if later(n, 1):
                            add_sum(n - 1, k + 1)

                    def start():
                        make_onehot(0, 0)
                        make_onehot(1, 1)

                    loop_visits(dve, start, visit, lambda: add_sum(V - 1, 1))
                    dve.wait_ge(sem("sum_added"), at["sum_added"] + V)
                    dve.wait_ge(sem("looked_up"), at["looked_up"] + V + 1)
                    dve.wait_ge(sem("transposed_copied"), at["transposed_copied"] + V + 2)
                else:
                    chunks, cols, to_table = DENSE[what]
                    source = {"rel": x_cur, "self": x_cur, "h1": x_cur, "gcn1": acc, "gcn2": acc, "mix": cat, "gate": cat,
                              "h2": wide, "h3": wide}[what]

                    def stage(w, s, turn, last):
                        if later(w, 2):
                            dve.wait_ge(sem("tile_transposed"), at["tile_transposed"] + w - 1)
                        dve.tensor_copy(tile_in[:, s:s + 1, 0:chunks * P], source[:, bass.ds(w, 1), 0:chunks * P]).then_inc(sem("tile_staged"), 1)

                    loop_tiles(dve, lambda: None, stage)
                    dve.wait_ge(sem("product_copied"), at["product_copied"] + W)

                if phase in (L0_SUM1, L0_SUM2):
                    tt(acc[:, :, 0:D], acc[:, :, 0:D], z, ALU.add)
                    tt(acc[:, :, 0:D], acc[:, :, 0:D], over_features(dis[:, :]), ALU.mult)
                elif what == "gcn1":
                    tt(z, z, over_windows(BIAS["L0_gnn_b1"]), ALU.add)
                    step(dve.tensor_scalar(z, z, 0.0, None, ALU.max))
                    tt(z, z, over_features(dis[:, :]), ALU.mult)
                elif what == "gcn2":
                    tt(x_cur[:, :, :], x_cur[:, :, :], z, ALU.add)
                    tt(x_cur[:, :, :], x_cur[:, :, :], over_windows(BIAS["L0_gnn_b2"]), ALU.add)
                    layer_norm(x_cur[:, :, :], spare)
                elif what == "norm":
                    tt(x_cur[:, :, :], x_cur[:, :, :], z, ALU.add)
                    tt(x_cur[:, :, :], x_cur[:, :, :], acc[:, :, 0:D], ALU.add)
                    tt(x_cur[:, :, :], x_cur[:, :, :], over_windows(BIAS["L1_gnn_bias"]), ALU.add)
                    layer_norm(x_cur[:, :, :], spare)
                elif phase == L2_SUM:
                    step(dve.tensor_scalar(has[:, :], count[:, :], 0.0, None, ALU.is_gt))
                    step(dve.tensor_scalar(count[:, :], count[:, :], 1.0, None, ALU.max))
                    step(dve.reciprocal(count[:, :], count[:, :]))
                    step(dve.tensor_copy(cat[:, :, 0:D], x_cur[:, :, :]))
                    tt(cat[:, :, D:2 * D], acc[:, :, 0:D], over_features(count[:, :]), ALU.mult)
                elif what == "mix":
                    tt(cat[:, :, D:2 * D], over_windows(BIAS["L2_gnn_b_neigh"]), over_features(has[:, :]), ALU.mult)
                    tt(cat[:, :, D:2 * D], cat[:, :, D:2 * D], z, ALU.add)
                    tt(cat[:, :, D:2 * D], cat[:, :, D:2 * D], over_windows(BIAS["L2_gnn_b_self"]), ALU.add)
                elif what == "gate":
                    tt(z, z, over_windows(BIAS["L2_gnn_b_gate"]), ALU.add)
                    ask()
                    tt(spare, cat[:, :, D:2 * D], x_cur[:, :, :], ALU.subtract)
                    tt(z, z, spare, ALU.mult)
                    tt(z, z, x_cur[:, :, :], ALU.add)
                    layer_norm(z, spare)
                    tt(z, z, over_windows(BIAS["L2_gnn_ln_gamma"]), ALU.mult)
                    tt(z, z, over_windows(BIAS["L2_gnn_ln_beta"]), ALU.add)
                    step(dve.tensor_scalar(z, z, 0.0, None, ALU.max))
                    tt(x_cur[:, :, :], x_cur[:, :, :], z, ALU.add)
                    layer_norm(x_cur[:, :, :], spare)
                elif what == "att8":
                    den = wide[:, :, HC:HC + HEADS]
                    step(dve.tensor_scalar(den, den, TINY, None, ALU.max))
                    step(dve.reciprocal(den, den))
                    heads = wide[:, :, 0:HC].rearrange("p w (h c) -> p w h c", h=HEADS)
                    tt(heads, heads, den.unsqueeze(3).to_broadcast([P, W, HEADS, HID]), ALU.mult)
                    tt(wide[:, :, 0:HC], wide[:, :, 0:HC], over_windows(bias_wide[:, att - 1, :]), ALU.add)
                    w = 0
                    for n in elu_parts():
                        part = wide[:, w:w + n, 0:HC]
                        low = setup_rows[:, 0:n * HC].rearrange("p (w c) -> p w c", w=n)
                        step(dve.tensor_scalar(low, part, 0.0, None, ALU.min))
                        ask()
                        step(dve.scalar_tensor_tensor(out=part, in0=low, scalar=-1.0, in1=part, op0=ALU.add, op1=ALU.max))
                        w += n
                elif what == "att1":
                    tt(z[:, 0:LOOP_W, :], h_one[:, 0:LOOP_W, 0:D], over_features(ab[:, 0:LOOP_W, 0]), ALU.mult)
                    tt(acc[:, 0:LOOP_W, 0:D], acc[:, 0:LOOP_W, 0:D], z[:, 0:LOOP_W, :], ALU.add)
                    tt(acc[:, 0:LOOP_W, D], acc[:, 0:LOOP_W, D], ab[:, 0:LOOP_W, 0], ALU.add)
                    step(dve.tensor_scalar(stat[:, :], acc[:, :, D], TINY, None, ALU.max))
                    step(dve.reciprocal(stat[:, :], stat[:, :]))
                    tt(acc[:, :, 0:D], acc[:, :, 0:D], over_features(stat[:, :]), ALU.mult)
                    tt(x_cur[:, :, :], x_cur[:, :, :], acc[:, :, 0:D], ALU.add)
                    tt(x_cur[:, :, :], x_cur[:, :, :], over_windows(BIAS["L3_gnn_b3"]), ALU.add)
                    layer_norm(x_cur[:, :, :], spare)
                    dve.sem_inc(sem("result_made"), 1)


def kernel(**inputs):
    import numpy as np
    import concourse.bacc as bacc
    from concourse.bass_utils import run_bass_kernel_spmd

    nc = bacc.Bacc("TRN2", target_bir_lowering=False, num_devices=1)
    arrays, args = {}, {}
    for name, value in inputs.items():
        value = np.ascontiguousarray(value)
        arrays[f"in_{name}"] = value
        args[name] = nc.dram_tensor(f"in_{name}", value.shape, mybir.dt.from_np(value.dtype), kind="ExternalInput").ap()
    result = nc.dram_tensor("result", (N, D), F32, kind="ExternalOutput").ap()
    gnn_kernel(nc, args, result)
    return run_bass_kernel_spmd(nc, [arrays], core_ids=[0]).results[0]["result"]
```

```python
from contextlib import ExitStack

import concourse.bass as bass
from concourse import mybir

F32 = mybir.dt.float32
I32 = mybir.dt.int32
F16 = mybir.dt.float16
BF16 = mybir.dt.bfloat16
ALU = mybir.AluOpType
ACT = mybir.ActivationFunctionType
AX = mybir.AxisListType.X

P = 128
N = 3125
E = 100000
D = 128
R = 8
HEADS, HID = 8, 64
HC = HEADS * HID
HALF = (HC + HEADS) // 2
N_LOOP = 625
WINDOWS = -(-N // P)
W = WINDOWS + WINDOWS % 2
NP = W * P
B = 4
GROUP = B * P
GROUPS = -(-E // GROUP)
V = GROUPS + WINDOWS - 1
UNROLL = 4
LONG_TURN = 12
AHEAD = 3
TILES = -(-E // P)
BATCHES = 2 + -(-(-(-TILES // UNROLL) - 2) // UNROLL) * UNROLL
T_PAD = BATCHES * UNROLL
DEG_LO = 25
DEG_HI = N // DEG_LO
CW = 16
CW_BLOCK = P // CW
C_WINDOWS = WINDOWS * CW_BLOCK
CB = 2
C_GROUPS = -(-E // (CB * P))
CV = -(-(C_GROUPS + C_WINDOWS - 1) // UNROLL) * UNROLL
C_COLS = WINDOWS * CW
RING = 8
WINDOW_BITS, PASS_BITS, BANK_BITS = C_WINDOWS.bit_length(), WINDOWS.bit_length(), RING.bit_length() - 1
STORE_LAG = 4
LOOP_W = -(-N_LOOP // P)
ROW = HC + 2 * HEADS
LN_EPS = 1e-5
SLOPE = 0.2
TINY = 1e-37

N_CONST = 13
assert V % UNROLL == 0 and W % 2 == 0 and DEG_HI * DEG_LO == N and CW_BLOCK == RING

PHASES = [("blocks", "plain"), ("dense", "gcn1"), ("blocks", "plain"), ("dense", "gcn2"),
          ("dense", "rel"), ("dense", "self"), ("pass", "norm"), ("blocks", "plain"), ("dense", "mix"), ("dense", "gate"),
          ("dense", "h1"), ("pass", "att8"), ("dense", "h2"), ("pass", "att8"), ("dense", "h3"), ("blocks", "att1")]
L0_SUM1, L0_SUM2, L2_SUM = (k for k, x in enumerate(PHASES) if x == ("blocks", "plain"))
N_WEIGHTS = 9 + 2 + 2 + 3 + 2 + 3
DENSE = {"gcn1": (1, D, 0), "gcn2": (1, D, 0), "rel": (1, R * D, R * D), "self": (1, D, 0), "mix": (2, D, 0),
         "gate": (2, D, 0), "h1": (1, ROW, HC), "h2": (HC // P, ROW, HC), "h3": (HC // P, D + 2, 0)}


BLOCK_SLOTS = {"plain": 3, "att1": 2}


def gained(kind, what):
    if kind == "pass":
        return {"onehot_ready": V + 2, "sum_ready": V, "sum_added": V, "transposed": V + 2, "transposed_copied": V + 2,
                "looked_up": V + 1, "look_ups_joined": V, "weighted": V, "factor_made": V,
                **({x: V for x in ("half_weighted", "last_weighted", "rows_used")} if what == "att8" else {}),
                "coef_made": 2 * V if what == "norm" else V,
                "index_staged": V + AHEAD, "gathered": V // 2 * 16}
    if kind == "blocks":
        out = {"block_summed": WINDOWS, "block_copied": WINDOWS}
        out.update({f"block_loaded{s}": len(range(s, WINDOWS, BLOCK_SLOTS[what])) * 16 for s in range(BLOCK_SLOTS[what])})
        if what == "att1":
            out.update({x: 2 * WINDOWS for x in ("slope1_made", "slope2_made", "slopes_joined", "block_weighed")})
        return out
    out = {"tile_staged": W, "tile_transposed": W, "tile_copied": W, "product_ready": W, "product_copied": W}
    if DENSE[what][2]:
        out["row_stored"] = W // 2 * 16
    return out


def before(phase, name):
    return sum(gained(*PHASES[k]).get(name, 0) for k in range(phase))


def gnn_kernel(nc, a, out):
    ctx = ExitStack()
    with ctx:
        def sb(name, shape, dt=F32):
            return ctx.enter_context(nc.sbuf_tensor(name, shape, dt))

        def ps(name, shape):
            return ctx.enter_context(nc.psum_tensor(name, shape, F32))

        sems = {}

        def sem(name):
            if name not in sems:
                sems[name] = ctx.enter_context(nc.semaphore(name))
            return sems[name]

        c_matrix = nc.dram_tensor("c_matrix", [WINDOWS, P, CW_BLOCK, C_COLS], F32).ap()
        degree_rows = nc.dram_tensor("degree_rows", [NP * R], F32).ap()
        rel_table = nc.dram_tensor("rel_table", [NP, R * D], F32).ap()
        att_table = [nc.dram_tensor(f"att_table{k}", [NP, ROW], F32).ap() for k in range(2)]
        target_rows = nc.dram_tensor("target_rows", [2, NP], F32).ap()

        ident = sb("ident", [P, P])
        ones = sb("ones", [P, P])
        iota_col = sb("iota_col", [P, P])
        iota_part = sb("iota_part", [P, 1])
        iota_rel = sb("iota_rel", [P, B, R])
        iota_visit = sb("iota_visit", [P, CV])
        iota_row = sb("iota_row", [P, C_WINDOWS])
        iota_node = sb("iota_node", [P, DEG_LO])
        iota_deg = sb("iota_deg", [P, DEG_LO * R], F16)
        iota_16 = sb("iota_16", [P, P], F16)
        iota_c = sb("iota_c", [P, C_COLS], F16)
        window_of = sb("window_of", [P, V + UNROLL], I32)
        c_window = sb("c_window", [P, CV], I32)
        c_pack = sb("c_pack", [P, CV // UNROLL], I32)
        look_pack = sb("look_pack", [P, V // UNROLL], I32)
        add_pack = sb("add_pack", [P, V // UNROLL], I32)
        c_end = sb("c_end", [P, C_WINDOWS], I32)
        edge_row = sb("edge_row", [P, V + AHEAD, B], I32)
        edge_rel_row = sb("edge_rel_row", [P, V + AHEAD, B], I32)
        edge_dst = sb("edge_dst", [P, V + 2, B])
        edge_type = sb("edge_type", [P, V, B])

        wide = sb("wide", [P, W, HC + HEADS])
        x_cur = sb("x_cur", [P, W, D])
        rel_norm = sb("rel_norm", [P, W, R])
        zero_row = sb("zero_row", [1, (NP - N) * R])
        count = sb("count", [P, W])
        dis = sb("dis", [P, W])
        stat = sb("stat", [P, W])
        ab = sb("ab", [P, W, 2 * HEADS])
        rel_degree = sb("rel_degree", [P, DEG_LO * R])
        node_degree = sb("node_degree", [P, DEG_LO])
        uf = sb("uf", [P, W, 2 * HEADS])
        tv = sb("tv", [P, W, 2 * HEADS])
        peak = sb("peak", [P, HEADS])
        peak_all = sb("peak_all", [P, HEADS])
        loop_mask = sb("loop_mask", [P, LOOP_W])
        has = sb("has", [P, W])

        w_gcn = sb("w_gcn", [P, 2, D])
        w_rel = sb("w_rel", [P, R, D])
        w_self = sb("w_self", [P, D])
        w_mix = sb("w_mix", [P, 2, D])
        w_gate = sb("w_gate", [P, 2, D])
        w_h1 = sb("w_h1", [P, 1, ROW])
        w_h2 = sb("w_h2", [P, HC // P, ROW])
        w_h3 = sb("w_h3", [P, HC // P, D + 2])
        rows = sb("rows", [P, 9 * D])
        bias_wide = sb("bias_wide", [P, 2, HC])

        rows_g = sb("rows_g", [P, 2, B, ROW])
        rows_w = sb("rows_w", [P, 2, B, HC + HEADS])
        onehot = sb("onehot", [P, UNROLL, B, P])
        onehot_t = sb("onehot_t", [P, 2, B, P], BF16)
        index_now = sb("index_now", [P, UNROLL, B], I32)
        parts = sb("parts", [P, W * 3 * 2 * HEADS], BF16)
        looked_up = sb("looked_up_values", [P, B, 2 * HEADS])
        factor = sb("factor", [P, B, 2 * HEADS])
        coef = sb("coef", [P, B])
        rel_hot = sb("rel_hot", [P, 2, B, R])
        tile_in = sb("tile_in", [P, 2, HC])
        tile_t = sb("tile_t", [P, 2, HC])
        tile_out = rows_w[:, :, :, :].rearrange("p s b c -> p s (b c)")
        loop_rows = rows_g[:, :, :, :].rearrange("p s b c -> p (s b c)")[:, 0:LOOP_W * HC].rearrange("p (w c) -> p w c", c=HC)

        flat = wide[:, :, :].rearrange("p w c -> p (w c)")
        CH, CCH = -(-GROUPS // P), -(-C_GROUPS // P)
        taken = [0]

        def scratch(cols, dt=F32):
            part = flat[:, taken[0]:taken[0] + cols]
            taken[0] += cols
            assert taken[0] <= W * (HC + HEADS)
            return part if dt is F32 else part.bitcast(dt)

        raw = scratch(CH * 3 * GROUP, I32).rearrange("p (c k e) -> p c k e", c=CH, k=3)
        c_raw = scratch(CCH * 2 * CB * P, I32).rearrange("p (c k e) -> p c k e", c=CCH, k=2)
        p_list, c_list = (flat[:, at:at + n].rearrange("p (c k e) -> p c k e", c=c, k=k)
                          for at, n, c, k in ((0, CH * 3 * GROUP, CH, 3), (CH * 3 * GROUP, CCH * 2 * CB * P, CCH, 2)))
        select = scratch(CH * V).rearrange("p (c v) -> p c v", c=CH)
        c_select = scratch(CCH * CV).rearrange("p (c v) -> p c v", c=CCH)
        free_order = scratch(2 * T_PAD, I32).rearrange("p (k t) -> p k t", k=2)
        deg_hi, deg_lo, deg_tmp = scratch(T_PAD), scratch(T_PAD), scratch(T_PAD)
        deg_int = scratch(T_PAD, I32)
        g_flat = rows_g[:, :, :, :].rearrange("p s b c -> p (s b c)")
        w_flat = rows_w[:, :, :, :].rearrange("p s b c -> p (s b c)")
        TH = 100
        below = w_flat[:, 0:TH * DEG_LO].rearrange("p (k d) -> p k d", k=TH)
        above = sb("above", [P, C_WINDOWS])
        step_row = sb("step_row", [P, C_WINDOWS])
        step_int = sb("step_int", [P, C_WINDOWS], I32)
        step_col = sb("step_col", [P, 4])
        window_f = sb("window_f", [P, CV + UNROLL])
        group_f = sb("group_f", [P, CV + UNROLL])
        reached = w_flat[:, 0:2 * CV].rearrange("p (c v) -> p c v", c=2)
        c_lo = sb("c_lo", [P, CV + 1, CB], F16)
        c_key = sb("c_key", [P, CV + 1, CB])
        deg_hot = w_flat[:, 0:UNROLL * DEG_LO * R].bitcast(F16).rearrange("p (u c) -> p u c", u=2 * UNROLL)
        hi_hot = g_flat[:, RING * C_COLS:RING * C_COLS + UNROLL * P].bitcast(F16).rearrange("p (u c) -> p u c", u=2 * UNROLL)
        lo_hot = onehot[:, :, :, :].rearrange("p u b c -> p (u b c)")[:, 0:UNROLL * CB * P // 2].bitcast(F16) \
            .rearrange("p (u b c) -> p u b c", u=UNROLL, b=CB)
        key_hot = w_flat[:, 0:UNROLL * CB * C_COLS // 2].bitcast(F16).rearrange("p (u b c) -> p u b c", u=UNROLL, b=CB)
        c_int = tile_t[:, :, :].rearrange("p s c -> p (s c)")[:, 0:CV].bitcast(I32).rearrange("p (k v) -> p k v", k=2)
        ring = g_flat[:, 0:RING * C_COLS].rearrange("p (k c) -> p k c", k=RING)
        cat = flat[:, 0:W * 2 * D].rearrange("p (w c) -> p w c", w=W)
        z = flat[:, W * 2 * D:W * 3 * D].rearrange("p (w c) -> p w c", w=W)
        acc = flat[:, W * 3 * D:W * (4 * D + 1)].rearrange("p (w c) -> p w c", w=W)
        spare = rows_w[:, :, :, :].rearrange("p s b c -> p (s b c)")[:, 0:W * D].rearrange("p (w c) -> p w c", w=W)
        setup_rows = g_flat
        c_flat = [flat[:, 0:CW_BLOCK * C_COLS], flat[:, CW_BLOCK * C_COLS:2 * CW_BLOCK * C_COLS], g_flat[:, 0:CW_BLOCK * C_COLS]]
        c_block = [slot.rearrange("p (d h) -> p d h", h=WINDOWS) for slot in c_flat]
        slope1 = g_flat[:, 0:CW_BLOCK * C_COLS].rearrange("p (d h) -> p d h", h=WINDOWS)
        slope2 = flat[:, W * 2 * D:W * 2 * D + CW_BLOCK * C_COLS].rearrange("p (d h) -> p d h", h=WINDOWS)
        h_one = w_flat[:, 0:W * (D + 1)].rearrange("p (w c) -> p w c", w=W)
        target_now = tile_t[:, :, 0:2 * P].rearrange("p s (k d) -> p s k d", k=2)
        att_rows = {"h1": w_flat[:, 0:2 * HC].rearrange("p (k c) -> p k c", k=2),
                    "h2": w_flat[:, 2 * HC:4 * HC].rearrange("p (k c) -> p k c", k=2),
                    "h3": w_flat[:, 4 * HC:4 * HC + 2 * D].rearrange("p (k c) -> p k c", k=2)}
        setup_product = w_flat[:, 5 * HC:6 * HC]

        banks = ps("banks", [P, RING, 512])
        ps_sum, ps_tail, ps_t, ps_v = (banks[:, 2 * k:2 * k + 2, :] for k in range(4))

        BIAS = {}
        for k, name in enumerate(["L0_gnn_b1", "L0_gnn_b2", "L1_gnn_bias", "L2_gnn_b_self", "L2_gnn_b_neigh",
                                  "L2_gnn_b_gate", "L2_gnn_ln_gamma", "L2_gnn_ln_beta", "L3_gnn_b3"]):
            BIAS[name] = rows[:, k * D:(k + 1) * D]

        def over_windows(row):
            return row.unsqueeze(1).to_broadcast([P, W, row.shape[-1]])

        def over_features(column, n=D):
            return column.unsqueeze(2).to_broadcast([P, column.shape[1], n])

        def gather_table(phase):
            att_before = sum(1 for k in range(phase) if PHASES[k] == ("pass", "att8"))
            kind = PHASES[phase][1]
            if kind == "norm":
                return rel_table.rearrange("n (r c) -> (n r) c", c=D), edge_rel_row, D
            return att_table[att_before], edge_row, ROW

        def lookup_values(kind):
            return (rel_norm, R) if kind == "norm" else (tv, 2 * HEADS)

        def parts_of(kind):
            n = 3 * lookup_values(kind)[1]
            return parts[:, 0:W * n].rearrange("p (w c) -> p w c", c=n)

        def loop_tiles(eng, head, body):
            head()
            body(0, 0, 0, False)
            body(1, 1, 0, False)
            with eng.Fori(1, W // 2 - 1) as i:
                body(i * 2, 0, i, False)
                body(i * 2 + 1, 1, i, False)
            body(W - 2, 0, W // 2 - 1, False)
            body(W - 1, 1, W // 2 - 1, True)

        def loop_blocks(eng, body, slots):
            for s in range(slots):
                body(s, s, 0)
            with eng.Fori(1, WINDOWS // slots) as i:
                for s in range(slots):
                    body(i * slots + s, s, i)
            for s in range(WINDOWS % slots):
                body(WINDOWS // slots * slots + s, s, WINDOWS // slots)

        def later(n, at):
            return not isinstance(n, int) or n >= at

        def unpack(eng, pack, i, bits, first=0, most=WINDOWS - 1):
            packed = eng.value_load(pack[0:1, bass.ds(i, 1)], min_val=0, max_val=2 ** (first + bits * UNROLL) - 1)
            return packed, [nc.s_assert_within(eng.snap((packed >> (first + bits * k)) & (2 ** bits - 1)), 0, most,
                                                 skip_runtime_bounds_check_because="the packed list holds windows and banks only")
                            for k in range(UNROLL)]

        def loop_visits(eng, head, body, tail, visits=V, turn=None, steps=UNROLL):
            assert (visits - UNROLL) % steps == 0
            head()
            for n in range(UNROLL):
                body(n, n)
            with eng.Fori(0, (visits - UNROLL) // steps) as i:
                if turn:
                    turn(i + 1)
                for k in range(steps):
                    body(i * steps + UNROLL + k, k % UNROLL)
            tail()

        def loop_batches(eng, body):
            body(0, 0)
            body(1, 1)
            with eng.Fori(0, (BATCHES - 2) // UNROLL) as i:
                for k in range(UNROLL):
                    body(i * UNROLL + 2 + k, k % 2)

        SOURCES = [(0, WINDOWS // 2 + 1), (WINDOWS // 2 + 1, WINDOWS)]
        N_TARGETS = (CW, P)
        N_EDGE_LOADS = 2 * (-(-(C_GROUPS - 1) // P) + 1) + 3 * (-(-(GROUPS - 1) // P) + 1)
        WALKS = [(C_WINDOWS, CV, C_GROUPS, CB, 2), (WINDOWS, V, GROUPS, B, 3)]

        def ordered(walk, k, b, half):
            if walk == 0:
                return (ps_sum, ps_tail, ps_t, ps_v)[2 * k + b][:, half, 0:CV // 2]
            return (ps_tail, ps_sum, ps_t)[k][:, b // 2, b % 2 * 256 + half * (V // 2):b % 2 * 256 + (half + 1) * (V // 2)]

        block = ctx.enter_context(nc.Block())

        @block.sync
        def _(sp):
            sp.wait_ge(sem("lists_cleared"), 3)
            for k, name in enumerate(["dst", "edge_type_8"]):
                whole = E // P
                sp.dma_start(free_order[:, k, 0:whole], a[name][0:whole * P].rearrange("(p t) -> p t", p=P)).then_inc(sem("free_loaded"), 16)
                sp.dma_start(free_order[0:E - whole * P, k, whole:whole + 1],
                             a[name][whole * P:E].rearrange("(p t) -> p t", t=1)).then_inc(sem("free_loaded"), 16)
            for lists, names, groups, size in ((c_raw, ("src", "dst"), C_GROUPS, CB * P), (raw, ("src", "dst", "edge_type_8"), GROUPS, GROUP)):
                for k, name in enumerate(names):
                    for g in range(0, groups - 1, P):
                        n = min(P, groups - 1 - g)
                        sp.dma_start(lists[0:n, g // P, k, :], a[name][g * size:(g + n) * size].rearrange("(g e) -> g e", e=size)
                                     ).then_inc(sem("edges_loaded"), 16)
                    g = (groups - 1) % P
                    sp.dma_start(lists[g:g + 1, (groups - 1) // P, k, 0:E - (groups - 1) * size],
                                 a[name][(groups - 1) * size:E].rearrange("(g e) -> g e", g=1)).then_inc(sem("edges_loaded"), 16)
            full = (N // P) * P
            sp.wait_ge(sem("x_cleared"), 1)
            sp.dma_start(x_cur[:, 0:N // P, :], a["x"][0:full, :].rearrange("(w p) c -> p w c", p=P)).then_inc(sem("x_loaded"), 16)
            sp.dma_start(x_cur[0:N - full, N // P, :], a["x"][full:N, :]).then_inc(sem("x_loaded"), 16)
            for name, row in BIAS.items():
                sp.dma_start(row, a[name].partition_broadcast(P)).then_inc(sem("weights_loaded"), 16)
            sp.dma_start(w_gcn[:, 0, :], a["L0_gnn_W1"]).then_inc(sem("weights_loaded"), 16)
            sp.dma_start(w_gcn[:, 1, :], a["L0_gnn_W2"]).then_inc(sem("weights_loaded"), 16)
            sp.dma_start(w_rel[:, :, :], a["L1_gnn_weight"].rearrange("r d o -> d r o")).then_inc(sem("weights_loaded"), 16)
            sp.dma_start(w_self[:, :], a["L1_gnn_self_weight"]).then_inc(sem("weights_loaded"), 16)
            sp.dma_start(tile_in[:, 0, 0:D], a["L2_gnn_W_self"]).then_inc(sem("weights_loaded"), 16)
            sp.dma_start(tile_in[:, 0, D:2 * D], a["L2_gnn_W_neigh"]).then_inc(sem("weights_loaded"), 16)
            sp.dma_start(tile_in[:, 0, 2 * D:4 * D], a["L2_gnn_W_gate"]).then_inc(sem("weights_loaded"), 16)
            sp.dma_start(w_h1[:, 0, 0:HC], a["L3_gnn_W1"]).then_inc(sem("weights_loaded"), 16)
            sp.dma_start(w_h2[:, :, 0:HC], a["L3_gnn_W2"].rearrange("(k p) c -> p k c", p=P)).then_inc(sem("weights_loaded"), 16)
            for k in range(2):
                sp.dma_start(bias_wide[:, k, :], a[f"L3_gnn_b{k + 1}"].partition_broadcast(P)).then_inc(sem("weights_loaded"), 16)
            sp.dma_start(w_h3[:, :, 0:D], a["L3_gnn_W3"].rearrange("(k p) c -> p k c", p=P)).then_inc(sem("weights_loaded"), 16)

            sp.wait_ge(sem("degree_rows_made"), 1)
            sp.dma_start(degree_rows[0:N * R].rearrange("(p c) -> p c", p=DEG_HI), rel_degree[0:DEG_HI, :]).then_inc(sem("degree_rows_stored"), 16)
            sp.dma_start(degree_rows[N * R:NP * R].rearrange("(a c) -> a c", a=1), zero_row[0:1, 0:(NP - N) * R]).then_inc(sem("degree_rows_stored"), 16)
            sp.wait_ge(sem("degree_rows_stored"), 32)
            sp.dma_start(rel_norm[:, :, :], degree_rows.rearrange("(w p r) -> p w r", p=P, r=R)).then_inc(sem("degrees_loaded"), 16)

            sp.sem_inc(sem("ring_slots_free"), RING - STORE_LAG)
            for w in range(RING - STORE_LAG, RING):
                sp.sem_inc(sem(f"c_stored{w}"), 16)
            with sp.Fori(0, WINDOWS) as j:
                for w in range(CW_BLOCK):
                    sp.wait_ge(sem("c_copied"), j * CW_BLOCK + w + 1)
                    sp.dma_start(c_matrix[bass.ds(j, 1), :, w, :].rearrange("j p c -> p (j c)"), ring[:, w, :]).then_inc(sem(f"c_stored{w}"), 16)
                    sp.wait_ge(sem(f"c_stored{(w - STORE_LAG) % RING}"), j * 16 + 16)
                    sp.sem_inc(sem("ring_slots_free"), 1)
            for w in range(RING - STORE_LAG, RING):
                sp.wait_ge(sem(f"c_stored{w}"), WINDOWS * 16 + 16)
                sp.sem_inc(sem("ring_slots_free"), 1)
            for k, side in enumerate(("src", "dst")):
                for layer, name in enumerate(("h1", "h2", "h3"), 1):
                    sp.dma_start(att_rows[name][:, k, :], a[f"L3_gnn_a_{side}{layer}"].rearrange("h c -> (h c)").partition_broadcast(P)).then_inc(sem("attention_loaded"), 16)

            att = 0
            for phase, (kind, what) in enumerate(PHASES):
                if kind == "blocks":
                    if what == "att1":
                        sp.wait_ge(sem("factors_made"), 3)
                        sp.dma_start(target_rows.rearrange("k (w p) -> (k w) p", p=P), tile_in[0:2 * W, 1, 0:P]).then_inc(sem("target_rows_stored"), 16)
                        sp.wait_ge(sem("target_rows_stored"), 16)
                    sp.wait_ge(sem("blocks_begun"), 1 + sum(PHASES[k][0] == "blocks" for k in range(phase)))
                    summed = before(phase, "block_summed")

                    slots = BLOCK_SLOTS[what]

                    def load_block(j, s, turn):
                        if what == "att1":
                            if later(j, 2):
                                sp.wait_ge(sem("slopes_joined"), 2 * j - 2)
                            for k in range(2):
                                sp.dma_start(tile_t[:, s, k * P:(k + 1) * P], target_rows[k, bass.ds(j * P, P)].partition_broadcast(P)
                                             ).then_inc(sem(f"target_loaded{s}"), 16)
                        if later(j, slots):
                            sp.wait_ge(sem("block_summed"), summed + j - slots + 1)
                        sp.dma_start(c_flat[s], c_matrix[bass.ds(j, 1), :, :, :].rearrange("j p w c -> p (j w c)")
                                     ).then_inc(sem(f"block_loaded{s}"), 16)

                    loop_blocks(sp, load_block, slots)
                if kind == "dense" and DENSE[what][2]:
                    cols = DENSE[what][2]
                    table = {"rel": rel_table, "h1": att_table[0], "h2": att_table[1]}[what]
                    copied, stored = before(phase, "product_copied"), before(phase, "row_stored")

                    with sp.Fori(0, W // 2) as i:
                        for s in range(2):
                            sp.wait_ge(sem("product_copied"), copied + i * 2 + s + 1)
                            sp.dma_start(table[bass.ds((i * 2 + s) * P, P), 0:cols], tile_out[:, s, 0:cols]).then_inc(sem(f"row_stored{s}"), 16)
                    for s in range(2):
                        sp.wait_ge(sem(f"row_stored{s}"), stored + W // 2 * 16)
                    sp.sem_inc(sem("rows_stored"), 1)
                if what == "att8":
                    att += 1
                    table = att_table[att - 1]
                    sp.dma_start(loop_rows[:, :, 0:HC], table[0:LOOP_W * P, 0:HC].rearrange("(w p) c -> p w c", p=P)).then_inc(sem("loop_rows_loaded"), 16)
                    sp.wait_ge(sem("factors_made"), att)
                    sp.dma_start(table[:, HC:ROW].rearrange("(w p) c -> p w c", p=P), uf[:, :, :]).then_inc(sem("factors_stored"), 16)
            sp.wait_ge(sem("result_made"), 1)
            sp.dma_start(out[0:full, :].rearrange("(w p) c -> p w c", p=P), x_cur[:, 0:N // P, :]).then_inc(sem("result_stored"), 16)
            sp.dma_start(out[full:N, :], x_cur[0:N - full, N // P, :]).then_inc(sem("result_stored"), 16)
            sp.wait_ge(sem("result_stored"), 32)

        @block.gpsimd
        def _(pool):
            pool.memset(free_order, -200).then_inc(sem("lists_cleared"), 1)
            pool.memset(c_raw[:, CCH - 1, :, :], -1).then_inc(sem("lists_cleared"), 1)
            pool.memset(raw[:, CH - 1, :, :], -1).then_inc(sem("lists_cleared"), 1)
            pool.memset(x_cur[:, N // P:W, :], 0.0).then_inc(sem("x_cleared"), 1)
            pool.memset(ident[:, :], 0.0).then_inc(sem("ident_zero"), 1)
            pool.wait_ge(sem("ident_zero"), 1)
            pool.affine_select(out=ident[:, :], in_=ident[:, :], compare_op=ALU.not_equal, fill=1.0, base=0,
                               pattern=[[-1, P]], channel_multiplier=1).then_inc(sem("constants"), 1)
            pool.iota(iota_col[:, :], pattern=[[1, P]], base=0, channel_multiplier=0,
                      allow_small_or_imprecise_dtypes=True).then_inc(sem("constants"), 1)
            pool.iota(iota_part[:, :], pattern=[[0, 1]], base=0, channel_multiplier=1,
                      allow_small_or_imprecise_dtypes=True).then_inc(sem("constants"), 1)
            pool.iota(iota_rel[:, :, :], pattern=[[0, B], [1, R]], base=0, channel_multiplier=0,
                      allow_small_or_imprecise_dtypes=True).then_inc(sem("constants"), 1)
            for tile, pattern, base, across in (
                    (iota_visit[:, :], [[1, CV]], 0, 0), (iota_row[:, :], [[1, C_WINDOWS]], 0, 0), (iota_node[:, :], [[1, DEG_LO]], 0, DEG_LO),
                    (iota_deg[:, :], [[1, DEG_LO * R]], 0, 0), (iota_c[:, :], [[1, C_COLS]], 0, 0), (iota_16[:, :], [[1, P]], 0, 0)):
                pool.iota(tile, pattern=pattern, base=base, channel_multiplier=across,
                          allow_small_or_imprecise_dtypes=True).then_inc(sem("constants"), 1)
            pool.memset(zero_row[:, :], 0.0).then_inc(sem("constants"), 1)
            pool.iota(loop_mask[:, :], pattern=[[P, LOOP_W]], base=0, channel_multiplier=1,
                      allow_small_or_imprecise_dtypes=True).then_inc(sem("constants"), 1)
            pool.memset(ones[:, :], 1.0).then_inc(sem("constants"), 1)

            passes = 0
            att = 0
            for phase, (kind, what) in enumerate(PHASES):
                if what in ("att8", "att1"):
                    att += 1
                    pool.wait_ge(sem("peak_ready"), att)
                    nh = HEADS if what == "att8" else 1
                    pool.partition_all_reduce(peak_all[:, 0:nh], peak[:, 0:nh], P, bass.bass_isa.ReduceOp.max).then_inc(sem("peak_reduced"), 1)
                if what == "att1":
                    pool.wait_ge(sem("blocks_begun"), sum(k == "blocks" for k, _ in PHASES))

                    def slope_one(j, s, turn):
                        pool.wait_ge(sem(f"target_loaded{s}"), turn * 32 + 32)
                        for q, (lo, hi) in enumerate(SOURCES):
                            if later(j, 1):
                                pool.wait_ge(sem("slopes_joined"), 2 * j + q - 1)
                            shape = [P, P, hi - lo]
                            pool.tensor_tensor(slope1[:, :, lo:hi], uf[:, lo:hi, 0].unsqueeze(1).to_broadcast(shape),
                                               target_now[:, s, 0, :].unsqueeze(2).to_broadcast(shape), ALU.mult
                                               ).then_inc(sem("slope1_made"), 1)

                    loop_blocks(pool, slope_one, BLOCK_SLOTS[what])
                if kind != "pass":
                    continue
                passes += 1
                table, index, cols = gather_table(phase)
                if what == "norm":
                    pool.wait_ge(sem("rows_stored"), 1)
                else:
                    pool.wait_ge(sem("factors_stored"), 16 * att)
                pool.wait_ge(sem("pass_begun"), passes)
                staged = before(phase, "index_staged")
                summed, half, used = (before(phase, x) for x in ("sum_ready", "half_weighted", "rows_used"))

                def gather(n, k):
                    s = k % 2
                    if later(n, 2):
                        if what == "att8":
                            pool.wait_ge(sem("half_weighted"), half + n - 1)
                        else:
                            pool.wait_ge(sem("sum_ready"), summed + n - 1)
                    pool.wait_ge(sem("index_staged"), staged + n + 1)
                    pool.sem_inc(sem("gather_turn"), 1)
                    for b in range(B):
                        if b == B // 2 and what == "att8" and later(n, 2):
                            pool.wait_ge(sem("rows_used"), used + n - 1)
                            pool.sem_inc(sem("gather_turn"), 1)
                        pool.indirect_dma_start(rows_g[:, s, b, 0:cols], None, table,
                                                bass.IndirectOffsetOnAxis(ap=index_now[:, k, b:b + 1], axis=0)
                                                ).then_inc(sem(f"gathered{s * B + b}"), 16)

                loop_visits(pool, lambda: None, gather, lambda: None, steps=LONG_TURN)

        def functions_before(what):
            if what not in ("att8", "att1"):
                return []
            nh, at = (HEADS if what == "att8" else 1), 0
            return [(uf[:, :, at:at + nh], ACT.Exp, 1.0), (uf[:, :, at + nh:at + 2 * nh], ACT.Exp, SLOPE),
                    (tv[:, :, 0:nh], ACT.Exp, 1 - SLOPE), (tv[:, :, nh:2 * nh], ACT.Exp, SLOPE - 1)]

        def functions_after(what):
            norm = [(stat[:, :], ACT.Sqrt, 1.0)]
            if what in ("gcn2", "norm", "att1"):
                return norm
            if what == "gate":
                return [(z, ACT.Sigmoid, 1.0)] + norm + norm
            if what == "att8":
                return [(setup_rows[:, 0:n * HC], ACT.Exp, 1.0) for n in elu_parts()]
            return []

        def elu_parts():
            most = 2 * B * ROW // HC
            return [min(most, W - w) for w in range(0, W, most)]

        @block.scalar
        def _(act):
            act.wait_ge(sem("degree_keys_ready"), 1)

            def hi_onehots(j, s):
                if later(j, 2):
                    act.wait_ge(sem("degree_batch_added"), j - 1)
                for k in range(UNROLL // 2, UNROLL):
                    last = act.activation(hi_hot[:, s * UNROLL + k, :], iota_16[:, :], ACT.Square, scale=-1.0,
                                          bias=deg_hi[:, bass.ds(j * UNROLL + k, 1)])
                last.then_inc(sem("hi_squared"), 1)
                act.wait_ge(sem("hi_squared"), j + 1)
                half = hi_hot[:, s * UNROLL + UNROLL // 2:(s + 1) * UNROLL, :]
                act.activation(half, half, ACT.Relu, scale=-1.0, bias=ones[:, 0:1]).then_inc(sem("hi_made"), 1)

            loop_batches(act, hi_onehots)
            act.wait_ge(sem("weights_turned"), 1)
            act.activation(w_mix[:, :, :].rearrange("p k c -> p (k c)"), ps_t[:, 0, 0:2 * D], ACT.Copy).then_inc(sem("weights_ready"), 1)
            act.activation(w_gate[:, :, :].rearrange("p k c -> p (k c)"), ps_t[:, 0, 2 * D:4 * D], ACT.Copy).then_inc(sem("weights_ready"), 1)

            act.wait_ge(sem("c_walk_ready"), 1)
            with act.Fori(0, WINDOWS) as j:
                for w in range(CW_BLOCK):
                    end = act.value_load(c_end[0:1, bass.ds(j * CW_BLOCK + w, 1)], min_val=1, max_val=CV)
                    act.wait_ge(sem("c_counted"), end)
                    act.wait_ge(sem("ring_slots_free"), j * CW_BLOCK + w + 1)
                    act.activation(ring[:, w, :], banks[:, w, 0:C_COLS], ACT.Copy).then_inc(sem("c_copied"), 1)
                    act.wait_ge(sem("c_copied"), j * CW_BLOCK + w + 1)
                    act.activation(banks[:, w, 0:C_COLS], ring[:, w, :], ACT.Copy, scale=0.0).then_inc(sem("banks_free"), 1)

            asked = 1
            act.wait_ge(sem("function_asked"), asked)
            act.activation(dis[:, :], dis[:, :], ACT.Sqrt).then_inc(sem("function_done"), 1)

            for phase, (kind, what) in enumerate(PHASES):
                for buffer, f, scale in functions_before(what):
                    asked += 1
                    act.wait_ge(sem("function_asked"), asked)
                    act.activation(buffer, buffer, f, scale=scale).then_inc(sem("function_done"), 1)
                if kind == "blocks":
                    summed = before(phase, "block_summed")
                    cols = D + 1 if what == "att1" else D

                    def slope_two(j, s, turn):
                        act.wait_ge(sem(f"target_loaded{s}"), turn * 32 + 32)
                        for q, (lo, hi) in enumerate(SOURCES):
                            if later(j, 1):
                                act.wait_ge(sem("block_weighed"), 2 * j + q - 1)
                            for h in range(lo, hi):
                                last = act.activation(slope2[:, :, h], target_now[:, s, 1, :], ACT.Copy, scale=uf[:, h, 1:2])
                            last.then_inc(sem("slope2_made"), 1)
                        if later(j, 1):
                            copy_block(j - 1, 1 - s, turn)

                    def copy_block(j, s, turn):
                        act.wait_ge(sem("block_summed"), summed + j + 1)
                        act.activation(acc[:, bass.ds(j, 1), 0:cols], banks[:, s:s + 1, 0:cols], ACT.Copy).then_inc(sem("block_copied"), 1)

                    if what == "att1":
                        act.wait_ge(sem("blocks_begun"), sum(k == "blocks" for k, _ in PHASES))
                        loop_blocks(act, slope_two, BLOCK_SLOTS[what])
                        copy_block(WINDOWS - 1, 0, 0)
                    else:
                        loop_blocks(act, copy_block, BLOCK_SLOTS[what])
                if kind == "pass":
                    turned, looked = before(phase, "transposed"), before(phase, "looked_up")

                    index = gather_table(phase)[1]
                    summed, attended, weighted, last_weighted = (before(phase, x) for x in ("sum_ready", "coef_made", "weighted", "last_weighted"))

                    def weigh_last(n, k):
                        s, b = k % 2, B - 1
                        act.wait_ge(sem("coef_made"), attended + n + 1)
                        for h in range(HEADS):
                            last = act.activation(rows_w[:, s, b, h * HID:(h + 1) * HID], rows_g[:, s, b, h * HID:(h + 1) * HID], ACT.Copy,
                                                  scale=rows_w[:, s, b, HC + h:HC + h + 1])
                        last.then_inc(sem("last_weighted"), 1)
                        act.wait_ge(sem("last_weighted"), last_weighted + n + 1)
                        act.wait_ge(sem("weighted"), weighted + n + 1)
                        act.sem_inc(sem("rows_used"), 1)

                    def stage_index(n, k):
                        if later(n, UNROLL):
                            act.wait_ge(sem("sum_ready"), summed + n - UNROLL + 1)
                        act.activation(index_now[:, k % UNROLL:k % UNROLL + 1, :], index[:, bass.ds(n, 1), :], ACT.Copy).then_inc(sem("index_staged"), 1)

                    def copy_onehot(m, k):
                        s = k % 2
                        act.wait_ge(sem("transposed"), turned + m + 1)
                        if later(m, 2):
                            act.wait_ge(sem("looked_up"), looked + m - 1)
                        act.activation(onehot_t[:, s, :, :].rearrange("p b c -> p (b c)"), ps_t[:, s, :],
                                       ACT.Copy).then_inc(sem("transposed_copied"), 1)

                    def start():
                        for n in range(AHEAD):
                            stage_index(n, n)
                        copy_onehot(0, 0)
                        copy_onehot(1, 1)

                    def visit(n, k):
                        if what == "att8":
                            weigh_last(n, k)
                        copy_onehot(n + 2, k + 2)
                        stage_index(n + AHEAD, k + AHEAD)

                    loop_visits(act, start, visit, lambda: None)
                elif kind == "dense":
                    chunks, cols, to_table = DENSE[what]
                    turned, product, stored = (before(phase, x) for x in ("tile_transposed", "product_ready", "row_stored"))

                    def copy_tile(w, s):
                        act.wait_ge(sem("tile_transposed"), turned + w + 1)
                        if later(w, 2):
                            act.wait_ge(sem("product_ready"), product + w - 1)
                        act.activation(tile_t[:, s, 0:chunks * P], ps_t[:, s, 0:chunks * P], ACT.Copy).then_inc(sem("tile_copied"), 1)

                    def copy_product(w, s, turn):
                        act.wait_ge(sem("product_ready"), product + w + 1)
                        if what == "h3":
                            act.activation(h_one[:, bass.ds(w, 1), 0:D], ps_sum[:, s:s + 1, 0:D], ACT.Copy)
                            act.activation(ab[:, bass.ds(w, 1), 0:2], ps_sum[:, s:s + 1, D:D + 2], ACT.Copy).then_inc(sem("product_copied"), 1)
                            return
                        if not to_table:
                            act.activation(z[:, bass.ds(w, 1), :], ps_sum[:, s:s + 1, 0:D], ACT.Copy).then_inc(sem("product_copied"), 1)
                            return
                        if later(w, 2):
                            act.wait_ge(sem(f"row_stored{s}"), stored + turn * 16)
                        split = ROW // 2 if cols == ROW else 512
                        act.activation(tile_out[:, s, 0:split], ps_sum[:, s, 0:split], ACT.Copy)
                        last = act.activation(tile_out[:, s, split:to_table], ps_tail[:, s, 0:to_table - split], ACT.Copy)
                        if cols == ROW:
                            last = act.activation(ab[:, bass.ds(w, 1), :], ps_tail[:, s:s + 1, HC - split:ROW - split], ACT.Copy)
                        last.then_inc(sem("product_copied"), 1)

                    def tile(w, s, turn, last):
                        if not last:
                            copy_tile(w + 1, 1 - s)
                        copy_product(w, s, turn)

                    loop_tiles(act, lambda: copy_tile(0, 0), tile)
                for buffer, f, scale in functions_after(what):
                    asked += 1
                    act.wait_ge(sem("function_asked"), asked)
                    act.activation(buffer, buffer, f, scale=scale).then_inc(sem("function_done"), 1)

        @block.tensor
        def _(pe):
            def degree_batch(j, s):
                pe.wait_ge(sem("degree_batch_ready"), j + 1)
                pe.wait_ge(sem("hi_made"), j + 1)
                for k in range(UNROLL):
                    last = pe.matmul(ps_v[:, 0, 0:DEG_LO * R], hi_hot[:, s * UNROLL + k, :], deg_hot[:, s * UNROLL + k, :],
                                     start=(isinstance(j, int) and j == 0 and k == 0), stop=True, skip_group_check=True)
                last.then_inc(sem("degree_batch_added"), 1)

            loop_batches(pe, degree_batch)

            for n, (windows, visits, groups, tiles, values) in enumerate(WALKS):
                pe.wait_ge(sem("above_ready"), n + 1)
                pe.matmul(ps_v[:, 0, 0:windows - 1], ones[:, :], above[:, 0:windows - 1], start=True, stop=True)
                for c in range(-(-(windows - 1) // P)):
                    k = min(P, windows - 1 - c * P)
                    last = pe.matmul(ps_v[0:k, 1, c:c + 1], above[:, c * P:c * P + k], ones[:, 0:1], start=True, stop=True)
                last.then_inc(sem("above_summed"), 1)
                pe.wait_ge(sem("reached_ready"), n + 1)
                parts = -(-(windows - 1) // P)
                for half in range(2):
                    for c in range(parts):
                        k = min(P, windows - 1 - c * P)
                        last = pe.matmul(ps_t[:, half, 0:visits // 2], ones[0:k, :], reached[0:k, c, half * (visits // 2):(half + 1) * (visits // 2)],
                                         start=(c == 0), stop=(c == parts - 1))
                last.then_inc(sem("windows_summed"), 1)
                pe.wait_ge(sem("select_ready"), n + 1)
                pick, source = (c_select, c_list) if n == 0 else (select, p_list)
                chunks = -(-groups // P)
                for k in range(values):
                    for b in range(tiles):
                        for half in range(2):
                            for c in range(chunks):
                                last = pe.matmul(ordered(n, k, b, half), source[:, c, k, b * P:(b + 1) * P],
                                                 pick[:, c, half * (visits // 2):(half + 1) * (visits // 2)], start=(c == 0), stop=(c == chunks - 1))
                last.then_inc(sem("lists_ordered"), 1)
            pe.wait_ge(sem("weights_loaded"), 16 * N_WEIGHTS)
            pe.wait_ge(sem("lists_taken"), 2)
            for k in range(4):
                last = pe.transpose(ps_t[:, 0, k * P:(k + 1) * P], tile_in[:, 0, k * P:(k + 1) * P], ident[:, :])
            last.then_inc(sem("weights_turned"), 1)
            pe.wait_ge(sem("weights_ready"), 2)

            pe.wait_ge(sem("c_walk_ready"), 1)

            turn_banks = []

            def next_banks(i):
                packed, turn_banks[:] = unpack(pe, c_pack, i, BANK_BITS, WINDOW_BITS, RING - 1)
                pe.wait_ge(sem("banks_free"), (packed & (2 ** WINDOW_BITS - 1)) + 1)

            def count_pairs(n, k):
                if isinstance(n, int):
                    bank = pe.value_load(c_window[0:1, n:n + 1], min_val=0, max_val=RING - 1)
                else:
                    bank = turn_banks[k]
                pe.wait_ge(sem("c_key_ready"), n + 1)
                for b in range(CB):
                    last = pe.matmul(banks[:, bass.ds(bank, 1), 0:C_COLS], lo_hot[:, k, b, :], key_hot[:, k, b, :],
                                     start=False, stop=True, skip_group_check=True)
                last.then_inc(sem("c_counted"), 1)

            loop_visits(pe, lambda: None, count_pairs, lambda: None, CV, next_banks)

            for phase, (kind, what) in enumerate(PHASES):
                at = {x: before(phase, x) for x in ("onehot_ready", "transposed_copied", "weighted", "half_weighted", "last_weighted", "gathered", "sum_added",
                                                    "tile_staged", "tile_copied", "product_copied", "block_copied",
                                                    "block_loaded0", "block_loaded1", "block_loaded2")}
                if kind == "blocks":
                    rows_of = {L0_SUM1: z, L0_SUM2: z, L2_SUM: x_cur}.get(phase, h_one)
                    cols = D + 1 if what == "att1" else D
                    if what == "att1":
                        pe.wait_ge(sem("targets_ready"), 1)
                        pe.transpose(ps_v[0:2 * W, 0, 0:P], tile_in[:, 0, 0:2 * W], ident[:, :]).then_inc(sem("targets_transposed"), 1)
                    pe.wait_ge(sem("blocks_begun"), 1 + sum(PHASES[k][0] == "blocks" for k in range(phase)))

                    slots = BLOCK_SLOTS[what]

                    def sum_block(j, s, turn):
                        pe.wait_ge(sem(f"block_loaded{s}"), at[f"block_loaded{s}"] + turn * 16 + 16)
                        if later(j, slots):
                            pe.wait_ge(sem("block_copied"), at["block_copied"] + j - slots + 1)
                        for h in range(WINDOWS):
                            for q, (lo, hi) in enumerate(SOURCES):
                                if what == "att1" and h == lo:
                                    pe.wait_ge(sem("block_weighed"), 2 * j + q + 1)
                            last = pe.matmul(banks[:, s, 0:cols], c_block[s][:, :, h], rows_of[:, h, 0:cols], start=(h == 0), stop=(h == WINDOWS - 1))
                        last.then_inc(sem("block_summed"), 1)

                    loop_blocks(pe, sum_block, slots)
                elif kind == "pass":
                    values, n_values = parts_of(what), 3 * lookup_values(what)[1]

                    turn_windows = []

                    def next_windows(i):
                        turn_windows[:] = unpack(pe, look_pack, i, PASS_BITS)[1]

                    def turn_onehot(m, k):
                        s, o = k % 2, k % UNROLL
                        pe.wait_ge(sem("onehot_ready"), at["onehot_ready"] + m + 1)
                        for b in range(B):
                            last = pe.transpose(ps_t[:, s, b * P:(b + 1) * P], onehot[:, o, b, :], ident[:, :])
                        last.then_inc(sem("transposed"), 1)

                    def look_up(m, k):
                        s = k % 2
                        window = turn_windows[k - 1] if not isinstance(m, int) else \
                            pe.value_load(window_of[0:1, m:m + 1], min_val=0, max_val=WINDOWS - 1)
                        if later(m, 2):
                            pe.wait_ge(sem("weighted"), at["weighted"] + m - 1)
                        pe.wait_ge(sem("transposed_copied"), at["transposed_copied"] + m + 1)
                        for b in range(B):
                            last = pe.matmul(ps_v[:, s, b * n_values:(b + 1) * n_values], onehot_t[:, s, b, :],
                                             values[:, bass.ds(window, 1), 0:n_values], start=True, stop=True)
                        last.then_inc(sem("looked_up"), 1)

                    def sum_rows(n, k):
                        s = k % 2
                        pe.wait_ge(sem("half_weighted" if what == "att8" else "weighted"),
                                   at["half_weighted" if what == "att8" else "weighted"] + n + 1)
                        if later(n, 2):
                            pe.wait_ge(sem("sum_added"), at["sum_added"] + n - 1)
                        for b in range(B):
                            if what == "norm":
                                pe.wait_ge(sem(f"gathered{s * B + b}"), at["gathered"] + (n - s) * 8 + 16)
                            if b == B // 2 and what == "att8":
                                pe.wait_ge(sem("weighted"), at["weighted"] + n + 1)
                            if b == B - 1 and what == "att8":
                                pe.wait_ge(sem("last_weighted"), at["last_weighted"] + n + 1)
                            flags = {"start": b == 0, "stop": b == B - 1}
                            hot = onehot[:, k, b, :]
                            if what == "att8":
                                pe.matmul(ps_sum[:, s, 0:HALF], hot, rows_w[:, s, b, 0:HALF], **flags)
                                last = pe.matmul(ps_tail[:, s, 0:HALF], hot, rows_w[:, s, b, HALF:2 * HALF], **flags)
                            else:
                                last = pe.matmul(ps_sum[:, s, 0:D], hot, rows_g[:, s, b, 0:D], **flags)
                        last.then_inc(sem("sum_ready"), 1)

                    def visit(n, k):
                        look_up(n + 1, k + 1)
                        turn_onehot(n + 2, k + 2)
                        sum_rows(n, k)

                    def start():
                        turn_onehot(0, 0)
                        look_up(0, 0)
                        turn_onehot(1, 1)

                    loop_visits(pe, start, visit, lambda: None, turn=next_windows)
                else:
                    chunks, cols, to_table = DENSE[what]
                    weights = {"gcn1": w_gcn[:, 0:1, :], "gcn2": w_gcn[:, 1:2, :], "rel": w_rel[:, :, :].rearrange("p r c -> p (r c)").unsqueeze(1),
                               "self": w_self[:, :].unsqueeze(1), "mix": w_mix, "gate": w_gate, "h1": w_h1, "h2": w_h2, "h3": w_h3}[what]

                    def turn_tile(w, s):
                        pe.wait_ge(sem("tile_staged"), at["tile_staged"] + w + 1)
                        if later(w, 2):
                            pe.wait_ge(sem("tile_copied"), at["tile_copied"] + w - 1)
                        for c in range(chunks):
                            last = pe.transpose(ps_t[:, s, c * P:(c + 1) * P], tile_in[:, s, c * P:(c + 1) * P], ident[:, :])
                        last.then_inc(sem("tile_transposed"), 1)

                    def product(w, s):
                        pe.wait_ge(sem("tile_copied"), at["tile_copied"] + w + 1)
                        if later(w, 2):
                            pe.wait_ge(sem("product_copied"), at["product_copied"] + w - 1)
                        split = ROW // 2 if cols == ROW else 512
                        for c in range(chunks):
                            for lo, bank in ((0, ps_sum), (split, ps_tail)):
                                n = min(split, cols - lo)
                                if n > 0:
                                    last = pe.matmul(bank[:, s, 0:n], tile_t[:, s, c * P:(c + 1) * P], weights[:, c, lo:lo + n],
                                                     start=(c == 0), stop=(c == chunks - 1))
                        last.then_inc(sem("product_ready"), 1)

                    def tile(w, s, turn, last):
                        if not last:
                            turn_tile(w + 1, 1 - s)
                        product(w, s)

                    loop_tiles(pe, lambda: turn_tile(0, 0), tile)

        @block.vector
        def _(dve):
            steps = 0

            def step(ins):
                nonlocal steps
                steps += 1
                ins.then_inc(sem("dve_step"), 1)
                dve.wait_ge(sem("dve_step"), steps)

            asked = 0

            def ask():
                nonlocal asked
                asked += 1
                dve.sem_inc(sem("function_asked"), 1)
                dve.wait_ge(sem("function_done"), asked)

            def tt(out_, x, y, op):
                step(dve.tensor_tensor(out_, x, y, op))

            def layer_norm(x, scratch):
                step(dve.tensor_reduce(stat[:, :], x, AX, ALU.add))
                step(dve.tensor_scalar(stat[:, :], stat[:, :], 1.0 / D, None, ALU.mult))
                tt(x, x, over_features(stat[:, :]), ALU.subtract)
                tt(scratch, x, x, ALU.mult)
                step(dve.tensor_reduce(stat[:, :], scratch, AX, ALU.add))
                step(dve.tensor_scalar(stat[:, :], stat[:, :], 1.0 / D, LN_EPS, ALU.mult, ALU.add))
                ask()
                step(dve.reciprocal(stat[:, :], stat[:, :]))
                tt(x, x, over_features(stat[:, :]), ALU.mult)

            dve.wait_ge(sem("constants"), N_CONST)
            dve.wait_ge(sem("free_loaded"), 64)
            step(dve.tensor_copy(deg_hi, free_order[:, 0, :]))
            step(dve.tensor_scalar(deg_lo, deg_hi, 1.0 / DEG_LO, 0.5 / DEG_LO - 0.5, ALU.mult, ALU.add))
            step(dve.tensor_copy(deg_int, deg_lo))
            step(dve.tensor_copy(deg_lo, deg_int))
            step(dve.scalar_tensor_tensor(out=deg_hi, in0=deg_lo, scalar=-float(DEG_LO), in1=deg_hi, op0=ALU.mult, op1=ALU.add))
            step(dve.tensor_scalar(deg_hi, deg_hi, float(R), None, ALU.mult))
            step(dve.tensor_copy(deg_tmp, free_order[:, 1, :]))
            tt(deg_tmp, deg_tmp, deg_hi, ALU.add)
            step(dve.tensor_copy(deg_hi, deg_lo))
            step(dve.tensor_copy(deg_lo, deg_tmp))
            dve.sem_inc(sem("degree_keys_ready"), 1)

            def degree_onehots(j, s):
                if later(j, 2):
                    dve.wait_ge(sem("degree_batch_added"), j - 1)
                for k in range(UNROLL):
                    tile, slot = bass.ds(j * UNROLL + k, 1), s * UNROLL + k
                    if k < UNROLL // 2:
                        dve.tensor_scalar(hi_hot[:, slot, :], iota_16[:, :], deg_hi[:, tile], None, ALU.is_equal)
                    last = dve.tensor_scalar(deg_hot[:, slot, :], iota_deg[:, :], deg_lo[:, tile], None, ALU.is_equal)
                last.then_inc(sem("degree_batch_ready"), 1)

            loop_batches(dve, degree_onehots)
            dve.wait_ge(sem("degree_batch_added"), BATCHES)
            step(dve.tensor_copy(rel_degree[:, :], ps_v[:, 0, 0:DEG_LO * R]))
            dve.sem_inc(sem("degree_rows_made"), 1)
            step(dve.tensor_reduce(node_degree[:, :], rel_degree[:, :].rearrange("p (d r) -> p d r", r=R), AX, ALU.add))

            dve.wait_ge(sem("edges_loaded"), 16 * N_EDGE_LOADS)
            for n, (windows, visits, groups, tiles, values) in enumerate(WALKS):
                size = N_TARGETS[n]
                for k in range(0, windows - 1, TH):
                    m = min(TH, windows - 1 - k)
                    step(dve.tensor_scalar(step_row[:, 0:m], iota_row[:, k:k + m], 1.0, float(size), ALU.add, ALU.mult))
                    tt(below[:, 0:m, :], iota_node[:, :].unsqueeze(1).to_broadcast([P, m, DEG_LO]),
                       step_row[:, 0:m].unsqueeze(2).to_broadcast([P, m, DEG_LO]), ALU.is_ge)
                    tt(below[:, 0:m, :], below[:, 0:m, :], node_degree[:, :].unsqueeze(1).to_broadcast([P, m, DEG_LO]), ALU.mult)
                    step(dve.tensor_reduce(above[:, k:k + m], below[:, 0:m, :], AX, ALU.add))
                dve.sem_inc(sem("above_ready"), 1)
                int_list, float_list = ((c_raw, c_list), (raw, p_list))[n]
                for k in range(values):
                    step(dve.tensor_scalar(float_list[:, :, k, :], int_list[:, :, k, :], 1.0 if k == 1 else 0.0, None, ALU.add if k == 1 else ALU.max))
                dve.wait_ge(sem("above_summed"), n + 1)
                shift = (tiles * P).bit_length() - 1
                parts = -(-(windows - 1) // P)
                step(dve.tensor_scalar(step_int[:, 0:windows - 1], ps_v[:, 0, 0:windows - 1], -1.0, float(E), ALU.mult, ALU.add))
                step(dve.tensor_scalar(step_int[:, 0:windows - 1], step_int[:, 0:windows - 1], shift, None, ALU.arith_shift_right))
                step(dve.tensor_copy(step_row[:, 0:windows - 1], step_int[:, 0:windows - 1]))
                step(dve.scalar_tensor_tensor(out=step_row[:, 0:windows - 1], in0=step_row[:, 0:windows - 1], scalar=1.0,
                                              in1=iota_row[:, 0:windows - 1], op0=ALU.add, op1=ALU.add))
                if n == 0:
                    step(dve.memset(c_end[:, :], CV))
                    step(dve.tensor_copy(c_end[:, 0:windows - 1], step_row[:, 0:windows - 1]))
                for c in range(parts):
                    k = min(P, windows - 1 - c * P)
                    step(dve.tensor_scalar(step_int[0:k, c:c + 1], ps_v[0:k, 1, c:c + 1], -1.0, float(E), ALU.mult, ALU.add))
                    step(dve.tensor_scalar(step_int[0:k, c:c + 1], step_int[0:k, c:c + 1], shift, None, ALU.arith_shift_right))
                    step(dve.tensor_copy(step_col[0:k, c:c + 1], step_int[0:k, c:c + 1]))
                    step(dve.scalar_tensor_tensor(out=step_col[0:k, c:c + 1], in0=step_col[0:k, c:c + 1], scalar=float(c * P + 1),
                                                  in1=iota_part[0:k, :], op0=ALU.add, op1=ALU.add))
                    step(dve.tensor_scalar(reached[0:k, c, 0:visits], iota_visit[0:k, 0:visits], step_col[0:k, c:c + 1], None, ALU.is_ge))
                dve.sem_inc(sem("reached_ready"), 1)
                dve.wait_ge(sem("windows_summed"), n + 1)
                half = visits // 2
                step(dve.tensor_copy(window_f[:, 0:half], ps_t[:, 0, 0:half]))
                step(dve.tensor_copy(window_f[:, half:visits], ps_t[:, 1, 0:half]))
                tt(group_f[:, 0:visits], iota_visit[:, 0:visits], window_f[:, 0:visits], ALU.subtract)
                pick = (c_select, select)[n]
                for c in range(-(-groups // P)):
                    step(dve.tensor_scalar(pick[:, c, :], group_f[:, 0:visits], float(-c * P), iota_part[:, 0:1], ALU.add, ALU.is_equal))
                dve.sem_inc(sem("select_ready"), 1)
                def pack_list(into, weights):
                    n = into.shape[-1]
                    packed = step_row[:, 0:n]
                    for k, (values, at, weight) in enumerate(weights):
                        each = values[:, at:at + n * UNROLL].rearrange("p (i u) -> p i u", u=UNROLL)[:, :, 0]
                        if k == 0:
                            step(dve.tensor_scalar(packed, each, float(weight), None, ALU.mult))
                        else:
                            step(dve.scalar_tensor_tensor(out=packed, in0=each, scalar=float(weight), in1=packed, op0=ALU.mult, op1=ALU.add))
                    step(dve.tensor_copy(into, packed))

                if n == 0:
                    step(dve.tensor_copy(c_window[:, :], window_f[:, 0:CV]))
                    bank_int = tile_t[:, :, :].rearrange("p s c -> p (s c)")[:, 0:CV].bitcast(I32)
                    step(dve.tensor_scalar(bank_int, c_window[:, :], RING - 1, None, ALU.bitwise_and))
                    step(dve.tensor_copy(group_f[:, 0:CV], bank_int))
                    pack_list(c_pack[:, :], [(window_f, UNROLL - 1, 1)] +
                              [(group_f, k, 2 ** (WINDOW_BITS + BANK_BITS * k)) for k in range(UNROLL)])
                else:
                    step(dve.memset(window_of[:, :], 0))
                    step(dve.tensor_copy(window_of[:, 0:V], window_f[:, 0:V]))
                    step(dve.memset(window_f[:, V:V + 2 * UNROLL], 0.0))
                    pack_list(look_pack[:, :], [(window_f, 1 + k, 2 ** (PASS_BITS * k)) for k in range(UNROLL)])
                    pack_list(add_pack[:, 1:], [(window_f, UNROLL - 1 + k, 2 ** (PASS_BITS * k)) for k in range(UNROLL)])
                step(dve.tensor_scalar(window_f[:, 0:visits], window_f[:, 0:visits], float(-size), -1.0, ALU.mult, ALU.add))
                dve.wait_ge(sem("lists_ordered"), n + 1)
                for b in range(tiles):
                    for half in range(2):
                        v = slice(half * (visits // 2), (half + 1) * (visits // 2))
                        if n == 0:
                            source, rest = c_int[:, 0, 0:visits // 2], c_int[:, 1, 0:visits // 2]
                            target, inside = group_f[:, 0:visits // 2], group_f[:, visits // 2:visits]
                            step(dve.tensor_copy(source, ordered(n, 0, b, half)))
                            step(dve.tensor_scalar(rest, source, P - 1, None, ALU.bitwise_and))
                            step(dve.tensor_copy(c_lo[:, v, b], rest))
                            step(dve.tensor_scalar(rest, source, P.bit_length() - 1, None, ALU.arith_shift_right))
                            tt(target, ordered(n, 1, b, half), window_f[:, v], ALU.add)
                            step(dve.scalar_tensor_tensor(out=c_key[:, v, b], in0=target, scalar=float(WINDOWS), in1=rest, op0=ALU.mult, op1=ALU.add))
                            step(dve.tensor_scalar(inside, target, 0.0, None, ALU.is_ge))
                            step(dve.scalar_tensor_tensor(out=inside, in0=target, scalar=float(CW), in1=inside, op0=ALU.is_lt, op1=ALU.mult))
                            step(dve.scalar_tensor_tensor(out=c_key[:, v, b], in0=c_key[:, v, b], scalar=1.0, in1=inside, op0=ALU.add, op1=ALU.mult))
                        else:
                            step(dve.tensor_tensor(edge_dst[:, v, b], ordered(n, 1, b, half), window_f[:, v], ALU.add))
                            step(dve.tensor_copy(edge_row[:, v, b], ordered(n, 0, b, half)))
                            step(dve.tensor_copy(edge_type[:, v, b], ordered(n, 2, b, half)))
                            step(dve.scalar_tensor_tensor(out=edge_rel_row[:, v, b], in0=ordered(n, 0, b, half), scalar=float(R),
                                                          in1=edge_type[:, v, b], op0=ALU.mult, op1=ALU.add))
                if n == 0:
                    step(dve.memset(c_key[:, CV:CV + 1, :], 0.0))
                    step(dve.memset(c_lo[:, CV:CV + 1, :], 0.0))
                    step(dve.tensor_scalar(c_key[:, :, :], c_key[:, :, :], -1.0, None, ALU.add))
                else:
                    step(dve.memset(edge_dst[:, V:V + 2, :], -1.0))
                    step(dve.memset(edge_row[:, V:V + AHEAD, :], 0))
                    step(dve.memset(edge_rel_row[:, V:V + AHEAD, :], 0))
                dve.sem_inc(sem("lists_taken"), 1)
            step(dve.tensor_scalar(loop_mask[:, :], loop_mask[:, :], float(N_LOOP), None, ALU.is_lt))

            dve.wait_ge(sem("weights_ready"), 2)
            step(dve.memset(banks[:, :, 0:C_COLS], 0.0))
            dve.sem_inc(sem("banks_free"), RING)
            dve.sem_inc(sem("c_walk_ready"), 1)

            def count_onehots(n, k):
                if later(n, UNROLL):
                    dve.wait_ge(sem("c_counted"), n - UNROLL + 1)
                dve.tensor_tensor(lo_hot[:, k, :, :], iota_16[:, :].unsqueeze(1).to_broadcast([P, CB, P]),
                                  c_lo[:, bass.ds(n, 1), :].rearrange("p v b -> p (v b)").unsqueeze(2).to_broadcast([P, CB, P]), ALU.is_equal)
                for b in range(CB):
                    last = dve.tensor_scalar(key_hot[:, k, b, :], iota_c[:, :],
                                             c_key[:, bass.ds(n, 1), b:b + 1].rearrange("p v b -> p (v b)"), None, ALU.is_equal)
                last.then_inc(sem("c_key_ready"), 1)

            loop_visits(dve, lambda: None, count_onehots, lambda: None, CV, steps=LONG_TURN)
            dve.wait_ge(sem("ring_slots_free"), RING + C_WINDOWS)
            dve.wait_ge(sem("banks_free"), RING + C_WINDOWS)

            dve.wait_ge(sem("x_loaded"), 32)
            dve.wait_ge(sem("degrees_loaded"), 16)
            step(dve.tensor_reduce(count[:, :], rel_norm[:, :, :], AX, ALU.add))
            step(dve.tensor_scalar(dis[:, :], count[:, :], 1.0, None, ALU.add))
            ask()
            step(dve.reciprocal(dis[:, :], dis[:, :]))
            step(dve.tensor_scalar(rel_norm[:, :, :], rel_norm[:, :, :], 1.0, None, ALU.max))
            step(dve.reciprocal(rel_norm[:, :, :], rel_norm[:, :, :]))
            tt(z, x_cur[:, :, :], over_features(dis[:, :]), ALU.mult)

            att = 0
            for phase, (kind, what) in enumerate(PHASES):
                at = {x: before(phase, x) for x in ("sum_ready", "sum_added", "looked_up", "look_ups_joined", "gathered", "factor_made", "coef_made",
                                                    "block_summed", "block_copied", "block_loaded0", "block_loaded1", "block_loaded2", "tile_transposed", "tile_staged", "product_copied", "onehot_ready", "transposed_copied")}
                nh = HEADS if what == "att8" else 1
                if what == "norm":
                    step(dve.memset(acc, 0.0))
                if kind == "blocks":
                    step(dve.memset(acc[:, WINDOWS:W, :], 0.0))
                if what in ("att8", "att1"):
                    att += 1
                    step(dve.tensor_reduce(peak[:, 0:nh], ab[:, :, 0:nh].rearrange("p w h -> p h w"), AX, ALU.max))
                    dve.sem_inc(sem("peak_ready"), 1)
                    dve.wait_ge(sem("peak_reduced"), att)
                    top = peak_all[:, 0:nh].unsqueeze(1).to_broadcast([P, W, nh])
                    tt(uf[:, :, 0:nh], ab[:, :, 0:nh], top, ALU.subtract)
                    tt(uf[:, :, nh:2 * nh], ab[:, :, 0:nh], top, ALU.subtract)
                    tt(ab[:, :, nh:2 * nh], ab[:, :, nh:2 * nh], top, ALU.add)
                    step(dve.tensor_scalar(tv[:, :, 0:nh], ab[:, :, nh:2 * nh], 0.0, None, ALU.min))
                    step(dve.tensor_scalar(tv[:, :, nh:2 * nh], ab[:, :, nh:2 * nh], 0.0, None, ALU.max))
                    for _ in functions_before(what):
                        ask()
                    if what == "att1":
                        step(dve.tensor_copy(tile_in[:, 0, 0:2 * W].rearrange("p (k w) -> p w k", k=2), tv[:, :, 0:2]))
                        dve.sem_inc(sem("targets_ready"), 1)
                        dve.wait_ge(sem("targets_transposed"), 1)
                        step(dve.tensor_copy(tile_in[0:2 * W, 1, 0:P], ps_v[0:2 * W, 0, 0:P]))
                    dve.sem_inc(sem("factors_made"), 1)
                    tt(ab[:, 0:LOOP_W, 0:2 * nh], uf[:, 0:LOOP_W, 0:2 * nh], tv[:, 0:LOOP_W, 0:2 * nh], ALU.mult)
                    tt(ab[:, 0:LOOP_W, 0:nh], ab[:, 0:LOOP_W, 0:nh], ab[:, 0:LOOP_W, nh:2 * nh], ALU.max)
                    tt(ab[:, 0:LOOP_W, 0:nh], ab[:, 0:LOOP_W, 0:nh], loop_mask[:, :].unsqueeze(2).to_broadcast([P, LOOP_W, nh]), ALU.mult)
                if what == "att8":
                    dve.wait_ge(sem("wide_cleared"), att * W)
                    dve.wait_ge(sem("loop_rows_loaded"), 16 * att)
                    for w in range(LOOP_W):
                        dve.tensor_tensor(wide[:, w, 0:HC].rearrange("p (h c) -> p h c", h=nh),
                                          loop_rows[:, w, 0:HC].rearrange("p (h c) -> p h c", h=nh),
                                          over_features(ab[:, w, 0:nh], HID), ALU.mult)
                    step(dve.tensor_copy(wide[:, 0:LOOP_W, HC:HC + nh], ab[:, 0:LOOP_W, 0:nh]))
                if what == "att1":
                    step(dve.memset(h_one[:, :, D:D + 1], 1.0))

                if kind == "pass":
                    values, n = lookup_values(what)
                    split = parts_of(what)
                    rest, rounded = (onehot[:, 2 * k:2 * k + 2, :, :].rearrange("p u b c -> p (u b c)")[:, 0:W * n]
                                     .rearrange("p (w v) -> p w v", v=n) for k in range(2))
                    step(dve.tensor_copy(rest, values[:, :, 0:n]))
                    for k in range(3):
                        step(dve.tensor_copy(split[:, :, k * n:(k + 1) * n], rest))
                        if k < 2:
                            step(dve.tensor_copy(rounded, split[:, :, k * n:(k + 1) * n]))
                            tt(rest, rest, rounded, ALU.subtract)

                if kind == "blocks":
                    dve.sem_inc(sem("blocks_begun"), 1)
                    if what == "att1":
                        def weigh_block(j, s, turn):
                            for q, (lo, hi) in enumerate(SOURCES):
                                one, two, counts = slope1[:, :, lo:hi], slope2[:, :, lo:hi], c_block[s][:, :, lo:hi]
                                dve.wait_ge(sem("slope2_made"), 2 * j + q + 1)
                                dve.wait_ge(sem("slope1_made"), 2 * j + q + 1)
                                dve.tensor_tensor(two, two, one, ALU.max).then_inc(sem("slopes_joined"), 1)
                                dve.wait_ge(sem("slopes_joined"), 2 * j + q + 1)
                                if q == 0:
                                    dve.wait_ge(sem(f"block_loaded{s}"), at[f"block_loaded{s}"] + turn * 16 + 16)
                                dve.tensor_tensor(counts, counts, two, ALU.mult).then_inc(sem("block_weighed"), 1)

                        loop_blocks(dve, weigh_block, BLOCK_SLOTS[what])
                    if phase == L0_SUM1:
                        dve.wait_ge(sem("attention_loaded"), 16 * 6)
                        for name, weight, heads, c_head in (("h1", w_h1, HEADS, HID), ("h2", w_h2, HEADS, HID), ("h3", w_h3, 1, D)):
                            cols = heads * c_head
                            for c in range(DENSE[name][0]):
                                for side in range(2):
                                    tt(setup_product[:, 0:cols], weight[:, c, 0:cols], att_rows[name][:, side, :], ALU.mult)
                                    step(dve.tensor_reduce(weight[:, c, cols + side * heads:cols + (side + 1) * heads],
                                                           setup_product[:, 0:cols].rearrange("p (h c) -> p h c", h=heads), AX, ALU.add))
                    dve.wait_ge(sem("block_copied"), at["block_copied"] + WINDOWS)
                elif kind == "pass":
                    dve.sem_inc(sem("pass_begun"), 1)

                    def make_onehot(m, k):
                        if later(m, UNROLL):
                            dve.wait_ge(sem("sum_ready"), at["sum_ready"] + m - UNROLL + 1)
                        for b in range(B):
                            last = dve.tensor_scalar(onehot[:, k % UNROLL, b, :], iota_col[:, :],
                                                     edge_dst[:, bass.ds(m, 1), b:b + 1].rearrange("p v b -> p (v b)"), None, ALU.is_equal)
                        last.then_inc(sem("onehot_ready"), 1)

                    def relations(n, s):
                        return dve.tensor_tensor(rel_hot[:, s, :, :], iota_rel[:, :, :],
                                                 edge_type[:, bass.ds(n, 1), :].rearrange("p v b -> p (v b)").unsqueeze(2).to_broadcast([P, B, R]),
                                                 ALU.is_equal)

                    def weigh(n, k):
                        s = k % 2

                        def join_look_up(n_values):
                            dve.wait_ge(sem("looked_up"), at["looked_up"] + n + 1)
                            dve.tensor_reduce(looked_up[:, :, 0:n_values],
                                              ps_v[:, s, 0:B * 3 * n_values].rearrange("p (b c v) -> p b v c", b=B, c=3), AX, ALU.add
                                              ).then_inc(sem("look_ups_joined"), 1)

                        if what == "norm":
                            relations(n, s).then_inc(sem("factor_made"), 1)
                            join_look_up(R)
                            dve.wait_ge(sem("factor_made"), at["factor_made"] + n + 1)
                            dve.wait_ge(sem("look_ups_joined"), at["look_ups_joined"] + n + 1)
                            dve.tensor_tensor(factor[:, :, 0:R], rel_hot[:, s, :, :], looked_up[:, :, 0:R],
                                              ALU.mult).then_inc(sem("coef_made"), 1)
                            dve.wait_ge(sem("coef_made"), at["coef_made"] + 2 * n + 1)
                            dve.tensor_reduce(coef[:, :], factor[:, :, 0:R], AX, ALU.add).then_inc(sem("coef_made"), 1)
                            dve.wait_ge(sem("coef_made"), at["coef_made"] + 2 * n + 2)
                        else:
                            join_look_up(2 * nh)
                            for b in range(B):
                                dve.wait_ge(sem(f"gathered{s * B + b}"), at["gathered"] + (n - s) * 8 + 16)
                            dve.wait_ge(sem("look_ups_joined"), at["look_ups_joined"] + n + 1)
                            first = HC
                            dve.tensor_tensor(factor[:, :, 0:2 * nh], rows_g[:, s, :, first:first + 2 * nh],
                                              looked_up[:, :, 0:2 * nh], ALU.mult).then_inc(sem("factor_made"), 1)
                            dve.wait_ge(sem("factor_made"), at["factor_made"] + n + 1)
                            if what == "att8" and later(n, 2):
                                dve.wait_ge(sem("sum_ready"), at["sum_ready"] + n - 1)
                            into = rows_w[:, s, :, HC:HC + nh]
                            dve.tensor_tensor(into, factor[:, :, 0:nh], factor[:, :, nh:2 * nh], ALU.max).then_inc(sem("coef_made"), 1)
                            dve.wait_ge(sem("coef_made"), at["coef_made"] + n + 1)
                        if what == "att8":
                            for b in range(B - 1):
                                last = dve.tensor_tensor(rows_w[:, s, b, 0:HC].rearrange("p (h c) -> p h c", h=HEADS),
                                                         rows_g[:, s, b, 0:HC].rearrange("p (h c) -> p h c", h=HEADS),
                                                         over_features(rows_w[:, s, b, HC:HC + HEADS], HID), ALU.mult)
                                if b == B // 2 - 1:
                                    last.then_inc(sem("half_weighted"), 1)
                        else:
                            for b in range(B):
                                last = dve.tensor_scalar(onehot[:, k, b, :], onehot[:, k, b, :], coef[:, b:b + 1], None, ALU.mult)
                        last.then_inc(sem("weighted"), 1)

                    turn_windows = []

                    def next_windows(i):
                        turn_windows[:] = unpack(dve, add_pack, i, PASS_BITS)[1]

                    def add_sum(n, k):
                        s = k % 2
                        window = turn_windows[k - 1] if not isinstance(n, int) else \
                            dve.value_load(window_of[0:1, n:n + 1], min_val=0, max_val=WINDOWS - 1)
                        dve.wait_ge(sem("sum_ready"), at["sum_ready"] + n + 1)
                        if later(n, 1):
                            dve.wait_ge(sem("sum_added"), at["sum_added"] + n)
                        if what == "att8":
                            for half, bank in enumerate((ps_sum, ps_tail)):
                                into = wide[:, bass.ds(window, 1), half * HALF:(half + 1) * HALF]
                                last = dve.tensor_tensor(into, into, bank[:, s:s + 1, 0:HALF], ALU.add)
                        else:
                            cols = D
                            last = dve.tensor_tensor(acc[:, bass.ds(window, 1), 0:cols], acc[:, bass.ds(window, 1), 0:cols],
                                                     ps_sum[:, s:s + 1, 0:cols], ALU.add)
                        last.then_inc(sem("sum_added"), 1)

                    def visit(n, k):
                        make_onehot(n + 2, k + 2)
                        weigh(n, k)
                        if later(n, 1):
                            add_sum(n - 1, k + 1)

                    def start():
                        make_onehot(0, 0)
                        make_onehot(1, 1)

                    loop_visits(dve, start, visit, lambda: add_sum(V - 1, 1), turn=next_windows)
                    dve.wait_ge(sem("sum_added"), at["sum_added"] + V)
                    dve.wait_ge(sem("looked_up"), at["looked_up"] + V + 1)
                    dve.wait_ge(sem("transposed_copied"), at["transposed_copied"] + V + 2)
                else:
                    chunks, cols, to_table = DENSE[what]
                    source = {"rel": x_cur, "self": x_cur, "h1": x_cur, "gcn1": acc, "gcn2": acc, "mix": cat, "gate": cat,
                              "h2": wide, "h3": wide}[what]

                    def stage(w, s, turn, last):
                        if later(w, 2):
                            dve.wait_ge(sem("tile_transposed"), at["tile_transposed"] + w - 1)
                        dve.tensor_copy(tile_in[:, s:s + 1, 0:chunks * P], source[:, bass.ds(w, 1), 0:chunks * P]).then_inc(sem("tile_staged"), 1)
                        if what in ("h1", "h2"):
                            dve.wait_ge(sem("tile_staged"), at["tile_staged"] + w + 1)
                            dve.tensor_scalar(wide[:, bass.ds(w, 1), :], iota_col[:, 0:1].unsqueeze(1).to_broadcast([P, 1, HC + HEADS]), 0.0, None,
                                              ALU.mult).then_inc(sem("wide_cleared"), 1)

                    loop_tiles(dve, lambda: None, stage)
                    dve.wait_ge(sem("product_copied"), at["product_copied"] + W)

                if phase in (L0_SUM1, L0_SUM2):
                    tt(acc[:, :, 0:D], acc[:, :, 0:D], z, ALU.add)
                    tt(acc[:, :, 0:D], acc[:, :, 0:D], over_features(dis[:, :]), ALU.mult)
                elif what == "gcn1":
                    tt(z, z, over_windows(BIAS["L0_gnn_b1"]), ALU.add)
                    step(dve.tensor_scalar(z, z, 0.0, None, ALU.max))
                    tt(z, z, over_features(dis[:, :]), ALU.mult)
                elif what == "gcn2":
                    tt(x_cur[:, :, :], x_cur[:, :, :], z, ALU.add)
                    tt(x_cur[:, :, :], x_cur[:, :, :], over_windows(BIAS["L0_gnn_b2"]), ALU.add)
                    layer_norm(x_cur[:, :, :], spare)
                elif what == "norm":
                    tt(x_cur[:, :, :], x_cur[:, :, :], z, ALU.add)
                    tt(x_cur[:, :, :], x_cur[:, :, :], acc[:, :, 0:D], ALU.add)
                    tt(x_cur[:, :, :], x_cur[:, :, :], over_windows(BIAS["L1_gnn_bias"]), ALU.add)
                    layer_norm(x_cur[:, :, :], spare)
                elif phase == L2_SUM:
                    step(dve.tensor_scalar(has[:, :], count[:, :], 0.0, None, ALU.is_gt))
                    step(dve.tensor_scalar(count[:, :], count[:, :], 1.0, None, ALU.max))
                    step(dve.reciprocal(count[:, :], count[:, :]))
                    step(dve.tensor_copy(cat[:, :, 0:D], x_cur[:, :, :]))
                    tt(cat[:, :, D:2 * D], acc[:, :, 0:D], over_features(count[:, :]), ALU.mult)
                elif what == "mix":
                    tt(cat[:, :, D:2 * D], over_windows(BIAS["L2_gnn_b_neigh"]), over_features(has[:, :]), ALU.mult)
                    tt(cat[:, :, D:2 * D], cat[:, :, D:2 * D], z, ALU.add)
                    tt(cat[:, :, D:2 * D], cat[:, :, D:2 * D], over_windows(BIAS["L2_gnn_b_self"]), ALU.add)
                elif what == "gate":
                    tt(z, z, over_windows(BIAS["L2_gnn_b_gate"]), ALU.add)
                    ask()
                    tt(spare, cat[:, :, D:2 * D], x_cur[:, :, :], ALU.subtract)
                    tt(z, z, spare, ALU.mult)
                    tt(z, z, x_cur[:, :, :], ALU.add)
                    layer_norm(z, spare)
                    tt(z, z, over_windows(BIAS["L2_gnn_ln_gamma"]), ALU.mult)
                    tt(z, z, over_windows(BIAS["L2_gnn_ln_beta"]), ALU.add)
                    step(dve.tensor_scalar(z, z, 0.0, None, ALU.max))
                    tt(x_cur[:, :, :], x_cur[:, :, :], z, ALU.add)
                    layer_norm(x_cur[:, :, :], spare)
                elif what == "att8":
                    den = wide[:, :, HC:HC + HEADS]
                    step(dve.tensor_scalar(den, den, TINY, None, ALU.max))
                    step(dve.reciprocal(den, den))
                    heads = wide[:, :, 0:HC].rearrange("p w (h c) -> p w h c", h=HEADS)
                    tt(heads, heads, den.unsqueeze(3).to_broadcast([P, W, HEADS, HID]), ALU.mult)
                    tt(wide[:, :, 0:HC], wide[:, :, 0:HC], over_windows(bias_wide[:, att - 1, :]), ALU.add)
                    w = 0
                    for n in elu_parts():
                        part = wide[:, w:w + n, 0:HC]
                        low = setup_rows[:, 0:n * HC].rearrange("p (w c) -> p w c", w=n)
                        step(dve.tensor_scalar(low, part, 0.0, None, ALU.min))
                        ask()
                        step(dve.scalar_tensor_tensor(out=part, in0=low, scalar=-1.0, in1=part, op0=ALU.add, op1=ALU.max))
                        w += n
                elif what == "att1":
                    tt(z[:, 0:LOOP_W, :], h_one[:, 0:LOOP_W, 0:D], over_features(ab[:, 0:LOOP_W, 0]), ALU.mult)
                    tt(acc[:, 0:LOOP_W, 0:D], acc[:, 0:LOOP_W, 0:D], z[:, 0:LOOP_W, :], ALU.add)
                    tt(acc[:, 0:LOOP_W, D], acc[:, 0:LOOP_W, D], ab[:, 0:LOOP_W, 0], ALU.add)
                    step(dve.tensor_scalar(stat[:, :], acc[:, :, D], TINY, None, ALU.max))
                    step(dve.reciprocal(stat[:, :], stat[:, :]))
                    tt(acc[:, :, 0:D], acc[:, :, 0:D], over_features(stat[:, :]), ALU.mult)
                    tt(x_cur[:, :, :], x_cur[:, :, :], acc[:, :, 0:D], ALU.add)
                    tt(x_cur[:, :, :], x_cur[:, :, :], over_windows(BIAS["L3_gnn_b3"]), ALU.add)
                    layer_norm(x_cur[:, :, :], spare)
                    dve.sem_inc(sem("result_made"), 1)


def kernel(**inputs):
    import numpy as np
    import concourse.bacc as bacc
    from concourse.bass_utils import run_bass_kernel_spmd

    nc = bacc.Bacc("TRN2", target_bir_lowering=False, num_devices=1)
    arrays, args = {}, {}
    for name, value in inputs.items():
        value = np.ascontiguousarray(value)
        arrays[f"in_{name}"] = value
        args[name] = nc.dram_tensor(f"in_{name}", value.shape, mybir.dt.from_np(value.dtype), kind="ExternalInput").ap()
    result = nc.dram_tensor("result", (N, D), F32, kind="ExternalOutput").ap()
    gnn_kernel(nc, args, result)
    return run_bass_kernel_spmd(nc, [arrays], core_ids=[0]).results[0]["result"]
```
